# Optimizing a Trainium2 kernel written in Bass

```python
import numpy as np
import jax
import jax.numpy as jnp

def _softmax(x, axis=-1):
    return jax.nn.softmax(x, axis=axis)

def _gelu(x):
    return jax.nn.gelu(x, approximate=True)

def _silu(x):
    return jax.nn.silu(x)

def _sigmoid(x):
    return jax.nn.sigmoid(x)

def _layernorm(x, axis=-1, eps=1e-05):
    m = jnp.mean(x, axis=axis, keepdims=True)
    v = jnp.var(x, axis=axis, keepdims=True)
    return (x - m) / jnp.sqrt(v + eps)

def _scatter_add(tgt, idx, src, axis=0):
    return tgt.at[idx].add(src)

def _segment_sum(src, seg, n):
    return jax.ops.segment_sum(src, seg, n)
kernel_name = 'mk_gnn_preln_d2_gnn_r32_451b53'

def setup_inputs(seed: int=0):
    np.random.seed(seed)
    _w = jnp.asarray

    def _rec_inputs():
        import jax
        import jax.numpy as jnp
        _gk = jax.random.key(seed)
        x = -0.0005121 + 1.001 * jax.random.normal(jax.random.fold_in(_gk, 1), (3125, 32), jnp.float32)
        src = jax.random.randint(jax.random.fold_in(_gk, 2), (100000,), 0, 3125, jnp.int32)
        dst = jnp.minimum((3125 * jax.random.uniform(jax.random.fold_in(_gk, 3), (100000,)) ** 2.0).astype(jnp.int32), 99999)
        _o = jnp.argsort(dst, stable=True)
        src = src[_o]
        dst = dst[_o]
        edge_attr_4 = 0.000398945 + 1.00003 * jax.random.normal(jax.random.fold_in(_gk, 11), (100000, 4), jnp.float32)
        return (x, src, dst, edge_attr_4)
    x, src, dst, edge_attr_4 = _rec_inputs()

    def _L0_gnn_setup():
        import jax, jax.numpy as jnp
        import numpy as np
        N_NODES = 3125
        N_EDGES = 50000
        IN_DIM = 32
        HID = 64
        OUT_DIM = 32
        EDGE_DIM = 4
        key = jax.random.key(seed)
        ks = jax.random.split(key, 12)
        x = jax.random.normal(ks[0], (N_NODES, IN_DIM), dtype=jnp.float32)
        edge_index = jax.random.randint(ks[1], (2, N_EDGES), 0, N_NODES, dtype=jnp.int32)
        edge_attr = jax.random.normal(ks[2], (N_EDGES, EDGE_DIM), dtype=jnp.float32)

        def lin(k, fan_in, fan_out):
            kw, kb = jax.random.split(k)
            bound = 1.0 / np.sqrt(fan_in)
            W = jax.random.uniform(kw, (fan_in, fan_out), minval=-bound, maxval=bound, dtype=jnp.float32)
            b = jax.random.uniform(kb, (fan_out,), minval=-bound, maxval=bound, dtype=jnp.float32)
            return (W, b)
        W1, b1 = lin(ks[3], 2 * IN_DIM, HID)
        W2, b2 = lin(ks[4], HID, 2 * HID)
        W3, b3 = lin(ks[5], 2 * HID, HID)
        W4, b4 = lin(ks[6], HID, OUT_DIM)
        return {'x': x, 'edge_index': edge_index, 'edge_attr': edge_attr, 'W1': W1, 'b1': b1, 'W2': W2, 'b2': b2, 'W3': W3, 'b3': b3, 'W4': W4, 'b4': b4}
    _L0_gnn_all = _L0_gnn_setup()
    _L0_gnn_in = {k: v for k, v in _L0_gnn_all.items() if k in ('W1', 'b1', 'W2', 'b2', 'W3', 'b3', 'W4', 'b4')}
    del _L0_gnn_all

    def _L1_gnn_setup():
        import jax, jax.numpy as jnp
        import numpy as np
        K = 10
        ALPHA = 0.1
        BETA = 0.9
        N_NODES = 3125
        N_EDGES = 50000
        D_FEAT = 32
        key = jax.random.key(seed)
        k1, k2 = jax.random.split(key)
        x = jax.random.normal(k1, (N_NODES, D_FEAT), dtype=jnp.float32)
        edge_index = jax.random.randint(k2, (2, N_EDGES), 0, N_NODES, dtype=jnp.int64)
        return {'x': x, 'edge_index': edge_index}
    _L1_gnn_all = _L1_gnn_setup()
    _L1_gnn_in = {k: v for k, v in _L1_gnn_all.items() if k in ()}
    del _L1_gnn_all
    return {'x': x, 'src': src, 'dst': dst, 'edge_attr_4': edge_attr_4, 'L0_gnn_W1': _L0_gnn_in['W1'], 'L0_gnn_b1': _L0_gnn_in['b1'], 'L0_gnn_W2': _L0_gnn_in['W2'], 'L0_gnn_b2': _L0_gnn_in['b2'], 'L0_gnn_W3': _L0_gnn_in['W3'], 'L0_gnn_b3': _L0_gnn_in['b3'], 'L0_gnn_W4': _L0_gnn_in['W4'], 'L0_gnn_b4': _L0_gnn_in['b4']}

def reference(x, src, dst, edge_attr_4, L0_gnn_W1, L0_gnn_b1, L0_gnn_W2, L0_gnn_b2, L0_gnn_W3, L0_gnn_b3, L0_gnn_W4, L0_gnn_b4):
    import jax
    import jax.numpy as jnp

    def _L0_gnn_ref(x, edge_index, edge_attr, W1, b1, W2, b2, W3, b3, W4, b4):
        import jax, jax.numpy as jnp
        import numpy as np
        N_NODES = 3125
        N_EDGES = 50000
        IN_DIM = 32
        HID = 64
        OUT_DIM = 32
        EDGE_DIM = 4
        j_idx = edge_index[0]
        i_idx = edge_index[1]
        x_j = x[j_idx]
        x_i = x[i_idx]
        msg = jnp.concatenate([x_i, x_j - x_i], axis=-1)
        h = jax.nn.relu(msg @ W1 + b1)
        h = jax.nn.relu(h @ W2 + b2)
        h = jax.nn.relu(h @ W3 + b3)
        m = h @ W4 + b4
        s = jax.ops.segment_sum(m, i_idx, num_segments=N_NODES)
        cnt = jax.ops.segment_sum(jnp.ones((m.shape[0],), m.dtype), i_idx, num_segments=N_NODES)
        return s / jnp.maximum(cnt, 1.0)[:, None]

    def _L1_gnn_ref(x, edge_index):
        import jax, jax.numpy as jnp
        import numpy as np
        K = 10
        ALPHA = 0.1
        BETA = 0.9
        N_NODES = 3125
        N_EDGES = 50000
        D_FEAT = 32
        n = x.shape[0]
        row, col = (edge_index[0], edge_index[1])
        ones = jnp.ones(row.shape[0], dtype=x.dtype)
        deg = jax.ops.segment_sum(ones, row, num_segments=n)
        deg = jnp.maximum(deg, jnp.asarray(1.0, x.dtype))
        w = jax.lax.rsqrt(deg[row] * deg[col])
        h = x
        out = h
        for _ in range(K):
            msg = w[:, None] * out[col]
            out = jax.ops.segment_sum(msg, row, num_segments=n)
            out = out * BETA + h * ALPHA
        gamma = BETA ** K + ALPHA * sum((BETA ** i for i in range(K)))
        return out / jnp.asarray(gamma, x.dtype)
    edge_index = jnp.stack([src, dst])
    h = jnp.maximum(_layernorm(x, axis=-1), 0.0)
    x = x + _L0_gnn_ref(h, edge_index, edge_attr_4, L0_gnn_W1, L0_gnn_b1, L0_gnn_W2, L0_gnn_b2, L0_gnn_W3, L0_gnn_b3, L0_gnn_W4, L0_gnn_b4)
    h = jnp.maximum(_layernorm(x, axis=-1), 0.0)
    x = x + _L1_gnn_ref(h, edge_index)
    return x

_drawn_inputs = setup_inputs


def setup_inputs(seed=0):
    import zlib

    import numpy as np

    out = dict(_drawn_inputs(seed))
    spreads = {}
    factors = {'L0_gnn_W1': 4.294, 'L0_gnn_b1': 8.0, 'L0_gnn_b2': 4.484}
    for name, (base, spread) in spreads.items():
        noise = np.random.default_rng([zlib.crc32(name.encode()), seed]).standard_normal(out[name].shape)
        drawn = base * np.exp(spread * noise) if base else spread * noise
        out[name] = jnp.asarray(drawn.astype(out[name].dtype))
    for name, factor in factors.items():
        out[name] = (out[name] * factor).astype(out[name].dtype)
    return out
```

```python
import numpy as np

import concourse.bass as bass
from concourse import mybir
from contextlib import ExitStack

F32 = mybir.dt.float32
BF16 = mybir.dt.bfloat16
F16 = mybir.dt.float16
I32 = mybir.dt.int32
I16 = mybir.dt.int16
ALU = mybir.AluOpType
ACT = mybir.ActivationFunctionType
AX = mybir.AxisListType

NODES, EDGES, FEAT, HID, HID2 = 3125, 100000, 32, 64, 128
P = 128
BLOCKS = -(-NODES // P)
LASTN = NODES - (BLOCKS - 1) * P
HI = BLOCKS
TILES = 4
BATCH = TILES * P
BATCHES = -(-EDGES // BATCH)
TAIL = EDGES - (BATCHES - 1) * BATCH
GB = BATCHES - P
SPAN = 64
PSPAN = 20
PCOLS = PSPAN * HI
PAD_DST = 4095
CCOLS = -(-(NODES + PSPAN) * HI // 2) * 2
SCOLS = BLOCKS * P
ITERS, ALPHA, BETA = 10, 0.1, 0.9
GAMMA = float(np.float32(BETA ** ITERS + ALPHA * sum(BETA ** i for i in range(ITERS))))
EPS = 1e-5
CHUNK = 512
CHUNKS = -(-NODES // CHUNK)
SCANS = 4
SCAN = -(-NODES * BLOCKS // ((ITERS - 2) * SCANS) // 2) * 2
assert SCAN * (ITERS - 2) * SCANS <= CCOLS


def build(nc, x, src, dst, W1, b1, W2, b2, W3, b3, W4, b4, out):
    V, A, T, G = nc.vector, nc.scalar, nc.tensor, nc.gpsimd
    ctx = ExitStack()
    with ctx:
        def sb(name, shape, dt):
            return ctx.enter_context(nc.sbuf_tensor(name, shape, dt))

        def sem(name):
            return ctx.enter_context(nc.semaphore(name))

        def dram(name, shape, dt):
            return nc.dram_tensor(name, shape, dt, kind="Internal").ap()

        p_tab = dram("p_tab", (SCOLS, HID), F32)
        q_tab = dram("q_tab", (SCOLS, HID), F32)
        idx_d = dram("idx_d", (P, BATCHES * TILES), I32)
        rel_d = dram("rel_d", (BATCHES, BATCH), I16)
        dst_d = dram("dst_d", (BATCHES, BATCH), I32)
        dcol_d = dram("dcol_d", (P, BATCHES * TILES), I32)
        y_tab = dram("y_tab", (SCOLS, FEAT), F32)
        max_d = dram("max_d", (P,), F32)
        tab_d = dram("tab_d", (BATCHES, 4), I32)

        C = sb("C", [P, CCOLS], BF16)
        sT = sb("sT", [P, SCOLS], F32)
        key = sb("key", [P, BATCHES, TILES], F32)
        locol = sb("locol", [P, BATCHES, TILES], F16)
        relcol = sb("relcol", [P, BATCHES, TILES], I16)
        tab = sb("tab", [1, BATCHES * 4], I32)
        ident = sb("ident", [P, P], F32)
        identb = sb("identb", [P, P], BF16)
        iota_c = sb("iota_c", [P, PCOLS], F16)
        iota_l = sb("iota_l", [P, P], F16)
        iota_s = sb("iota_s", [P, SPAN], F32)
        pcol = sb("pcol", [P, 1], F32)
        w2s = sb("w2s", [P, HID2], F32)
        w3s = sb("w3s", [HID2, HID], F32)
        w4s = sb("w4s", [HID + 1, FEAT + 1], F32)
        b2c = sb("b2c", [HID2, 1], F32)
        ones1 = sb("ones1", [1, P], F32)
        b3r = sb("b3r", [1, TILES, HID], F32)
        idx = sb("idx", [P, 2, TILES], I32)
        onesb = sb("onesb", [P, 1], BF16)
        stats = sb("stats", [P, 4, BLOCKS], F32)

        class Region:
            def __init__(self, ap):
                self.ap, self.at = ap, 0

            def take(self, n):
                self.at += n
                assert self.at <= self.ap.shape[1], (self.at, self.ap.shape)
                return self.ap[:, self.at - n:self.at]

        work = sb("work", [P, 6650], F32)
        flags = sb("flags", [1, 2], I32)
        mrow = sb("mrow", [1, P + 1], F32)
        roff = sb("roff", [P, 1], F32)
        gidx = sb("gidx", [P, 5, TILES], I32)
        r = Region(work[:, :])
        grow = work[0:SPAN, 2 * TILES * HID:2 * TILES * HID + BATCH].bitcast(I32)
        gat = r.take(2 * TILES * HID).rearrange("p (s n) -> p s n", s=2)
        relb = r.take(BATCH).bitcast(I16).rearrange("p (s n) -> p s n", s=2)[0:SPAN]
        pw = r.take(2 * HID).rearrange("p (s n) -> p s n", s=2)[0:SPAN]
        ohT = r.take(2 * BATCH).rearrange("p (s n) -> p s n", s=2)[0:SPAN]
        ohS = r.take(2 * TILES * SPAN).rearrange("p (s j n) -> p s j n", s=2, j=TILES)
        ohL = r.take(TILES * P).bitcast(BF16).rearrange("p (s j n) -> p s j n", s=2, j=TILES)
        ohC = r.take(TILES * PCOLS).bitcast(BF16).rearrange("p (s j n) -> p s j n", s=2, j=TILES)
        h1s = r.take(TILES * HID)
        h1t = r.take(2 * P)
        h2s = r.take(BATCH)
        h3s = r.take(TILES * (HID + 1)).rearrange("p (j n) -> p j n", j=TILES)
        r = Region(work[:, :])
        stage = [r.take(P * HI // 2).bitcast(BF16) for _ in range(2)]
        maxima = stage[1][:, 0:SCAN]
        ycur = stage[0].bitcast(F32)[:, 0:BLOCKS * FEAT].rearrange("p (b f) -> p b f", f=FEAT)
        ygat = stage[0].bitcast(F32)[:, 800:800 + TILES * FEAT]
        ylo = stage[0].bitcast(F32)[:, 1000:1000 + TILES * P].rearrange("p (j n) -> p j n", j=TILES)
        yexp = stage[1].bitcast(F32)[:, 0:HI * FEAT].rearrange("p (a f) -> p a f", f=FEAT)
        zrow = stage[1].bitcast(F32)[0:1, 1088:1600]
        yhi = stage[1].bitcast(F32)[:, 800:800 + TILES * HI].rearrange("p (j n) -> p j n", j=TILES)
        x1 = r.take(BLOCKS * FEAT).rearrange("p (b f) -> p b f", f=FEAT)
        hg = r.take(BLOCKS * FEAT).rearrange("p (b f) -> p b f", f=FEAT)
        ah = r.take(BLOCKS * FEAT).rearrange("p (b f) -> p b f", f=FEAT)
        osb = [r.take(CHUNK)[0:3 * FEAT] for _ in range(2)]
        r = Region(sT[:, :])
        y3 = [r.take(BLOCKS * 3 * FEAT // 2).bitcast(BF16).rearrange("p (b k f) -> p b k f", k=3, f=FEAT) for _ in range(2)]
        yv = r.take(4 * FEAT).rearrange("p (b f) -> p b f", f=FEAT)
        yr = r.take(4 * FEAT).rearrange("p (b f) -> p b f", f=FEAT)
        sum3 = r.take(FEAT)
        degrow = sT[0:1, :]

        TAILF = 3 * SCOLS + 9 * 1024 + 512 + 2 * 784 + 800 + 192
        T0 = (CCOLS - 2 * TAILF) // 2 * 2
        r = Region(C[:, T0:T0 + 2 * TAILF].bitcast(F32))
        carve = r.take
        hT = carve(SCOLS)[0:FEAT + 1, :]
        pq = carve(SCOLS).rearrange("p (b f) -> p b f", f=2 * HID)
        lnb = carve(SCOLS)
        xc = lnb[:, 0:BLOCKS * FEAT].rearrange("p (b f) -> p b f", f=FEAT)
        sq = lnb[:, BLOCKS * FEAT:2 * BLOCKS * FEAT].rearrange("p (b f) -> p b f", f=FEAT)
        hn = lnb[:, 2 * BLOCKS * FEAT:3 * BLOCKS * FEAT].rearrange("p (b f) -> p b f", f=FEAT)
        dN = carve(1024).bitcast(I32).rearrange("p (c e) -> p c e", c=2)
        sN = carve(1024).bitcast(I32).rearrange("p (c e) -> p c e", c=2)
        aN = carve(1024).bitcast(I32).rearrange("p (c e) -> p c e", c=2)
        lN = carve(1024).bitcast(I32).rearrange("p (c e) -> p c e", c=2)
        relF = carve(1024).rearrange("p (c e) -> p c e", c=2)
        keyF = carve(1024).rearrange("p (c e) -> p c e", c=2)
        floF = carve(1024).rearrange("p (c e) -> p c e", c=2)
        relN = carve(512).bitcast(I16).rearrange("p (c e) -> p c e", c=2)
        srcf = carve(1024).rearrange("p (c e) -> p c e", c=2)
        idxt = carve(BATCHES * TILES).bitcast(I32).rearrange("p (g j) -> p g j", j=TILES)
        dclF = carve(1024).rearrange("p (c e) -> p c e", c=2)
        dcolt = carve(BATCHES * TILES).bitcast(I32).rearrange("p (g j) -> p g j", j=TILES)
        x_sb = carve(BLOCKS * FEAT).rearrange("p (b f) -> p b f", f=FEAT)
        wpq = carve(2 * HID)[0:FEAT + 1]
        w1b = carve(HID)[0:FEAT]
        pmn = sb("pmn", [P, 4], F32)
        pmx = sb("pmx", [P, 4], F32)
        bmn = sb("bmn", [P, 2], F32)
        bmx = sb("bmx", [P, 2], F32)
        pfl = sb("pfl", [P, 4], F32)
        tabN = sb("tabN", [P, 2, 4], I32)

        psum = ctx.enter_context(nc.psum_tensor("psum", [P, 8, 512], F32))
        banks = [psum[:, n, :] for n in range(8)]
        H1, H1T, H2, H3, SEG, CP = banks[0], banks[1], banks[2:4], banks[4], banks[5], banks[6:8]

        s_edges, s_x, s_w, s_pads, s_const = (sem(n) for n in ("s_edges", "s_x", "s_w", "s_pads", "s_const"))
        s_dve = sem("s_dve")
        s_var, s_std = sem("s_var"), sem("s_std")
        s_h, s_wpq, s_h3one = sem("s_h"), sem("s_wpq"), sem("s_h3one")
        s_idxN, s_keyN = sem("s_idxN"), sem("s_keyN")
        s_fill, s_evac = sem("s_fill"), sem("s_evac")
        s_tables, s_rel, s_tabw, s_tab, s_clear = (sem(n) for n in ("s_tables", "s_rel", "s_tabw", "s_tab", "s_clear"))
        idx_loaded = [sem(f"idx_loaded{i}") for i in range(2)]
        landed = [sem(f"landed{i}") for i in range(2)]
        rel_loaded = [sem(f"rel_loaded{i}") for i in range(2)]
        pw_loaded = [sem(f"pw_loaded{i}") for i in range(2)]
        ohT_made, ohS_made = sem("ohT_made"), sem("ohS_made")
        ohC_made = [sem(f"ohC_made{u}") for u in range(2)]
        cp_done = [sem(f"cp_done{u}") for u in range(2)]
        cp_added = [sem(f"cp_added{u}") for u in range(2)]
        h1_done, h1_out, h1t_done, h1t_out = sem("h1_done"), sem("h1_out"), sem("h1t_done"), sem("h1t_out")
        h2_done, h2_out, h3_done, h3_out = sem("h2_done"), sem("h2_out"), sem("h3_done"), sem("h3_out")
        seg_done, seg_added = sem("seg_done"), sem("seg_added")
        s_gen, flag_set, turns, edges_done = sem("s_gen"), sem("flag_set"), sem("turns"), sem("edges_done")
        scanned, s_max, s_max2, flag2_set, turns2 = sem("scanned"), sem("s_max"), sem("s_max2"), sem("flag2_set"), sem("turns2")
        s_x1pad, s_x1, s_res, s_out, s_out2 = sem("s_x1pad"), sem("s_x1"), sem("s_res"), sem("s_out"), sem("s_out2")
        staged, turned, turn_a, turn_d = sem("staged"), sem("turned"), sem("turn_a"), sem("turn_d")
        m_done, ones_set = sem("m_done"), sem("ones_set")
        dg_done, dg_out, dg_col = sem("dg_done"), sem("dg_out"), sem("dg_col")
        v2, sd2, dmx, sdd = sem("v2"), sem("sd2"), sem("dmx"), sem("sdd")
        y_set, o_done, o_out, r_done, y_made = sem("y_set"), sem("o_done"), sem("o_out"), sem("r_done"), sem("y_made")
        y_step, gathers_begun = sem("y_step"), sem("gathers_begun")
        y2_step = sem("y2_step")

        NW, NC = -(-NODES // SPAN), -(-NODES // PSPAN)
        LOADS = 3 * 16 + TILES * 16
        PSTEP, SSTEP, CSTEP = 16 + 3, 4, 4
        P_AT = LOADS + 2
        MLP_AT = P_AT + NW * PSTEP
        S_AT = MLP_AT + 8
        K_AT = S_AT + NW * SSTEP
        C_AT = K_AT + 6
        TURNS = C_AT + NC * CSTEP
        GCOL = 13
        Y_LOADS = 2 * 16 + TILES * 16
        YT_AT = Y_LOADS + 4
        YTURNS = YT_AT + 2 * TILES
        PASS = 16 + 1 + BATCHES * YTURNS + 1

        def general(e, body_fast, body_general):
            e.wait_ge(flag_set, 1)
            wide_batches = e.value_load(flags[0:1, 0:1], min_val=0, max_val=1)
            with e.If(wide_batches < 1):
                body_fast()
            with e.Else():
                body_general()

        SPLIT = [(0, 6), (6, 12), (12, 18), (18, HI)]
        bankb = [b[:, :].bitcast(BF16) for b in banks]
        MB = 15

        def turned_cols(w, lo, n):
            return C[:, bass.ds(w * NODES + lo, n)]

        FILLS = [("hT", n) for n in range(7)] + [("src", c) for c in range(2)] + [("pq", n) for n in range(7)] + \
                [(a, c) for a in ("lo", "key", "rel", "dcol") for c in range(2)]
        PQ_DONE = FILLS.index(("pq", 6)) + 1
        SRC_DONE = FILLS.index(("src", 1)) + 1
        PRE = len(FILLS)
        NAT = {"src": srcf, "lo": floF, "key": keyF, "rel": relF, "dcol": dclF}

        def groups(n):
            return range(4 * n, min(4 * n + 4, BLOCKS))

        block = ctx.enter_context(nc.Block())

        @block.sync
        def _(sp):
            xv = x[0:(BLOCKS - 1) * P, :].rearrange("(b p) f -> p b f", p=P)
            sp.dma_start(x_sb[:, 0:BLOCKS - 1, :], xv).then_inc(s_x, 16)
            sp.wait_ge(s_pads, 3)
            sp.dma_start(x_sb[0:LASTN, BLOCKS - 1, :], x[(BLOCKS - 1) * P:NODES, :]).then_inc(s_x, 16)
            full = (BATCHES - 1 - P)
            for nat, e in ((dN, dst), (sN, src)):
                sp.dma_start(nat[:, 0, :], e[0:P * BATCH].rearrange("(p e) -> p e", e=BATCH)).then_inc(s_edges, 16)
                sp.dma_start(nat[0:full, 1, :], e[P * BATCH:(P + full) * BATCH].rearrange("(p e) -> p e", e=BATCH)).then_inc(s_edges, 16)
                sp.dma_start(nat[full:full + 1, 1, 0:TAIL], e[EDGES - TAIL:EDGES].rearrange("(p e) -> p e", p=1)).then_inc(s_edges, 16)
            sp.wait_ge(s_evac, SRC_DONE)
            sp.dma_start(idx_d, idxt[:, :, :].rearrange("p g j -> p (g j)")).then_inc(s_tables, 16)
            sp.wait_ge(s_evac, PQ_DONE)
            sp.dma_start(p_tab.rearrange("(b p) f -> p b f", p=P), pq[:, :, 0:HID]).then_inc(s_tables, 16)
            sp.dma_start(q_tab.rearrange("(b p) f -> p b f", p=P), pq[:, :, HID:2 * HID]).then_inc(s_tables, 16)
            sp.wait_ge(s_keyN, 1)
            sp.dma_start(rel_d[0:P, :], relN[:, 0, :]).then_inc(s_rel, 16)
            sp.dma_start(rel_d[P:BATCHES, :], relN[0:GB, 1, :]).then_inc(s_rel, 16)
            sp.dma_start(tab_d[0:P, :], tabN[:, 0, :]).then_inc(s_tabw, 16)
            sp.dma_start(tab_d[P:BATCHES, :], tabN[0:GB, 1, :]).then_inc(s_tabw, 16)
            sp.dma_start(dst_d[0:P, :], dN[:, 0, :]).then_inc(s_gen, 16)
            sp.dma_start(dst_d[P:BATCHES, :], dN[0:GB, 1, :]).then_inc(s_gen, 16)
            sp.wait_ge(s_evac, PRE)
            sp.dma_start(dcol_d, dcolt[:, :, :].rearrange("p g j -> p (g j)")).then_inc(s_gen, 16)
            sp.wait_ge(s_tabw, 32)
            sp.dma_start(tab[:, :], tab_d.rearrange("g c -> (g c)").rearrange("(o n) -> o n", o=1)).then_inc(s_tab, 16)
            sp.wait_ge(s_tab, 16)
            sp.wait_ge(s_rel, 32)
            sp.wait_ge(s_tables, 48)

            def load(i, s, prev, done64):
                if done64 is not None:
                    sp.wait_ge(landed[s], done64)
                sp.dma_start(idx[:, s, :], idx_d[:, bass.ds(TILES * i, TILES)]).then_inc(idx_loaded[s], 16)
                base = sp.value_load(tab[0:1, bass.ds(4 * i, 1)], min_val=0, max_val=NODES - 1)
                if prev is not None:
                    sp.wait_ge(ohT_made, prev)
                sp.dma_start(relb[:, s, :], rel_d[bass.ds(i, 1), :].rearrange("o e -> (o e)").partition_broadcast(SPAN)).then_inc(rel_loaded[s], 16)
                if prev is not None:
                    sp.wait_ge(h1_done, prev)
                sp.dma_start(pw[:, s, :], p_tab[bass.ds(base, SPAN), :]).then_inc(pw_loaded[s], 16)

            def edges():
                load(0, 0, None, None)
                load(1, 1, None, None)
                with sp.Fori(1, BATCHES // 2) as m:
                    for s in range(2):
                        load(2 * m + s, s, 2 * m + s - 1, 64 * m)

            def edges_general():
                sp.wait_ge(s_gen, 48)
                with sp.Fori(0, BATCHES) as i:
                    at = i * TURNS + 1
                    sp.wait_ge(turns, at)
                    sp.dma_start(idx[:, 0, :], idx_d[:, bass.ds(TILES * i, TILES)]).then_inc(turns, 16)
                    sp.wait_ge(turns, at + 16)
                    sp.dma_start(gidx[:, 1, :], dcol_d[:, bass.ds(TILES * i, TILES)]).then_inc(turns, 16)
                    sp.wait_ge(turns, at + 32)
                    sp.dma_start(grow, dst_d[bass.ds(i, 1), :].rearrange("o e -> (o e)").partition_broadcast(SPAN)).then_inc(turns, 16)
                    with sp.Fori(0, NW) as w:
                        sp.wait_ge(turns, at + P_AT + w * PSTEP)
                        sp.dma_start(pw[:, 0, :], p_tab[bass.ds(w * SPAN, SPAN), :]).then_inc(turns, 16)

            general(sp, edges, edges_general)
            sp.wait_ge(s_x1pad, 1)
            sp.dma_start(x1[:, 0:BLOCKS - 1, :], xv).then_inc(s_x1, 16)
            sp.dma_start(x1[0:LASTN, BLOCKS - 1, :], x[(BLOCKS - 1) * P:NODES, :]).then_inc(s_x1, 16)
            sp.wait_ge(s_max, 1)
            sp.dma_start(max_d.rearrange("(n o) -> n o", o=1), roff[:, 0:1]).then_inc(s_max2, 16)
            sp.wait_ge(s_max2, 16)
            sp.dma_start(mrow[:, 1:P + 1], max_d.rearrange("(o n) -> o n", o=1)).then_inc(s_max2, 16)
            for n in range(CHUNKS):
                sp.wait_ge(s_res, n + 1)
                lo, hi = 4 * n, min(4 * n + 4, BLOCKS)
                if hi < BLOCKS:
                    sp.dma_start(out[lo * P:hi * P, :].rearrange("(b p) f -> p b f", p=P), ycur[:, lo:hi, :]).then_inc(s_out, 16)
                else:
                    sp.dma_start(out[lo * P:NODES, :], ycur[0:LASTN, lo, :]).then_inc(s_out, 16)
            sp.wait_ge(s_out, 16 * CHUNKS)
            sp.wait_ge(flag2_set, 1)
            large = sp.value_load(flags[0:1, 1:2], min_val=0, max_val=1)
            with sp.If(large > 0):
                with sp.Fori(0, ITERS + 1) as t:
                    sp.wait_ge(turns2, t * PASS + 1)
                    sp.dma_start(y_tab.rearrange("(b p) f -> p b f", p=P), ycur).then_inc(turns2, 16)
                    with sp.Fori(0, BATCHES) as i:
                        at = t * PASS + 17 + i * YTURNS + 1
                        sp.wait_ge(turns2, at)
                        sp.dma_start(gidx[:, 0, :], idx_d[:, bass.ds(TILES * i, TILES)]).then_inc(turns2, 16)
                        sp.wait_ge(turns2, at + 16)
                        sp.dma_start(gidx[:, 1, :], dcol_d[:, bass.ds(TILES * i, TILES)]).then_inc(turns2, 16)
                sp.wait_ge(turns2, (ITERS + 1) * PASS + 1)
                sp.dma_start(out[0:(BLOCKS - 1) * P, :].rearrange("(b p) f -> p b f", p=P), ycur[:, 0:BLOCKS - 1, :]).then_inc(s_out2, 16)
                sp.dma_start(out[(BLOCKS - 1) * P:NODES, :], ycur[0:LASTN, BLOCKS - 1, :]).then_inc(s_out2, 16)
                sp.wait_ge(s_out2, 32)

        @block.gpsimd
        def _(g):
            G.iota(iota_c[:, :], [[1, PCOLS]], base=0, channel_multiplier=0, allow_small_or_imprecise_dtypes=True).then_inc(s_const, 1)
            G.iota(iota_l[:, :], [[1, P]], base=0, channel_multiplier=0, allow_small_or_imprecise_dtypes=True).then_inc(s_const, 1)
            G.iota(iota_s[:, :], [[1, SPAN]], base=0, channel_multiplier=0, allow_small_or_imprecise_dtypes=True).then_inc(s_const, 1)
            G.iota(pcol[:, :], [[1, 1]], base=0, channel_multiplier=1, allow_small_or_imprecise_dtypes=True).then_inc(s_const, 1)
            G.memset(ident[:, :], 0.0).then_inc(s_const, 1)
            G.memset(identb[:, :], 0.0).then_inc(s_const, 1)
            g.wait_ge(s_const, 6)
            for m in (ident, identb):
                G.affine_select(out=m[:, :], in_=m[:, :], compare_op=ALU.not_equal, fill=1.0, base=0,
                                pattern=[[-1, P]], channel_multiplier=1).then_inc(s_const, 1)
            half = T0 // 2 // 2 * 2
            G.memset(C[:, half:T0].bitcast(F32), 0.0).then_inc(s_clear, 1)
            g.wait_ge(s_tables, 48)

            def gather(i, s, loads, prev):
                g.wait_ge(idx_loaded[s], loads)
                if prev is not None:
                    g.wait_ge(h1_done, prev)
                g.sem_inc(gathers_begun, 1)
                for j in range(TILES):
                    G.indirect_dma_start(out=gat[:, s, j * HID:(j + 1) * HID], out_offset=None, in_=q_tab,
                                         in_offset=bass.IndirectOffsetOnAxis(ap=idx[:, s, j:j + 1], axis=0)).then_inc(landed[s], 16)

            def edges():
                gather(0, 0, 16, None)
                gather(1, 1, 16, None)
                with g.Fori(1, BATCHES // 2) as m:
                    for s in range(2):
                        gather(2 * m + s, s, 16 * m + 16, 2 * m + s - 1)

            def edges_general():
                with g.Fori(0, BATCHES) as i:
                    g.wait_ge(turns, i * TURNS + 1 + 48)
                    g.sem_inc(gathers_begun, 1)
                    for j in range(TILES):
                        G.indirect_dma_start(out=gat[:, 0, j * HID:(j + 1) * HID], out_offset=None, in_=q_tab,
                                             in_offset=bass.IndirectOffsetOnAxis(ap=idx[:, 0, j:j + 1], axis=0)).then_inc(turns, 16)

            general(g, edges, edges_general)
            g.wait_ge(flag2_set, 1)
            large = g.value_load(flags[0:1, 1:2], min_val=0, max_val=1)
            with g.If(large > 0):
                with g.Fori(0, ITERS + 1) as t:
                    with g.Fori(0, BATCHES) as i:
                        g.wait_ge(turns2, t * PASS + 17 + i * YTURNS + 1 + 32)
                        g.sem_inc(gathers_begun, 1)
                        for j in range(TILES):
                            G.indirect_dma_start(out=ygat[:, j * FEAT:(j + 1) * FEAT], out_offset=None, in_=y_tab,
                                                 in_offset=bass.IndirectOffsetOnAxis(ap=gidx[:, 1, j:j + 1], axis=0)).then_inc(turns2, 16)

        @block.scalar
        def _(act):
            for dst_ap, src_ap in ((wpq[FEAT:FEAT + 1, 0:HID], b1.rearrange("(o n) -> o n", o=1)),
                                   (wpq[0:FEAT, 0:HID], W1[0:FEAT, :]), (wpq[0:FEAT, HID:2 * HID], W1[FEAT:2 * FEAT, :]),
                                   (w1b[:, :], W1[FEAT:2 * FEAT, :]),
                                   (w2s[0:HID, :], W2), (w2s[HID:2 * HID, :], W2), (w3s[:, :], W3),
                                   (w4s[0:HID, 0:FEAT], W4), (w4s[HID:HID + 1, 0:FEAT], b4.rearrange("(o n) -> o n", o=1)),
                                   (b2c[:, :], b2.rearrange("(n o) -> n o", o=1)),
                                   (b3r[:, :, :], b3.rearrange("(o n) -> o n", o=1).unsqueeze(1).to_broadcast([1, TILES, HID]))):
                act.dma_start(dst_ap, src_ap).then_inc(s_w, 16)
            act.wait_ge(s_var, 1)
            A.activation(stats[:, 2, :], stats[:, 1, :], ACT.Sqrt).then_inc(s_std, 1)
            for f, (what, n) in enumerate(FILLS):
                act.wait_ge(s_fill, f + 1)
                bank = banks[f % 8]
                if what == "hT":
                    w = len(groups(n)) * P
                    A.activation(hT[0:FEAT, n * 512:n * 512 + w], bank[0:FEAT, 0:w], ACT.Copy).then_inc(s_evac, 1)
                elif what == "pq":
                    k = len(groups(n))
                    A.activation(pq[:, 4 * n:4 * n + k, :], bank[:, 0:k * P].rearrange("p (b f) -> p b f", f=P), ACT.Copy).then_inc(s_evac, 1)
                else:
                    dest = {"src": idxt, "lo": locol, "key": key, "rel": relcol, "dcol": dcolt}[what]
                    gc = P if n == 0 else GB
                    A.activation(dest[:, n * P:n * P + gc, :].rearrange("p g j -> p j g"),
                                 bank[:, :].rearrange("p (j g) -> p j g", j=TILES)[:, :, 0:gc], ACT.Copy).then_inc(s_evac, 1)

            def stage1(i):
                act.wait_ge(h1_done, i + 1)
                if not isinstance(i, int) or i >= 1:
                    act.wait_ge(h1t_done, i)
                A.activation(h1s[:, :], H1[:, 0:TILES * HID], ACT.Relu).then_inc(h1_out, 1)

            def stage2(i):
                act.wait_ge(h1t_done, i + 1)
                if not isinstance(i, int) or i >= 1:
                    act.wait_ge(h2_done, i)
                A.activation(h1t[:, :], H1T[:, 0:2 * P], ACT.Copy).then_inc(h1t_out, 1)

            def stage3(i):
                act.wait_ge(h2_done, i + 1)
                if not isinstance(i, int) or i >= 1:
                    act.wait_ge(h3_done, i)
                A.activation(h2s[:, :].rearrange("p (q e) -> p q e", q=2), psum[:, 2:4, 0:256], ACT.Relu, bias=b2c[:, 0:1]).then_inc(h2_out, 1)

            def stage4(i):
                act.wait_ge(h3_done, i + 1)
                if not isinstance(i, int) or i >= 1:
                    act.wait_ge(seg_done, i)
                A.activation(h3s[:, :, 0:HID], H3[:, 0:TILES * HID].rearrange("p (j f) -> p j f", f=HID), ACT.Relu).then_inc(h3_out, 1)

            def edges():
                stage1(0)
                stage2(0)
                stage3(0)
                stage1(1)
                stage4(0)
                stage2(1)
                stage3(1)
                with act.Fori(1, BATCHES // 2) as m:
                    for s in range(2):
                        i = 2 * m + s
                        stage1(i)
                        stage4(i - 1)
                        stage2(i)
                        stage3(i)
                stage4(BATCHES - 1)

            def edges_general():
                with act.Fori(0, BATCHES) as i:
                    at = i * TURNS + 1 + MLP_AT
                    act.wait_ge(turns, at)
                    A.activation(h1s, H1[:, 0:TILES * HID], ACT.Relu).then_inc(turns, 1)
                    act.wait_ge(turns, at + 2)
                    A.activation(h1t, H1T[:, 0:2 * P], ACT.Copy).then_inc(turns, 1)
                    act.wait_ge(turns, at + 4)
                    A.activation(h2s.rearrange("p (q e) -> p q e", q=2), psum[:, 2:4, 0:256], ACT.Relu, bias=b2c[:, 0:1]).then_inc(turns, 1)
                    act.wait_ge(turns, at + 6)
                    A.activation(h3s[:, :, 0:HID], H3[:, 0:TILES * HID].rearrange("p (j f) -> p j f", f=HID), ACT.Relu).then_inc(turns, 1)

            general(act, edges, edges_general)
            act.wait_ge(edges_done, 1)
            def turn_out(w, s, k):
                act.wait_ge(turned, w + 1)
                for f in range(3):
                    lo, hi = SPLIT[f]
                    ins = A.activation(turned_cols(w, lo * P, (hi - lo) * P)[0:k, :], bankb[4 * s + f][0:k, 0:(hi - lo) * P], ACT.Copy)
                ins.then_inc(turn_a, 1)

            with act.Fori(0, BLOCKS // 2) as m:
                for s in range(2):
                    turn_out(2 * m + s, s, P)
            turn_out(BLOCKS - 1, 0, LASTN)
            for n in range(CHUNKS):
                w = min(CHUNK, NODES - n * CHUNK)
                act.wait_ge(dg_done, n + 1)
                A.activation(degrow[0:1, n * CHUNK:n * CHUNK + w], banks[n % 2][0:1, 0:w], ACT.Copy).then_inc(dg_out, 1)
            act.wait_ge(v2, 1)
            A.activation(stats[:, 2, :], stats[:, 1, :], ACT.Sqrt).then_inc(sd2, 1)
            act.wait_ge(dmx, 1)
            A.activation(stats[:, 1, :], stats[:, 0, :], ACT.Sqrt).then_inc(sdd, 1)

            def chunk_out(t, n, par):
                q = CHUNKS * t + n
                w = min(CHUNK, NODES - n * CHUNK)
                act.wait_ge(o_done, q + 1)
                if not isinstance(t, int) or q >= 2:
                    act.wait_ge(r_done, q - 1)
                A.activation(osb[par][:, 0:w], banks[par][0:3 * FEAT, 0:w], ACT.Copy).then_inc(o_out, 1)

            for n in range(CHUNKS):
                chunk_out(0, n, n % 2)
            with act.Fori(0, (ITERS - 2) // 2) as m:
                for u in range(2):
                    for n in range(CHUNKS):
                        chunk_out(2 * m + 1 + u, n, (1 + u + n) % 2)
            for n in range(CHUNKS):
                chunk_out(ITERS - 1, n, (ITERS - 1 + n) % 2)
            act.wait_ge(flag2_set, 1)
            large = act.value_load(flags[0:1, 1:2], min_val=0, max_val=1)
            with act.If(large > 0):
                act.wait_ge(dmx, 2)
                A.activation(stats[:, 1, :], stats[:, 0, :], ACT.Sqrt).then_inc(sdd, 1)

        @block.vector
        def _(dve):
            chain = [0]

            def link(ins):
                chain[0] += 1
                ins.then_inc(s_dve, 1)
                dve.wait_ge(s_dve, chain[0])

            def wide(ap):
                return ap.unsqueeze(2).to_broadcast([P, ap.shape[1], FEAT])

            def center(xin, xc, sq):
                link(V.tensor_reduce(stats[:, 0, :], xin, AX.X, ALU.add))
                link(V.tensor_scalar(stats[:, 1, :], stats[:, 0, :], 1.0 / FEAT, None, ALU.mult))
                link(V.tensor_tensor(xc, xin, wide(stats[:, 1, :]), ALU.subtract))
                link(V.tensor_tensor(sq, xc, xc, ALU.mult))
                link(V.tensor_reduce(stats[:, 0, :], sq, AX.X, ALU.add))

            V.memset(x_sb[:, BLOCKS - 1, :], 0.0).then_inc(s_pads, 1)
            V.memset(dN[:, 1, :], PAD_DST).then_inc(s_pads, 1)
            V.memset(sN[:, 1, :], 0).then_inc(s_pads, 1)
            V.memset(h3s[:, :, HID:HID + 1], 1.0).then_inc(s_h3one, 1)
            V.memset(ones1[:, :], 1.0).then_inc(s_h3one, 1)
            V.memset(onesb[:, :], 1.0).then_inc(s_h3one, 1)
            V.memset(hT[FEAT:FEAT + 1, :], 1.0).then_inc(s_h3one, 1)
            V.memset(wpq[FEAT:FEAT + 1, HID:2 * HID], 0.0).then_inc(s_h3one, 1)
            V.memset(w4s[:, FEAT:FEAT + 1], 0.0).then_inc(s_h3one, 1)
            dve.wait_ge(s_h3one, 6)
            V.memset(w4s[HID:HID + 1, FEAT:FEAT + 1], 1.0).then_inc(s_h3one, 1)
            dve.wait_ge(s_x, 32)
            center(x_sb, xc, sq)
            V.tensor_scalar(stats[:, 1, :], stats[:, 0, :], 1.0 / FEAT, EPS, ALU.mult, ALU.add).then_inc(s_var, 1)
            dve.wait_ge(s_w, 16 * 11)
            V.tensor_tensor(wpq[0:FEAT, 0:HID], wpq[0:FEAT, 0:HID], w1b[:, :], ALU.subtract).then_inc(s_wpq, 1)
            dve.wait_ge(s_std, 1)
            link(V.reciprocal(stats[:, 3, :], stats[:, 2, :]))
            link(V.tensor_tensor(hn, xc, stats[:, 3, :].unsqueeze(2).to_broadcast([P, BLOCKS, FEAT]), ALU.mult))
            V.tensor_scalar(hn, hn, 0.0, None, ALU.max).then_inc(s_h, 1)
            dve.wait_ge(s_edges, 96)
            V.tensor_copy(srcf[:, :, :], sN).then_inc(s_idxN, 1)
            link(V.tensor_scalar(lN, sN, P - 1, None, ALU.bitwise_and))
            V.tensor_copy(floF, lN).then_inc(s_idxN, 1)
            link(V.tensor_scalar(aN, sN, 7, None, ALU.arith_shift_right))
            d4 = dN.rearrange("p c (u e) -> p (c u) e", u=2)
            link(V.tensor_reduce(pmn[:, :], d4, AX.X, ALU.min))
            link(V.tensor_reduce(pmx[:, :], d4, AX.X, ALU.max))
            link(V.tensor_scalar(pmn[:, :], pmn[:, :], float(NODES - 1), None, ALU.min))
            link(V.tensor_scalar(pmx[:, :], pmx[:, :], float(NODES - 1), None, ALU.min))
            pn = pmn[:, :].rearrange("p (c u) -> p c u", u=2)
            px = pmx[:, :].rearrange("p (c u) -> p c u", u=2)
            link(V.tensor_tensor(bmn[:, :], pn[:, :, 0], pn[:, :, 1], ALU.min))
            link(V.tensor_tensor(bmx[:, :], px[:, :, 0], px[:, :, 1], ALU.max))
            for c in range(2):
                link(V.tensor_scalar(relF[:, c, :], dN[:, c, :], bmn[:, c:c + 1], None, ALU.subtract))
                for u in range(2):
                    q = slice(u * 256, u * 256 + 256)
                    link(V.tensor_scalar(keyF[:, c, q], dN[:, c, q], pmn[:, 2 * c + u:2 * c + u + 1], float(HI), ALU.subtract, ALU.mult))
            V.tensor_copy(relN, relF).then_inc(s_idxN, 1)
            V.tensor_tensor(keyF, keyF, aN, ALU.add).then_inc(s_idxN, 1)
            V.tensor_scalar(dclF, dN, float(SCOLS - 1), None, ALU.min).then_inc(s_idxN, 1)
            link(V.tensor_tensor(pmx[:, :], pmx[:, :], pmn[:, :], ALU.subtract))
            link(V.tensor_tensor(bmx[:, :], bmx[:, :], bmn[:, :], ALU.subtract))
            link(V.tensor_scalar(pfl[:, :], pmx[:, :], float(PSPAN), None, ALU.is_ge))
            link(V.tensor_scalar(bmx[:, :], bmx[:, :], float(SPAN), None, ALU.is_ge))
            fl = pfl[:, :].rearrange("p (c u) -> p c u", u=2)
            link(V.tensor_tensor(bmx[:, :], bmx[:, :], fl[:, :, 0], ALU.max))
            link(V.tensor_tensor(tabN[:, :, 3], bmx[:, :], fl[:, :, 1], ALU.max))
            link(V.tensor_copy(tabN[:, :, 0], bmn[:, :]))
            link(V.tensor_scalar(tabN[:, :, 1:3], pn, float(HI), None, ALU.mult))
            V.memset(stats[:, 0, 0:1], 0.0).then_inc(s_keyN, 1)
            V.memset(sT[0:HID + 1, :], 0.0).then_inc(s_clear, 1)
            half = T0 // 2 // 2 * 2
            V.memset(C[:, 0:half], 0.0).then_inc(s_clear, 1)
            dve.wait_ge(s_evac, PRE)
            dve.wait_ge(s_tables, 48)
            dve.wait_ge(s_rel, 32)
            dve.wait_ge(s_gen, 48)
            V.memset(C[:, T0:CCOLS], 0.0).then_inc(s_clear, 1)
            dve.wait_ge(s_clear, 4)
            dve.wait_ge(s_tab, 16)

            def is0(i, n):
                return isinstance(i, int) and i < n

            def onehots(i, s, loads):
                dve.wait_ge(rel_loaded[s], loads)
                if not is0(i, 2):
                    dve.wait_ge(h1_done, i - 1)
                V.tensor_scalar(ohT[:, s, :], relb[:, s, :], pcol[0:SPAN, 0:1], None, ALU.is_equal).then_inc(ohT_made, 1)
                if not is0(i, 2):
                    dve.wait_ge(seg_done, i - 1)
                V.tensor_tensor(ohS[:, s, :, :], iota_s[:, :].unsqueeze(1).to_broadcast([P, TILES, SPAN]),
                                relcol[:, bass.ds(i, 1), :].rearrange("p o j -> p (o j)").unsqueeze(2).to_broadcast([P, TILES, SPAN]),
                                ALU.is_equal).then_inc(ohS_made, 1)

            def count_onehots(i, s):
                if not is0(i, 2):
                    dve.wait_ge(cp_done[1], i - 1)
                V.tensor_tensor(ohL[:, s, :, :], iota_l[:, :].unsqueeze(1).to_broadcast([P, TILES, P]),
                                locol[:, bass.ds(i, 1), :].rearrange("p o j -> p (o j)").unsqueeze(2).to_broadcast([P, TILES, P]),
                                ALU.is_equal)
                kcol = key[:, bass.ds(i, 1), :].rearrange("p o j -> p (o j)")
                for j in range(TILES):
                    ins = V.tensor_scalar(ohC[:, s, j, :], iota_c[:, :], kcol[:, j:j + 1], None, ALU.is_equal)
                    if j % 2:
                        ins.then_inc(ohC_made[j // 2], 1)

            def add_counts(i):
                for u in range(2):
                    b = dve.value_load(tab[0:1, bass.ds(4 * i + 1 + u, 1)], min_val=0, max_val=(NODES - 1) * HI)
                    dve.wait_ge(cp_done[u], i + 1)
                    if u == 0 and not is0(i, 1):
                        dve.wait_ge(cp_added[1], i)
                    if u == 1:
                        dve.wait_ge(cp_added[0], i + 1)
                    w = C[:, bass.ds(b, PCOLS)]
                    V.tensor_tensor(w, CP[u][:, 0:PCOLS], w, ALU.add).then_inc(cp_added[u], 1)

            def add_sums(i):
                b = dve.value_load(tab[0:1, bass.ds(4 * i, 1)], min_val=0, max_val=NODES - 1)
                dve.wait_ge(seg_done, i + 1)
                if not is0(i, 1):
                    dve.wait_ge(seg_added, i)
                w = sT[0:HID + 1, bass.ds(b, SPAN)]
                V.tensor_tensor(w, SEG[0:HID + 1, 0:SPAN], w, ALU.add).then_inc(seg_added, 1)

            def edges():
                onehots(0, 0, 16)
                count_onehots(0, 0)
                onehots(1, 1, 16)
                count_onehots(1, 1)
                add_counts(0)
                add_sums(0)
                with dve.Fori(1, BATCHES // 2) as m:
                    for s in range(2):
                        i = 2 * m + s
                        onehots(i, s, 16 * m + 16)
                        count_onehots(i, s)
                        add_counts(i - 1)
                        add_sums(i - 1)
                add_counts(BATCHES - 1)
                add_sums(BATCHES - 1)
                dve.wait_ge(cp_added[1], BATCHES)
                dve.wait_ge(seg_added, BATCHES)

            def edges_general():
                wcol = ohS[0:SPAN, 1, 0, 0:1]
                with dve.Fori(0, BATCHES) as i:
                    at = i * TURNS + 1
                    dve.wait_ge(turns, at + LOADS + 1)
                    V.tensor_copy(wcol, pcol[0:SPAN, 0:1]).then_inc(turns, 1)
                    with dve.Fori(0, NW) as w:
                        dve.wait_ge(turns, at + P_AT + w * PSTEP + 16)
                        V.tensor_scalar(ohT[:, 0, :], grow, wcol, None, ALU.is_equal).then_inc(turns, 1)
                        dve.wait_ge(turns, at + P_AT + w * PSTEP + 18)
                        V.tensor_scalar(wcol, wcol, float(SPAN), None, ALU.add).then_inc(turns, 1)
                    dve.wait_ge(turns, at + MLP_AT + 7)
                    V.memset(roff[:, :], 0.0).then_inc(turns, 1)
                    tcol = gidx[:, 1, :].unsqueeze(2).to_broadcast([P, TILES, SPAN])
                    with dve.Fori(0, NW) as w:
                        dve.wait_ge(turns, at + S_AT + w * SSTEP)
                        V.scalar_tensor_tensor(out=ohS[:, 0, :, :], in0=iota_s[:, :].unsqueeze(1).to_broadcast([P, TILES, SPAN]),
                                               scalar=roff[:, 0:1], in1=tcol, op0=ALU.add, op1=ALU.is_equal).then_inc(turns, 1)
                        dve.wait_ge(turns, at + S_AT + w * SSTEP + 2)
                        v = sT[0:HID + 1, bass.ds(w * SPAN, SPAN)]
                        V.tensor_tensor(v, SEG[0:HID + 1, 0:SPAN], v, ALU.add).then_inc(turns, 1)
                        dve.wait_ge(turns, at + S_AT + w * SSTEP + 3)
                        V.tensor_scalar(roff[:, :], roff[:, :], float(SPAN), None, ALU.add).then_inc(turns, 1)
                    dve.wait_ge(turns, at + K_AT)
                    V.tensor_scalar(gidx[:, 2, :], idx[:, 0, :], 7, None, ALU.arith_shift_right).then_inc(turns, 1)
                    dve.wait_ge(turns, at + K_AT + 1)
                    V.tensor_scalar(gidx[:, 3, :], idx[:, 0, :], P - 1, None, ALU.bitwise_and).then_inc(turns, 1)
                    dve.wait_ge(turns, at + K_AT + 2)
                    gkey = gidx[:, 4, :].bitcast(F32)
                    V.tensor_scalar(gkey, gidx[:, 1, :], float(HI), None, ALU.mult).then_inc(turns, 1)
                    dve.wait_ge(turns, at + K_AT + 3)
                    V.tensor_tensor(gkey, gkey, gidx[:, 2, :], ALU.add).then_inc(turns, 1)
                    dve.wait_ge(turns, at + K_AT + 4)
                    V.tensor_tensor(ohL[:, 0, :, :], iota_l[:, :].unsqueeze(1).to_broadcast([P, TILES, P]),
                                    gidx[:, 3, :].unsqueeze(2).to_broadcast([P, TILES, P]), ALU.is_equal).then_inc(turns, 1)
                    dve.wait_ge(turns, at + K_AT + 5)
                    V.memset(roff[:, :], 0.0).then_inc(turns, 1)
                    with dve.Fori(0, NC) as w:
                        dve.wait_ge(turns, at + C_AT + w * CSTEP)
                        for j in range(TILES):
                            last = V.tensor_scalar(ohC[:, 0, j, :], iota_c[:, :], roff[:, 0:1], gkey[:, j:j + 1], ALU.add, ALU.is_equal)
                        last.then_inc(turns, 1)
                        dve.wait_ge(turns, at + C_AT + w * CSTEP + 2)
                        v = C[:, bass.ds(w * PCOLS, PCOLS)]
                        V.tensor_tensor(v, CP[0][:, 0:PCOLS], v, ALU.add).then_inc(turns, 1)
                        dve.wait_ge(turns, at + C_AT + w * CSTEP + 3)
                        V.tensor_scalar(roff[:, :], roff[:, :], float(PCOLS), None, ALU.add).then_inc(turns, 1)
                dve.wait_ge(turns, BATCHES * TURNS + 1)

            V.tensor_reduce(flags[:, 0:1], tab[:, :].rearrange("o (g c) -> o g c", c=4)[:, :, 3], AX.X, ALU.max).then_inc(flag_set, 1)
            dve.sem_inc(turns, 1)
            general(dve, edges, edges_general)
            dve.sem_inc(edges_done, 1)
            V.memset(x1[:, BLOCKS - 1, :], 0.0).then_inc(s_x1pad, 1)

            def copy_block(w, s, k):
                if later(w, 2):
                    dve.wait_ge(turned, w - 1)
                V.tensor_copy(stage[s][:, 0:k * HI], C[:, bass.ds(w * (P * HI), k * HI)]).then_inc(staged, 1)

            def turn_out(w, s, k):
                dve.wait_ge(turned, w + 1)
                lo = SPLIT[3][0] * P
                V.tensor_copy(turned_cols(w, lo, NODES - lo)[0:k, :], bankb[4 * s + 3][0:k, 0:NODES - lo]).then_inc(turn_d, 1)

            def later(w, n):
                return not (isinstance(w, int) and w < n)

            copy_block(0, 0, P)
            copy_block(1, 1, P)
            turn_out(0, 0, P)
            with dve.Fori(0, BLOCKS // 2 - 1) as m:
                for s in range(2):
                    copy_block(2 * m + 2 + s, s, P)
                    turn_out(2 * m + 1 + s, 1 - s, P)
            copy_block(BLOCKS - 1, 0, LASTN)
            turn_out(BLOCKS - 2, 1, P)
            turn_out(BLOCKS - 1, 0, LASTN)

            dve.wait_ge(m_done, 1)
            dve.wait_ge(s_x1, 32)
            msum = [(banks[6], 0, MB), (banks[7], MB, BLOCKS)]
            tmpg = stage[1].bitcast(F32)[:, 0:BLOCKS * FEAT].rearrange("p (b f) -> p b f", f=FEAT)
            tmpf = stage[0].bitcast(F32)[:, 0:BLOCKS * FEAT].rearrange("p (b f) -> p b f", f=FEAT)
            for b, lo, hi in msum:
                v = b[:, 0:(hi - lo) * (FEAT + 1)].rearrange("p (b f) -> p b f", f=FEAT + 1)
                link(V.tensor_scalar(stats[:, 0, lo:hi], v[:, :, FEAT], 1.0, None, ALU.max))
            link(V.reciprocal(stats[:, 1, :], stats[:, 0, :]))
            for b, lo, hi in msum:
                v = b[:, 0:(hi - lo) * (FEAT + 1)].rearrange("p (b f) -> p b f", f=FEAT + 1)
                link(V.tensor_tensor(tmpf[:, lo:hi, :], v[:, :, 0:FEAT], wide(stats[:, 1, lo:hi]), ALU.mult))
            link(V.tensor_tensor(x1, x1, tmpf, ALU.add))
            center(x1, ah, tmpf)
            V.tensor_scalar(stats[:, 1, :], stats[:, 0, :], 1.0 / FEAT, EPS, ALU.mult, ALU.add).then_inc(v2, 1)
            dve.wait_ge(sd2, 1)
            link(V.reciprocal(stats[:, 3, :], stats[:, 2, :]))
            link(V.tensor_tensor(hg, ah, wide(stats[:, 3, :]), ALU.mult))
            link(V.tensor_scalar(hg, hg, 0.0, None, ALU.max))
            dve.wait_ge(dg_col, 1)
            V.tensor_scalar(stats[:, 0, :], banks[5][:, 0:BLOCKS], 1.0, None, ALU.max).then_inc(dmx, 1)
            dve.wait_ge(sdd, 1)
            link(V.reciprocal(stats[:, 2, :], stats[:, 1, :]))
            dinv, c1, cf = stats[:, 2, :], stats[:, 3, :], stats[:, 0, :]
            link(V.scalar_tensor_tensor(out=c1, in0=dinv, scalar=BETA, in1=dinv, op0=ALU.mult, op1=ALU.mult))
            link(V.tensor_scalar(cf, dinv, BETA / GAMMA, None, ALU.mult))
            link(V.tensor_tensor(tmpf, hg, wide(dinv), ALU.mult))
            link(V.tensor_scalar(ah, tmpf, ALPHA, None, ALU.mult))
            link(V.tensor_scalar(hg, hg, ALPHA / GAMMA, None, ALU.mult))

            def split(y, res, dest):
                link(V.tensor_copy(dest[:, :, 0, :], y))
                link(V.tensor_tensor(res, y, dest[:, :, 0, :], ALU.subtract))
                link(V.tensor_copy(dest[:, :, 1, :], res))
                return V.tensor_tensor(dest[:, :, 2, :], res, dest[:, :, 1, :], ALU.subtract)

            for k in range(3):
                q = slice(k * FEAT, (k + 1) * FEAT)
                V.tensor_copy(sum3[q, :], ident[q, q]).then_inc(ones_set, 1)
            split(tmpf, tmpg, y3[0]).then_inc(y_set, 1)
            dve.wait_ge(y_set, 1)
            V.memset(maxima, 0.0).then_inc(scanned, 1)

            def new_y(t, n, par, src_par, last=False):
                q = CHUNKS * t + n
                lo, hi = 4 * n, min(4 * n + 4, BLOCKS)
                k = hi - lo
                rows = P if hi < BLOCKS else LASTN
                dve.wait_ge(r_done, q + 1)
                if last and n:
                    dve.wait_ge(s_res, n)
                rv = banks[2 + par][0:rows, 0:k * FEAT].rearrange("p (b f) -> p b f", f=FEAT)
                c = (cf if last else c1)[0:rows, lo:hi].unsqueeze(2).to_broadcast([rows, k, FEAT])
                yb, rb = yv[0:rows, 0:k, :], yr[0:rows, 0:k, :]
                done = [0]

                def step(ins):
                    done[0] += 1
                    ins.then_inc(y_step, 1)
                    dve.wait_ge(y_step, (5 * q if not last else 5 * CHUNKS * t + n) + done[0])

                step(V.tensor_tensor(yb, rv, c, ALU.mult))
                if last:
                    V.tensor_tensor(yb, yb, hg[0:rows, lo:hi, :], ALU.add).then_inc(y_made, 1)
                    dve.wait_ge(y_made, q + 1)
                    V.tensor_tensor(ycur[0:rows, lo:hi, :], x1[0:rows, lo:hi, :], yb, ALU.add).then_inc(s_res, 1)
                    return
                step(V.tensor_tensor(yb, yb, ah[0:rows, lo:hi, :], ALU.add))
                dest = y3[1 - src_par][0:rows, lo:hi]
                step(V.tensor_copy(dest[:, :, 0, :], yb))
                step(V.tensor_tensor(rb, yb, dest[:, :, 0, :], ALU.subtract))
                step(V.tensor_copy(dest[:, :, 1, :], rb))
                V.tensor_tensor(dest[:, :, 2, :], rb, dest[:, :, 1, :], ALU.subtract).then_inc(y_made, 1)

            for n in range(CHUNKS):
                new_y(0, n, n % 2, 0)
            with dve.Fori(0, (ITERS - 2) // 2) as m:
                for u in range(2):
                    for n in range(CHUNKS):
                        new_y(2 * m + 1 + u, n, (1 + u + n) % 2, (1 + u) % 2)
                        if n < SCANS:
                            at = (2 * m + u) * SCANS + n
                            dve.wait_ge(scanned, at + 1)
                            V.tensor_tensor(maxima, maxima, C[:, bass.ds(at * SCAN, SCAN)], ALU.max).then_inc(scanned, 1)
            dve.wait_ge(scanned, (ITERS - 2) * SCANS + 1)
            V.tensor_reduce(roff[:, :], maxima, AX.X, ALU.max).then_inc(s_max, 1)
            for n in range(CHUNKS):
                new_y(ITERS - 1, n, (ITERS - 1 + n) % 2, (ITERS - 1) % 2, last=True)
                if n == 2:
                    dve.wait_ge(s_max2, 32)
                    link(V.tensor_reduce(mrow[:, 0:1], mrow[:, 1:P + 1], AX.X, ALU.max))
                    V.tensor_scalar(flags[:, 1:2], mrow[:, 0:1], 256.0, None, ALU.is_ge).then_inc(flag2_set, 1)

            def passes(t, final=False):
                with dve.Fori(0, BATCHES) as i:
                    at = t * PASS + 17 + i * YTURNS + 1 + Y_LOADS
                    dve.wait_ge(turns2, at)
                    V.tensor_scalar(gidx[:, 2, :], gidx[:, 0, :], 7, None, ALU.arith_shift_right).then_inc(turns2, 1)
                    dve.wait_ge(turns2, at + 1)
                    V.tensor_scalar(gidx[:, 3, :], gidx[:, 0, :], P - 1, None, ALU.bitwise_and).then_inc(turns2, 1)
                    dve.wait_ge(turns2, at + 2)
                    V.tensor_tensor(ylo, iota_l[:, :].unsqueeze(1).to_broadcast([P, TILES, P]),
                                    gidx[:, 3, :].unsqueeze(2).to_broadcast([P, TILES, P]), ALU.is_equal).then_inc(turns2, 1)
                    dve.wait_ge(turns2, at + 3)
                    V.tensor_tensor(yhi, iota_l[:, 0:HI].unsqueeze(1).to_broadcast([P, TILES, HI]),
                                    gidx[:, 2, :].unsqueeze(2).to_broadcast([P, TILES, HI]), ALU.is_equal).then_inc(turns2, 1)
                    for j in range(TILES):
                        dve.wait_ge(turns2, at + 4 + 2 * j)
                        V.tensor_tensor(yexp, yhi[:, j, :].unsqueeze(2).to_broadcast([P, HI, FEAT]),
                                        ygat[:, j * FEAT:(j + 1) * FEAT].unsqueeze(1).to_broadcast([P, HI, FEAT]), ALU.mult).then_inc(turns2, 1)
                dve.wait_ge(turns2, (t + 1) * PASS)

            dve.wait_ge(flag2_set, 1)
            large = dve.value_load(flags[0:1, 1:2], min_val=0, max_val=1)
            with dve.If(large > 0):
                dve.wait_ge(s_out, 16 * CHUNKS)
                sums = [psum[:, 0, 0:GCOL * FEAT].rearrange("p (b f) -> p b f", f=FEAT),
                        psum[:, 1, 0:(HI - GCOL) * FEAT].rearrange("p (b f) -> p b f", f=FEAT)]
                parts = [(sums[0], 0, GCOL), (sums[1], GCOL, HI)]
                link(V.memset(zrow, 0.0))
                link(V.memset(ycur, 1.0))
                link(V.memset(ycur[:, BLOCKS - 1, :], 0.0))
                link(V.memset(ycur[0:LASTN, BLOCKS - 1, :], 1.0))
                dve.sem_inc(turns2, 1)
                passes(0)
                for v, lo, hi in parts:
                    link(V.tensor_scalar(stats[:, 0, lo:hi], v[:, :, 0], 1.0, None, ALU.max))
                V.memset(roff[:, :], 0.0).then_inc(dmx, 1)
                dve.wait_ge(sdd, 2)
                link(V.reciprocal(stats[:, 2, :], stats[:, 1, :]))
                link(V.scalar_tensor_tensor(out=c1, in0=dinv, scalar=BETA, in1=dinv, op0=ALU.mult, op1=ALU.mult))
                link(V.tensor_scalar(cf, dinv, BETA / GAMMA, None, ALU.mult))
                link(V.tensor_tensor(ah, hg, wide(dinv), ALU.mult))
                link(V.tensor_scalar(ycur, ah, GAMMA / ALPHA, None, ALU.mult))
                V.tensor_scalar(ah, ah, GAMMA, None, ALU.mult).then_inc(turns2, 1)
                with dve.Fori(1, ITERS) as t:
                    passes(t)
                    for k, (v, lo, hi) in enumerate(parts):
                        V.tensor_tensor(ycur[:, lo:hi, :], v, wide(c1[:, lo:hi]), ALU.mult).then_inc(y2_step, 1)
                    dve.wait_ge(y2_step, 2 * t)
                    V.tensor_tensor(ycur, ycur, ah, ALU.add).then_inc(turns2, 1)
                passes(ITERS)
                for k, (v, lo, hi) in enumerate(parts):
                    link(V.tensor_tensor(ycur[:, lo:hi, :], v, wide(cf[:, lo:hi]), ALU.mult))
                link(V.tensor_tensor(ycur, ycur, hg, ALU.add))
                V.tensor_tensor(ycur, ycur, x1, ALU.add).then_inc(turns2, 1)

        @block.tensor
        def _(pe):
            pe.wait_ge(s_const, 8)
            for f, (what, n) in enumerate(FILLS):
                bank = banks[f % 8]
                if f >= 8:
                    pe.wait_ge(s_evac, f - 7)
                if what == "hT":
                    pe.wait_ge(s_h, 1)
                    for k, b in enumerate(groups(n)):
                        last = T.transpose(bank[0:FEAT, k * P:(k + 1) * P], hn[:, b, :], ident[:, :])
                elif what == "pq":
                    pe.wait_ge(s_evac, 7)
                    pe.wait_ge(s_wpq, 1)
                    pe.wait_ge(s_h3one, 7)
                    for k, b in enumerate(groups(n)):
                        last = T.matmul(bank[:, k * P:(k + 1) * P], hT[:, b * P:(b + 1) * P], wpq[:, :], start=True, stop=True)
                else:
                    pe.wait_ge(s_idxN, {"src": 1, "lo": 2, "rel": 3, "key": 4, "dcol": 5}[what])
                    gc = P if n == 0 else GB
                    for j in range(TILES):
                        last = T.transpose(bank[:, j * P:j * P + gc], NAT[what][0:gc, n, j * P:(j + 1) * P], ident[0:gc, 0:gc])
                last.then_inc(s_fill, 1)
            pe.wait_ge(s_evac, PRE)

            def later(i, n):
                return not (isinstance(i, int) and i < n)

            def stage1(i, s, loads, lands):
                pe.wait_ge(landed[s], lands)
                if later(i, 1):
                    pe.wait_ge(h1_out, i)
                T.matmul(H1[:, 0:TILES * HID], ident[:, :], gat[:, s, :], start=True, stop=False, skip_group_check=True)
                pe.wait_ge(pw_loaded[s], loads)
                pe.wait_ge(ohT_made, i + 1)
                for j in range(TILES):
                    last = T.matmul(H1[:, j * HID:(j + 1) * HID], ohT[:, s, j * P:(j + 1) * P], pw[:, s, :],
                                    start=False, stop=True, skip_group_check=True)
                last.then_inc(h1_done, 1)

            def stage2(i):
                pe.wait_ge(h1_out, i + 1)
                if later(i, 1):
                    pe.wait_ge(h1t_out, i)
                for c in range(2):
                    last = T.transpose(H1T[:, c * P:(c + 1) * P], h1s[:, c * P:(c + 1) * P], ident[:, :])
                last.then_inc(h1t_done, 1)

            def stage3(i):
                pe.wait_ge(h1t_out, i + 1)
                if later(i, 1):
                    pe.wait_ge(h2_out, i)
                for q in range(2):
                    last = T.matmul(H2[q][:, 0:256], w2s[q * HID:(q + 1) * HID, :], h1t[q * HID:(q + 1) * HID, :],
                                    start=True, stop=True)
                last.then_inc(h2_done, 1)

            def third_layer():
                T.matmul(H3[:, 0:TILES * HID], ones1[:, :], b3r[:, :, :].rearrange("o j f -> o (j f)"), start=True, stop=False, skip_group_check=True)
                for j in range(TILES):
                    q, c = j % 2, j // 2
                    last = T.matmul(H3[:, j * HID:(j + 1) * HID], h2s[:, q * 256 + c * P:q * 256 + (c + 1) * P], w3s[:, :],
                                    start=False, stop=True, skip_group_check=True)
                return last

            def stage4(i):
                pe.wait_ge(h2_out, i + 1)
                if later(i, 1):
                    pe.wait_ge(h3_out, i)
                third_layer().then_inc(h3_done, 1)

            def stage5(i, s):
                pe.wait_ge(h3_out, i + 1)
                pe.wait_ge(ohS_made, i + 1)
                if later(i, 1):
                    pe.wait_ge(seg_added, i)
                for j in range(TILES):
                    last = T.matmul(SEG[0:HID + 1, 0:SPAN], h3s[:, j, :], ohS[:, s, j, :], start=j == 0, stop=j == TILES - 1)
                last.then_inc(seg_done, 1)

            def counts(i, s):
                for u in range(2):
                    pe.wait_ge(ohC_made[u], i + 1)
                    if later(i, 1):
                        pe.wait_ge(cp_added[u], i)
                    for j in (2 * u, 2 * u + 1):
                        last = T.matmul(CP[u][:, 0:PCOLS], ohL[:, s, j, :], ohC[:, s, j, :], start=j == 2 * u, stop=j == 2 * u + 1)
                    last.then_inc(cp_done[u], 1)

            def edges():
                stage1(0, 0, 16, 64)
                stage2(0)
                stage3(0)
                counts(0, 0)
                stage1(1, 1, 16, 64)
                stage4(0)
                stage2(1)
                stage5(0, 0)
                stage3(1)
                counts(1, 1)
                with pe.Fori(1, BATCHES // 2) as m:
                    for s in range(2):
                        i = 2 * m + s
                        stage1(i, s, 16 * m + 16, 64 * m + 64)
                        stage4(i - 1)
                        stage2(i)
                        stage5(i - 1, 1 - s)
                        stage3(i)
                        counts(i, s)
                stage4(BATCHES - 1)
                stage5(BATCHES - 1, 1)

            def edges_general():
                with pe.Fori(0, BATCHES) as i:
                    at = i * TURNS + 1
                    pe.wait_ge(turns, at + LOADS)
                    T.matmul(H1[:, 0:TILES * HID], ident[:, :], gat[:, 0, :], start=True, stop=False, skip_group_check=True).then_inc(turns, 1)
                    with pe.Fori(0, NW) as w:
                        pe.wait_ge(turns, at + P_AT + w * PSTEP + 17)
                        for j in range(TILES):
                            last = T.matmul(H1[:, j * HID:(j + 1) * HID], ohT[:, 0, j * P:(j + 1) * P], pw[:, 0, :],
                                            start=False, stop=False, skip_group_check=True)
                        last.then_inc(turns, 1)
                    pe.wait_ge(turns, at + MLP_AT + 1)
                    for c in range(2):
                        last = T.transpose(H1T[:, c * P:(c + 1) * P], h1s[:, c * P:(c + 1) * P], ident[:, :])
                    last.then_inc(turns, 1)
                    pe.wait_ge(turns, at + MLP_AT + 3)
                    for q in range(2):
                        last = T.matmul(H2[q][:, 0:256], w2s[q * HID:(q + 1) * HID, :], h1t[q * HID:(q + 1) * HID, :], start=True, stop=True)
                    last.then_inc(turns, 1)
                    pe.wait_ge(turns, at + MLP_AT + 5)
                    third_layer().then_inc(turns, 1)
                    with pe.Fori(0, NW) as w:
                        pe.wait_ge(turns, at + S_AT + w * SSTEP + 1)
                        for j in range(TILES):
                            last = T.matmul(SEG[0:HID + 1, 0:SPAN], h3s[:, j, :], ohS[:, 0, j, :], start=j == 0, stop=j == TILES - 1)
                        last.then_inc(turns, 1)
                    with pe.Fori(0, NC) as w:
                        pe.wait_ge(turns, at + C_AT + w * CSTEP + 1)
                        for j in range(TILES):
                            last = T.matmul(CP[0][:, 0:PCOLS], ohL[:, 0, j, :], ohC[:, 0, j, :], start=j == 0, stop=j == TILES - 1)
                        last.then_inc(turns, 1)

            general(pe, edges, edges_general)
            pe.wait_ge(edges_done, 1)
            def turn(w, s, k):
                pe.wait_ge(staged, w + 1)
                if later(w, 2):
                    pe.wait_ge(turn_a, w - 1)
                    pe.wait_ge(turn_d, w - 1)
                v = stage[s].rearrange("p (t a) -> p t a", a=HI)
                for f, (lo, hi) in enumerate(SPLIT):
                    for a in range(lo, hi):
                        last = T.transpose(bankb[4 * s + f][0:k, (a - lo) * P:(a - lo + 1) * P], v[:, 0:k, a], identb[:, :])
                last.then_inc(turned, 1)

            turn(0, 0, P)
            turn(1, 1, P)
            with pe.Fori(1, BLOCKS // 2) as m:
                for s in range(2):
                    turn(2 * m + s, s, P)
            turn(BLOCKS - 1, 0, LASTN)
            pe.wait_ge(turn_a, BLOCKS)
            pe.wait_ge(turn_d, BLOCKS)
            for b in range(BLOCKS):
                bank, k = (banks[6], b) if b < MB else (banks[7], b - MB)
                last = T.matmul(bank[:, k * (FEAT + 1):(k + 1) * (FEAT + 1)], sT[0:HID + 1, b * P:(b + 1) * P], w4s[:, :], start=True, stop=True)
            last.then_inc(m_done, 1)
            for n in range(CHUNKS):
                w = min(CHUNK, NODES - n * CHUNK)
                if n >= 2:
                    pe.wait_ge(dg_out, n - 1)
                for b in range(BLOCKS):
                    k = P if b < BLOCKS - 1 else LASTN
                    last = T.matmul(banks[n % 2][0:1, 0:w], onesb[0:k, 0:1], C[0:k, b * NODES + n * CHUNK:b * NODES + n * CHUNK + w],
                                    start=b == 0, stop=b == BLOCKS - 1)
                last.then_inc(dg_done, 1)
            pe.wait_ge(dg_out, CHUNKS)
            for b in range(BLOCKS):
                last = T.matmul(banks[5][:, b:b + 1], degrow[0:1, b * P:(b + 1) * P], ones1[0:1, 0:1], start=True, stop=True)
            last.then_inc(dg_col, 1)

            def gather_groups(t, n, par):
                q = CHUNKS * t + n
                pe.wait_ge(o_out, q + 1)
                if later(t, 1) or q >= 2:
                    pe.wait_ge(y_made, q - 1)
                for b in range(4 * n, min(4 * n + 4, BLOCKS)):
                    k = P if b < BLOCKS - 1 else LASTN
                    o = b - 4 * n
                    last = T.matmul(banks[2 + par][0:k, o * FEAT:(o + 1) * FEAT], osb[par][:, o * P:o * P + k], sum3[0:3 * FEAT, :],
                                    start=True, stop=True)
                last.then_inc(r_done, 1)

            def iteration(t, tp):
                for n in range(CHUNKS):
                    q = CHUNKS * t + n
                    par = (tp + n) % 2
                    w = min(CHUNK, NODES - n * CHUNK)
                    if later(t, 1) or q >= 2:
                        pe.wait_ge(o_out, q - 1)
                    for b in range(BLOCKS):
                        if n == 0 and b % 4 == 0 and later(t, 1):
                            pe.wait_ge(y_made, CHUNKS * (t - 1) + b // 4 + 1)
                        k = P if b < BLOCKS - 1 else LASTN
                        last = T.matmul(banks[par][0:3 * FEAT, 0:w], y3[tp][0:k, b, :, :].rearrange("p k f -> p (k f)"),
                                        C[0:k, b * NODES + n * CHUNK:b * NODES + n * CHUNK + w], start=b == 0, stop=b == BLOCKS - 1)
                        if b == 8 and (n > 0 or later(t, 1)):
                            if n > 0:
                                gather_groups(t, n - 1, 1 - par)
                            else:
                                gather_groups(t - 1, CHUNKS - 1, 1 - par)
                    last.then_inc(o_done, 1)

            pe.wait_ge(y_set, 1)
            pe.wait_ge(ones_set, 3)
            iteration(0, 0)
            with pe.Fori(0, (ITERS - 2) // 2) as m:
                iteration(2 * m + 1, 1)
                iteration(2 * m + 2, 0)
            iteration(ITERS - 1, (ITERS - 1) % 2)
            gather_groups(ITERS - 1, CHUNKS - 1, (ITERS + CHUNKS) % 2)
            pe.wait_ge(flag2_set, 1)
            large = pe.value_load(flags[0:1, 1:2], min_val=0, max_val=1)
            with pe.If(large > 0):
                with pe.Fori(0, ITERS + 1) as t:
                    pe.wait_ge(turns2, t * PASS + 1 + 16)
                    for k in range(2):
                        last = T.matmul(banks[k][:, :], ones1[:, :], zrow[0:1, :], start=True, stop=False, skip_group_check=True)
                    last.then_inc(turns2, 1)
                    with pe.Fori(0, BATCHES) as i:
                        at = t * PASS + 17 + i * YTURNS + 1 + YT_AT
                        for j in range(TILES):
                            pe.wait_ge(turns2, at + 2 * j + 1)
                            for k, (lo, hi) in enumerate(((0, GCOL), (GCOL, HI))):
                                last = T.matmul(banks[k][:, 0:(hi - lo) * FEAT], ylo[:, j, :], yexp[:, lo:hi, :].rearrange("p a f -> p (a f)"),
                                                start=False, stop=False, skip_group_check=True)
                            last.then_inc(turns2, 1)


_INS = ["x", "src", "dst"] + [f"L0_gnn_{a}{n}" for n in range(1, 5) for a in "Wb"]


def kernel(**inputs):
    import concourse.bacc as bacc
    from concourse.bass_utils import run_bass_kernel_spmd as run

    nc = bacc.Bacc("TRN2", target_bir_lowering=False, num_devices=1)
    arrays, args = {}, []
    for name in _INS:
        a = np.ascontiguousarray(inputs[name])
        arrays[f"in_{name}"] = a
        args.append(nc.dram_tensor(f"in_{name}", a.shape, mybir.dt.from_np(a.dtype), kind="ExternalInput").ap())
    result = nc.dram_tensor("out_0", (NODES, FEAT), F32, kind="ExternalOutput").ap()
    build(nc, *args, result)
    return run(nc, [arrays], core_ids=[0]).results[0]["out_0"]
```

```python
import numpy as np

import concourse.bass as bass
from concourse import mybir
from contextlib import ExitStack

F32 = mybir.dt.float32
BF16 = mybir.dt.bfloat16
F16 = mybir.dt.float16
I32 = mybir.dt.int32
I16 = mybir.dt.int16
ALU = mybir.AluOpType
ACT = mybir.ActivationFunctionType
AX = mybir.AxisListType

NODES, EDGES, FEAT, HID, HID2 = 3125, 100000, 32, 64, 128
P = 128
BLOCKS = -(-NODES // P)
LASTN = NODES - (BLOCKS - 1) * P
HI = BLOCKS
TILES = 4
BATCH = TILES * P
BATCHES = -(-EDGES // BATCH)
TAIL = EDGES - (BATCHES - 1) * BATCH
GB = BATCHES - P
SPAN = 64
PSPAN = 20
PWIN, PARTS = 32, 3
PCOLS = PSPAN * HI
SLOTS = 4
PROWS = PARTS * PWIN
PAD_DST = 4095
CCOLS = -(-(NODES + PSPAN) * HI // 2) * 2
SCOLS = BLOCKS * P
ITERS, ALPHA, BETA = 10, 0.1, 0.9
GAMMA = float(np.float32(BETA ** ITERS + ALPHA * sum(BETA ** i for i in range(ITERS))))
EPS = 1e-5
CHUNK = 512
CHUNKS = -(-NODES // CHUNK)
SCANS = 4
SCAN = -(-NODES * BLOCKS // ((ITERS - 2) * SCANS) // 2) * 2
assert SCAN * (ITERS - 2) * SCANS <= CCOLS


def build(nc, x, src, dst, W1, b1, W2, b2, W3, b3, W4, b4, out):
    V, A, T, G = nc.vector, nc.scalar, nc.tensor, nc.gpsimd
    ctx = ExitStack()
    with ctx:
        def sb(name, shape, dt):
            return ctx.enter_context(nc.sbuf_tensor(name, shape, dt))

        def sem(name):
            return ctx.enter_context(nc.semaphore(name))

        def dram(name, shape, dt):
            return nc.dram_tensor(name, shape, dt, kind="Internal").ap()

        TABC = 8
        p_tab = dram("p_tab", (SCOLS, PARTS * HID), BF16)
        q_tab = dram("q_tab", (SCOLS, PARTS * HID), BF16)
        idx_d = dram("idx_d", (P, BATCHES * TILES), I32)
        rel_d = dram("rel_d", (BATCHES, BATCH), I16)
        dst_d = dram("dst_d", (BATCHES, BATCH), I32)
        dcol_d = dram("dcol_d", (P, BATCHES * TILES), I32)
        y_tab = dram("y_tab", (SCOLS, FEAT), F32)
        max_d = dram("max_d", (P,), F32)
        tab_d = dram("tab_d", (BATCHES, TABC), I32)

        C = sb("C", [P, CCOLS], BF16)
        sT = sb("sT", [P, SCOLS], F32)
        key = sb("key", [P, BATCHES, TILES], F32)
        locol = sb("locol", [P, BATCHES, TILES], F16)
        hicol = sb("hicol", [P, BATCHES, TILES], F16)
        relcol = sb("relcol", [P, BATCHES, TILES], I16)
        tab = sT[96:97, 0:BATCHES * TABC].bitcast(I32)
        identb = sb("identb", [P, P], BF16)
        iota_c = sb("iota_c", [P, PCOLS], F16)
        iota_l = sb("iota_l", [P, P], F16)
        iota_s = sb("iota_s", [P, SPAN], F16)
        pcol = sb("pcol", [P, 1], F32)
        w2s = sb("w2s", [HID, HID2], F32)
        w3s = sb("w3s", [HID2, HID], F32)
        w4s = sb("w4s", [HID + 1, FEAT + 1], F32)
        b2c = sb("b2c", [HID2, 1], F32)
        ones1 = sb("ones1", [1, P], F32)
        b3p = sb("b3p", [96, TILES, HID], BF16)
        ones3 = sb("ones3", [96, P], BF16)
        pmod = sb("pmod", [P, 1], F32)
        idx = sb("idx", [P, SLOTS, TILES], I32)
        stats = sb("stats", [P, 4, BLOCKS], F32)

        class Region:
            def __init__(self, ap):
                self.ap, self.at = ap, 0

            def take(self, n):
                self.at += n
                assert self.at <= self.ap.shape[1], (self.at, self.ap.shape)
                return self.ap[:, self.at - n:self.at]

        work = sb("work", [P, 7600], F32)
        flags = sb("flags", [1, 2], I32)
        roff = sb("roff", [P, 1], F32)
        gidx = work[:, 1520:1520 + 5 * TILES].bitcast(I32).rearrange("p (c j) -> p c j", j=TILES)
        r = Region(work[:, :])
        gat = r.take(SLOTS * TILES * PARTS * HID // 2).bitcast(BF16).rearrange("p (s j k n) -> p s j k n", s=SLOTS, j=TILES, k=PARTS)
        relb = r.take(BATCH).bitcast(I16).rearrange("p (s n) -> p s n", s=2)[0:PROWS]
        pw = r.take(2 * HID).bitcast(BF16).rearrange("p (s u n) -> p s u n", s=2, u=2)[0:PROWS]
        ohT = r.take(BATCH).bitcast(BF16).rearrange("p (s n) -> p s n", s=2)[0:PROWS]
        ohS = r.take(2 * TILES * SPAN).rearrange("p (s j n) -> p s j n", s=2, j=TILES)
        ohL = r.take(TILES * P).bitcast(BF16).rearrange("p (s j n) -> p s j n", s=2, j=TILES)
        ohH = r.take(TILES * HI).bitcast(BF16).rearrange("p (s j n) -> p s j n", s=2, j=TILES)
        ohC = r.take(TILES * PCOLS).bitcast(BF16).rearrange("p (s j n) -> p s j n", s=2, j=TILES)
        cst = r.take(PCOLS).bitcast(BF16).rearrange("p (u n) -> p u n", u=2)
        h1s = r.take(BATCH)[0:HID]
        h2s = r.take(BATCH)
        h3s = r.take(TILES * (HID + 1)).rearrange("p (j n) -> p j n", j=TILES)
        grow = work[0:PROWS, 2 * TILES * PARTS * HID // 2:2 * TILES * PARTS * HID // 2 + BATCH].bitcast(I32)
        r = Region(work[:, :])
        stage = [r.take(P * HI // 2).bitcast(BF16) for _ in range(2)]
        maxima = stage[1][:, 0:SCAN]
        mrow = stage[1].bitcast(F32)[0:1, 1400:1400 + P + 1]
        ycur = stage[0].bitcast(F32)[:, 0:BLOCKS * FEAT].rearrange("p (b f) -> p b f", f=FEAT)
        ygat = stage[0].bitcast(F32)[:, 800:800 + TILES * FEAT]
        ylo = stage[0].bitcast(F32)[:, 1000:1000 + TILES * P].rearrange("p (j n) -> p j n", j=TILES)
        yexp = stage[1].bitcast(F32)[:, 0:HI * FEAT].rearrange("p (a f) -> p a f", f=FEAT)
        zrow = stage[1].bitcast(F32)[0:1, 1088:1600]
        yhi = stage[1].bitcast(F32)[:, 800:800 + TILES * HI].rearrange("p (j n) -> p j n", j=TILES)
        x1 = r.take(BLOCKS * FEAT).rearrange("p (b f) -> p b f", f=FEAT)
        hg = r.take(BLOCKS * FEAT).rearrange("p (b f) -> p b f", f=FEAT)
        ah = r.take(BLOCKS * FEAT).rearrange("p (b f) -> p b f", f=FEAT)
        TMPF = r.at
        osb = [r.take(CHUNK)[0:3 * FEAT] for _ in range(2)]
        r = Region(sT[:, :])
        y3 = [r.take(BLOCKS * 3 * FEAT // 2).bitcast(BF16).rearrange("p (b k f) -> p b k f", k=3, f=FEAT) for _ in range(2)]
        yv = r.take(4 * FEAT).rearrange("p (b f) -> p b f", f=FEAT)
        yr = r.take(4 * FEAT).rearrange("p (b f) -> p b f", f=FEAT)
        sum3 = r.take(FEAT)

        TAILF = SCOLS + 9 * 1024
        T0 = CCOLS - 2 * TAILF
        T1 = CCOLS - 2 * 4 * 2 * BATCH
        r = Region(C[:, T0:T0 + 2 * TAILF].bitcast(F32))

        def batches(dt):
            return r.take(2 * BATCH).bitcast(dt).rearrange("p (c e) -> p c e", c=2)

        hT = r.take(SCOLS)[0:FEAT + 1, :]
        dN, sN, aN = (batches(I32) for _ in range(3))
        relF, keyF, floF, srcf, dclF = (batches(F32) for _ in range(5))
        fhi = srcf
        pqr = batches(F32)
        r = Region(sT[:, :])
        xc, sq, hn, x_sb = (r.take(BLOCKS * FEAT).rearrange("p (b f) -> p b f", f=FEAT) for _ in range(4))
        r = Region(work[:, :])
        pq = r.take(BLOCKS * PARTS * HID).bitcast(BF16).rearrange("p (h b k f) -> p h b k f", h=2, k=PARTS, f=HID)
        idxt = r.take(BATCHES * TILES).bitcast(I32).rearrange("p (g j) -> p g j", j=TILES)
        wpq = r.take(2 * HID)[0:FEAT + 1]
        w1b = r.take(HID)[0:FEAT]
        b3f = r.take(TILES * HID).rearrange("p (j n) -> p j n", j=TILES)[0:96]
        ident = r.take(P)
        relN = r.take(BATCH).bitcast(I16).rearrange("p (c e) -> p c e", c=2)
        dcolt = r.take(BATCHES * TILES).bitcast(I32).rearrange("p (g j) -> p g j", j=TILES)
        pmn = r.take(4)
        pmx = r.take(4)
        bmn = r.take(2)
        bmx = r.take(2)
        pfl = r.take(4)
        tabN = r.take(2 * TABC).bitcast(I32).rearrange("p (c k) -> p c k", c=2)

        psum = ctx.enter_context(nc.psum_tensor("psum", [P, 8, 512], F32))
        banks = [psum[:, n, :] for n in range(8)]
        H1, H2, H3, CP = banks[0:2], banks[2], banks[3], banks[6:8]
        SEG, DEG = psum[:, 4, 0:SPAN], psum[:, 5, 0:HI]
        key_f = key[:, :, :].rearrange("p g j -> p (g j)")
        deg, droot, dinv, c1, cf = (key_f[:, n * BLOCKS:(n + 1) * BLOCKS] for n in range(5))

        s_edges, s_x, s_w, s_pads, s_const = (sem(n) for n in ("s_edges", "s_x", "s_w", "s_pads", "s_const"))
        s_dve = sem("s_dve")
        s_var, s_std = sem("s_var"), sem("s_std")
        s_h, s_wpq, s_h3one = sem("s_h"), sem("s_wpq"), sem("s_h3one")
        s_idxN, s_keyN = sem("s_idxN"), sem("s_keyN")
        s_fill, s_evac = sem("s_fill"), sem("s_evac")
        s_tables, s_rel, s_tabw, s_tab, s_clear = (sem(n) for n in ("s_tables", "s_rel", "s_tabw", "s_tab", "s_clear"))
        idx_loaded = [sem(f"idx_loaded{i}") for i in range(SLOTS)]
        landed = [sem(f"landed{i}") for i in range(SLOTS)]
        rel_loaded = [sem(f"rel_loaded{i}") for i in range(2)]
        pw_loaded = [sem(f"pw_loaded{i}") for i in range(2)]
        cst_made, s_pqr, s_pq2 = [sem(f"cst_made{u}") for u in range(2)], sem("s_pqr"), sem("s_pq2")
        s_clear0, s_dcol = sem("s_clear0"), sem("s_dcol")
        s_pq1 = sem("s_pq1")
        s_b3, s_b3p = sem("s_b3"), sem("s_b3p")
        ohT_made, ohS_made = sem("ohT_made"), sem("ohS_made")
        ohC_made = [sem(f"ohC_made{u}") for u in range(2)]
        cp_done = [sem(f"cp_done{u}") for u in range(2)]
        cp_added = [sem(f"cp_added{u}") for u in range(2)]
        h1_done, h1_out = sem("h1_done"), sem("h1_out")
        h2_done, h2_out, h3_done, h3_out = sem("h2_done"), sem("h2_out"), sem("h3_done"), sem("h3_out")
        seg_done, seg_added = sem("seg_done"), sem("seg_added")
        s_gen, flag_set, turns, edges_done = sem("s_gen"), sem("flag_set"), sem("turns"), sem("edges_done")
        scanned, s_max, s_max2, flag2_set, turns2 = sem("scanned"), sem("s_max"), sem("s_max2"), sem("flag2_set"), sem("turns2")
        s_x1pad, s_x1, s_res, s_out, s_out2 = sem("s_x1pad"), sem("s_x1"), sem("s_res"), sem("s_out"), sem("s_out2")
        staged, turned, turn_a, turn_d = sem("staged"), sem("turned"), sem("turn_a"), sem("turn_d")
        m_done, m_read, ones_set = sem("m_done"), sem("m_read"), sem("ones_set")
        v2, sd2, dmx, sdd = sem("v2"), sem("sd2"), sem("dmx"), sem("sdd")
        y_set, o_done, o_out, r_done, y_made = sem("y_set"), sem("o_done"), sem("o_out"), sem("r_done"), sem("y_made")
        y_step, gathers_begun = sem("y_step"), sem("gathers_begun")
        y2_step, landed_gen = sem("y2_step"), sem("landed_gen")
        landed_y = [sem(f"landed_y{k}") for k in range(3)]

        NP, NW, NC = (-(-NODES // n) for n in (PWIN, SPAN, PSPAN))
        LOADS = 3 * 16
        PSTEP, SSTEP, CSTEP = 16 + 3, 4, 4
        P_AT = LOADS + 2
        MLP_AT = P_AT + NP * PSTEP
        S_AT = MLP_AT + 6
        K_AT = S_AT + NW * SSTEP
        C_AT = K_AT + 8
        TURNS = C_AT + NC * CSTEP
        GCOL = 13
        Y_LOADS = 2 * 16
        YT_AT = Y_LOADS + 4
        YTURNS = YT_AT + 2 * TILES
        PASS = 16 + 1 + BATCHES * YTURNS + 1

        def general(e, body_fast, body_general):
            e.wait_ge(flag_set, 1)
            wide_batches = e.value_load(flags[0:1, 0:1], min_val=0, max_val=1)
            with e.If(wide_batches < 1):
                body_fast()
            with e.Else():
                body_general()

        SPLIT = [(0, 5), (5, 10), (10, 18), (18, HI)]
        TD = 2 * 5
        psum_b = psum[:, :, :].bitcast(BF16)
        bankb = [b[:, :].bitcast(BF16) for b in banks]
        MB = 15

        def later(i, n):
            return not (isinstance(i, int) and i < n)

        def turned_cols(w, lo, n):
            return C[:, bass.ds(w * NODES + lo, n)]

        FILLS = [("hT", n) for n in range(7)] + [("src", c) for c in range(2)] + [("pq", n) for n in range(7)] + \
                [(a, c) for a in ("rel", "lo", "hi", "key", "dcol") for c in range(2)]
        PQ_DONE = FILLS.index(("pq", 6)) + 1
        SRC_DONE = FILLS.index(("src", 1)) + 1
        PRE = len(FILLS)
        NAT = {"src": srcf, "lo": floF, "hi": fhi, "key": keyF, "rel": relF, "dcol": dclF}

        def groups(n):
            return range(4 * n, min(4 * n + 4, BLOCKS))

        def part(n, k):
            return pq[:, :, 4 * n:4 * n + len(groups(n)), k, :]

        def by_half(buf, k):
            return buf.rearrange("p (b h f) -> p h b f", h=2, f=HID)[:, :, 0:k, :]

        block = ctx.enter_context(nc.Block())

        @block.sync
        def _(sp):
            xv = x[0:(BLOCKS - 1) * P, :].rearrange("(b p) f -> p b f", p=P)
            sp.dma_start(x_sb[:, 0:BLOCKS - 1, :], xv).then_inc(s_x, 16)
            sp.wait_ge(s_pads, 3)
            sp.dma_start(x_sb[0:LASTN, BLOCKS - 1, :], x[(BLOCKS - 1) * P:NODES, :]).then_inc(s_x, 16)
            full = (BATCHES - 1 - P)
            for nat, e in ((dN, dst), (sN, src)):
                sp.dma_start(nat[:, 0, :], e[0:P * BATCH].rearrange("(p e) -> p e", e=BATCH)).then_inc(s_edges, 16)
                sp.dma_start(nat[0:full, 1, :], e[P * BATCH:(P + full) * BATCH].rearrange("(p e) -> p e", e=BATCH)).then_inc(s_edges, 16)
                sp.dma_start(nat[full:full + 1, 1, 0:TAIL], e[EDGES - TAIL:EDGES].rearrange("(p e) -> p e", p=1)).then_inc(s_edges, 16)
            sp.wait_ge(s_edges, 96)
            sp.dma_start(dst_d[0:P, :], dN[:, 0, :]).then_inc(s_gen, 16)
            sp.dma_start(dst_d[P:BATCHES, :], dN[0:GB, 1, :]).then_inc(s_gen, 16)
            sp.wait_ge(s_keyN, 1)
            sp.dma_start(rel_d[0:P, :], relN[:, 0, :]).then_inc(s_rel, 16)
            sp.dma_start(rel_d[P:BATCHES, :], relN[0:GB, 1, :]).then_inc(s_rel, 16)
            sp.dma_start(tab_d[0:P, :], tabN[:, 0, :]).then_inc(s_tabw, 16)
            sp.dma_start(tab_d[P:BATCHES, :], tabN[0:GB, 1, :]).then_inc(s_tabw, 16)
            sp.wait_ge(s_evac, SRC_DONE)
            sp.dma_start(idx_d, idxt[:, :, :].rearrange("p g j -> p (g j)")).then_inc(s_tables, 16)
            sp.wait_ge(s_tabw, 32)
            sp.dma_start(tab[:, :], tab_d.rearrange("g c -> (g c)").rearrange("(o n) -> o n", o=1)).then_inc(s_tab, 16)
            sp.wait_ge(s_pq1, 7)
            sp.wait_ge(s_pq2, 7)
            for h, table in ((1, q_tab), (0, p_tab)):
                sp.dma_start(table.rearrange("(b p) c -> p b c", p=P), pq[:, h, :, :, :].rearrange("p b k f -> p b (k f)")).then_inc(s_tables, 16)
            sp.wait_ge(s_evac, PRE)
            sp.dma_start(dcol_d, dcolt[:, :, :].rearrange("p g j -> p (g j)")).then_inc(s_dcol, 16)
            sp.wait_ge(s_tab, 16)
            sp.wait_ge(s_rel, 32)
            sp.wait_ge(s_tables, 16 * 3)

            def load(i, s, q, gathered):
                if gathered is not None:
                    sp.wait_ge(landed[q], gathered)
                sp.dma_start(idx[:, q, :], idx_d[:, bass.ds(TILES * i, TILES)]).then_inc(idx_loaded[q], 16)
                base = [sp.value_load(tab[0:1, bass.ds(TABC * i + 4 + u, 1)], min_val=0, max_val=NODES - 1) for u in range(2)]
                if later(i, 2):
                    sp.wait_ge(ohT_made, i - 1)
                sp.dma_start(relb[:, s, :], rel_d[bass.ds(i, 1), :].rearrange("o e -> (o e)").partition_broadcast(PROWS)).then_inc(rel_loaded[s], 16)
                if later(i, 2):
                    sp.wait_ge(h1_done, i - 1)
                for u in range(2):
                    sp.dma_start(pw[:, s, u, :], p_tab[bass.ds(base[u], PWIN), :].rearrange("r (k f) -> k r f", k=PARTS)).then_inc(pw_loaded[s], 16)

            def edges():
                for i in range(SLOTS):
                    load(i, i % 2, i, None)
                with sp.Fori(1, BATCHES // SLOTS) as m:
                    for q in range(SLOTS):
                        load(SLOTS * m + q, q % 2, q, 64 * m)

            def edges_general():
                sp.wait_ge(s_gen, 32)
                sp.wait_ge(s_dcol, 16)
                with sp.Fori(0, BATCHES) as i:
                    at = i * TURNS + 1
                    sp.wait_ge(turns, at)
                    sp.dma_start(idx[:, 0, :], idx_d[:, bass.ds(TILES * i, TILES)]).then_inc(turns, 16)
                    sp.wait_ge(turns, at + 16)
                    sp.dma_start(gidx[:, 1, :], dcol_d[:, bass.ds(TILES * i, TILES)]).then_inc(turns, 16)
                    sp.wait_ge(turns, at + 32)
                    sp.dma_start(grow, dst_d[bass.ds(i, 1), :].rearrange("o e -> (o e)").partition_broadcast(PROWS)).then_inc(turns, 16)
                    with sp.Fori(0, NP) as w:
                        sp.wait_ge(turns, at + P_AT + w * PSTEP)
                        sp.dma_start(pw[:, 0, 0, :], p_tab[bass.ds(w * PWIN, PWIN), :].rearrange("r (k f) -> k r f", k=PARTS)).then_inc(turns, 16)

            general(sp, edges, edges_general)
            sp.wait_ge(s_x1pad, 1)
            sp.dma_start(x1[:, 0:BLOCKS - 1, :], xv).then_inc(s_x1, 16)
            sp.dma_start(x1[0:LASTN, BLOCKS - 1, :], x[(BLOCKS - 1) * P:NODES, :]).then_inc(s_x1, 16)
            sp.wait_ge(s_max, 1)
            sp.dma_start(max_d.rearrange("(n o) -> n o", o=1), roff[:, 0:1]).then_inc(s_max2, 16)
            sp.wait_ge(s_max2, 16)
            sp.dma_start(mrow[:, 1:P + 1], max_d.rearrange("(o n) -> o n", o=1)).then_inc(s_max2, 16)
            for n in range(CHUNKS):
                sp.wait_ge(s_res, n + 1)
                lo, hi = 4 * n, min(4 * n + 4, BLOCKS)
                if hi < BLOCKS:
                    sp.dma_start(out[lo * P:hi * P, :].rearrange("(b p) f -> p b f", p=P), ycur[:, lo:hi, :]).then_inc(s_out, 16)
                else:
                    sp.dma_start(out[lo * P:NODES, :], ycur[0:LASTN, lo, :]).then_inc(s_out, 16)
            sp.wait_ge(s_out, 16 * CHUNKS)
            sp.wait_ge(flag2_set, 1)
            large = sp.value_load(flags[0:1, 1:2], min_val=0, max_val=1)
            with sp.If(large > 0):
                with sp.Fori(0, ITERS + 1) as t:
                    sp.wait_ge(turns2, t * PASS + 1)
                    sp.dma_start(y_tab.rearrange("(b p) f -> p b f", p=P), ycur).then_inc(turns2, 16)
                    with sp.Fori(0, BATCHES) as i:
                        at = t * PASS + 17 + i * YTURNS + 1
                        sp.wait_ge(turns2, at)
                        sp.dma_start(gidx[:, 0, :], idx_d[:, bass.ds(TILES * i, TILES)]).then_inc(turns2, 16)
                        sp.wait_ge(turns2, at + 16)
                        sp.dma_start(gidx[:, 1, :], dcol_d[:, bass.ds(TILES * i, TILES)]).then_inc(turns2, 16)
                sp.wait_ge(turns2, (ITERS + 1) * PASS + 1)
                sp.dma_start(out[0:(BLOCKS - 1) * P, :].rearrange("(b p) f -> p b f", p=P), ycur[:, 0:BLOCKS - 1, :]).then_inc(s_out2, 16)
                sp.dma_start(out[(BLOCKS - 1) * P:NODES, :], ycur[0:LASTN, BLOCKS - 1, :]).then_inc(s_out2, 16)
                sp.wait_ge(s_out2, 32)

        @block.gpsimd
        def _(g):
            G.iota(iota_c[:, :], [[1, PCOLS]], base=0, channel_multiplier=0, allow_small_or_imprecise_dtypes=True).then_inc(s_const, 1)
            G.iota(iota_l[:, :], [[1, P]], base=0, channel_multiplier=0, allow_small_or_imprecise_dtypes=True).then_inc(s_const, 1)
            G.iota(iota_s[:, :], [[1, SPAN]], base=0, channel_multiplier=0, allow_small_or_imprecise_dtypes=True).then_inc(s_const, 1)
            G.iota(pcol[:, :], [[1, 1]], base=0, channel_multiplier=1, allow_small_or_imprecise_dtypes=True).then_inc(s_const, 1)
            for k in range(PARTS):
                g.wait_ge(s_const, 4 + k)
                G.iota(pmod[k * PWIN:(k + 1) * PWIN, :], [[1, 1]], base=0, channel_multiplier=1, allow_small_or_imprecise_dtypes=True).then_inc(s_const, 1)
            g.wait_ge(s_const, 7)
            G.memset(ident[:, :], 0.0).then_inc(s_const, 1)
            G.memset(identb[:, :], 0.0).then_inc(s_const, 1)
            g.wait_ge(s_const, 9)
            for m in (ident, identb):
                G.affine_select(out=m[:, :], in_=m[:, :], compare_op=ALU.not_equal, fill=1.0, base=0,
                                pattern=[[-1, P]], channel_multiplier=1).then_inc(s_const, 1)
            G.memset(C[:, 0:T0].bitcast(F32), 0.0).then_inc(s_clear0, 1)
            g.wait_ge(s_evac, 7)
            G.memset(sT[0:HID + 1, :], 0.0).then_inc(s_clear, 1)
            g.wait_ge(s_evac, PQ_DONE)
            G.memset(C[:, T0:T0 + 2 * SCOLS].bitcast(F32), 0.0).then_inc(s_clear, 1)
            g.wait_ge(s_tables, 16 * 3)

            def gather(i, q, loads):
                g.wait_ge(idx_loaded[q], loads)
                if later(i, SLOTS):
                    g.wait_ge(h1_done, i - SLOTS + 1)
                g.sem_inc(gathers_begun, 1)
                for j in range(TILES):
                    G.indirect_dma_start(out=gat[:, q, j, :, :].rearrange("p k f -> p (k f)"), out_offset=None, in_=q_tab,
                                         in_offset=bass.IndirectOffsetOnAxis(ap=idx[:, q, j:j + 1], axis=0)).then_inc(landed[q], 16)

            def edges():
                for i in range(SLOTS):
                    gather(i, i, 16)
                with g.Fori(1, BATCHES // SLOTS) as m:
                    for q in range(SLOTS):
                        gather(SLOTS * m + q, q, 16 * m + 16)

            def edges_general():
                with g.Fori(0, BATCHES) as i:
                    g.wait_ge(turns, i * TURNS + 1 + 48)
                    g.sem_inc(gathers_begun, 1)
                    for j in range(TILES):
                        G.indirect_dma_start(out=gat[:, 0, j, :, :].rearrange("p k f -> p (k f)"), out_offset=None, in_=q_tab,
                                             in_offset=bass.IndirectOffsetOnAxis(ap=idx[:, 0, j:j + 1], axis=0)).then_inc(landed_gen, 16)

            general(g, edges, edges_general)
            g.wait_ge(flag2_set, 1)
            large = g.value_load(flags[0:1, 1:2], min_val=0, max_val=1)
            with g.If(large > 0):
                def gather_y(t, k):
                    with g.Fori(0, BATCHES) as i:
                        g.wait_ge(turns2, t * PASS + 17 + i * YTURNS + 1 + 32)
                        g.sem_inc(gathers_begun, 1)
                        for j in range(TILES):
                            G.indirect_dma_start(out=ygat[:, j * FEAT:(j + 1) * FEAT], out_offset=None, in_=y_tab,
                                                 in_offset=bass.IndirectOffsetOnAxis(ap=gidx[:, 1, j:j + 1], axis=0)).then_inc(landed_y[k], 16)

                gather_y(0, 0)
                with g.Fori(0, (ITERS - 1) // 3) as m:
                    for k in range(3):
                        gather_y(3 * m + k + 1, (k + 1) % 3)
                gather_y(ITERS, ITERS % 3)

        @block.scalar
        def _(act):
            for dst_ap, src_ap in ((wpq[FEAT:FEAT + 1, 0:HID], b1.rearrange("(o n) -> o n", o=1)),
                                   (wpq[0:FEAT, 0:HID], W1[0:FEAT, :]), (wpq[0:FEAT, HID:2 * HID], W1[FEAT:2 * FEAT, :]),
                                   (w1b[:, :], W1[FEAT:2 * FEAT, :]),
                                   (w2s[:, :], W2), (w3s[:, :], W3),
                                   (w4s[0:HID, 0:FEAT], W4), (w4s[HID:HID + 1, 0:FEAT], b4.rearrange("(o n) -> o n", o=1)),
                                   (b2c[:, :], b2.rearrange("(n o) -> n o", o=1))):
                act.dma_start(dst_ap, src_ap).then_inc(s_w, 16)
            act.wait_ge(s_b3, 1)
            for k in range(PARTS):
                act.dma_start(b3f[32 * k:32 * k + 1, :, :], b3.rearrange("(o n) -> o n", o=1).unsqueeze(1).to_broadcast([1, TILES, HID])).then_inc(s_w, 16)
            act.wait_ge(s_var, 1)
            A.activation(stats[:, 2, :], stats[:, 1, :], ACT.Sqrt).then_inc(s_std, 1)

            def second_part(n):
                k = len(groups(n))
                act.wait_ge(s_pqr, n + 1)
                A.activation(part(n, 1), by_half(pqr[:, n % 2, :], k), ACT.Copy).then_inc(s_pq1, 1)

            for f, (what, n) in enumerate(FILLS):
                act.wait_ge(s_fill, f + 1)
                bank = banks[f % 8]
                if what == "hT":
                    w = len(groups(n)) * P
                    A.activation(hT[0:FEAT, n * 512:n * 512 + w], bank[0:FEAT, 0:w], ACT.Copy).then_inc(s_evac, 1)
                elif what == "pq":
                    k = len(groups(n))
                    A.activation(part(n, 0), by_half(bank, k), ACT.Copy).then_inc(s_evac, 1)
                    if n:
                        second_part(n - 1)
                    if n == 6:
                        second_part(n)
                else:
                    dest = {"src": idxt, "lo": locol, "hi": hicol, "key": key, "rel": relcol, "dcol": dcolt}[what]
                    gc = P if n == 0 else GB
                    A.activation(dest[:, n * P:n * P + gc, :].rearrange("p g j -> p j g"),
                                 bank[:, :].rearrange("p (j g) -> p j g", j=TILES)[:, :, 0:gc], ACT.Copy).then_inc(s_evac, 1)

            def stage1(i, s):
                act.wait_ge(h1_done, i + 1)
                if later(i, 1):
                    act.wait_ge(h2_done, i)
                A.activation(h1s, H1[s][0:HID, :], ACT.Relu).then_inc(h1_out, 1)

            def stage2(i):
                act.wait_ge(h2_done, i + 1)
                if later(i, 1):
                    act.wait_ge(h3_done, i)
                A.activation(h2s, H2, ACT.Relu, bias=b2c[:, 0:1]).then_inc(h2_out, 1)

            def stage3(i):
                act.wait_ge(h3_done, i + 1)
                if later(i, 1):
                    act.wait_ge(seg_done, i)
                A.activation(h3s[:, :, 0:HID], H3[:, 0:TILES * HID].rearrange("p (j f) -> p j f", f=HID), ACT.Relu).then_inc(h3_out, 1)

            def counts_out(i, u):
                act.wait_ge(cp_done[u], i + 1)
                if later(i, 1):
                    act.wait_ge(cp_added[u], i)
                A.activation(cst[:, u, :], CP[u][:, 0:PCOLS], ACT.Copy).then_inc(cst_made[u], 1)

            def step(i, s):
                stage1(i, s)
                if later(i, 1):
                    stage3(i - 1)
                counts_out(i, 0)
                stage2(i)
                counts_out(i, 1)

            def edges():
                step(0, 0)
                step(1, 1)
                with act.Fori(1, BATCHES // 2) as m:
                    step(2 * m, 0)
                    step(2 * m + 1, 1)
                stage3(BATCHES - 1)

            def edges_general():
                with act.Fori(0, BATCHES) as i:
                    at = i * TURNS + 1 + MLP_AT
                    act.wait_ge(turns, at)
                    A.activation(h1s, H1[0][0:HID, :], ACT.Relu).then_inc(turns, 1)
                    act.wait_ge(turns, at + 2)
                    A.activation(h2s, H2, ACT.Relu, bias=b2c[:, 0:1]).then_inc(turns, 1)
                    act.wait_ge(turns, at + 4)
                    A.activation(h3s[:, :, 0:HID], H3[:, 0:TILES * HID].rearrange("p (j f) -> p j f", f=HID), ACT.Relu).then_inc(turns, 1)

            act.wait_ge(s_clear0, 1)
            act.wait_ge(s_b3p, 1)
            act.wait_ge(s_gen, 32)
            A.activation(C[:, T1:CCOLS].bitcast(F32), C[:, 0:CCOLS - T1].bitcast(F32), ACT.Copy).then_inc(s_clear, 1)
            general(act, edges, edges_general)
            act.wait_ge(edges_done, 1)
            def turn_out(w, s, k):
                act.wait_ge(turned, w + 1)
                for f in (2, 3):
                    lo, hi = SPLIT[f][0] * P, min(SPLIT[f][1] * P, NODES)
                    ins = A.activation(turned_cols(w, lo, hi - lo)[0:k, :], bankb[4 * s + f][0:k, 0:hi - lo], ACT.Copy)
                ins.then_inc(turn_a, 1)

            act.wait_ge(dmx, 1)
            A.activation(droot, deg, ACT.Sqrt).then_inc(sdd, 1)
            act.wait_ge(v2, 1)
            A.activation(stats[:, 2, :], stats[:, 1, :], ACT.Sqrt).then_inc(sd2, 1)
            with act.Fori(0, BLOCKS // 2) as m:
                for s in range(2):
                    turn_out(2 * m + s, s, P)
            turn_out(BLOCKS - 1, 0, LASTN)
            def chunk_out(t, n, par):
                q = CHUNKS * t + n
                w = min(CHUNK, NODES - n * CHUNK)
                act.wait_ge(o_done, q + 1)
                if not isinstance(t, int) or q >= 2:
                    act.wait_ge(r_done, q - 1)
                A.activation(osb[par][:, 0:w], banks[par][0:3 * FEAT, 0:w], ACT.Copy).then_inc(o_out, 1)

            act.wait_ge(turn_d, BLOCKS)
            for n in range(CHUNKS):
                chunk_out(0, n, n % 2)
            with act.Fori(0, (ITERS - 2) // 2) as m:
                for u in range(2):
                    for n in range(CHUNKS):
                        chunk_out(2 * m + 1 + u, n, (1 + u + n) % 2)
            for n in range(CHUNKS):
                chunk_out(ITERS - 1, n, (ITERS - 1 + n) % 2)
            act.wait_ge(flag2_set, 1)
            large = act.value_load(flags[0:1, 1:2], min_val=0, max_val=1)
            with act.If(large > 0):
                act.wait_ge(dmx, 2)
                A.activation(droot, deg, ACT.Sqrt).then_inc(sdd, 1)

        @block.vector
        def _(dve):
            chain = [0]

            def link(ins):
                chain[0] += 1
                ins.then_inc(s_dve, 1)
                dve.wait_ge(s_dve, chain[0])

            def wide(ap):
                return ap.unsqueeze(2).to_broadcast([P, ap.shape[1], FEAT])

            def center(xin, xc, sq):
                link(V.tensor_reduce(stats[:, 0, :], xin, AX.X, ALU.add))
                link(V.tensor_scalar(stats[:, 1, :], stats[:, 0, :], 1.0 / FEAT, None, ALU.mult))
                link(V.tensor_tensor(xc, xin, wide(stats[:, 1, :]), ALU.subtract))
                link(V.tensor_tensor(sq, xc, xc, ALU.mult))
                link(V.tensor_reduce(stats[:, 0, :], sq, AX.X, ALU.add))

            V.memset(x_sb[:, BLOCKS - 1, :], 0.0).then_inc(s_pads, 1)
            V.memset(dN[:, 1, :], PAD_DST).then_inc(s_pads, 1)
            V.memset(sN[:, 1, :], SCOLS - 1).then_inc(s_pads, 1)
            V.memset(ones1[:, :], 1.0).then_inc(s_h3one, 1)
            V.memset(hT[FEAT:FEAT + 1, :], 1.0).then_inc(s_h3one, 1)
            V.memset(wpq[FEAT:FEAT + 1, HID:2 * HID], 0.0).then_inc(s_h3one, 1)
            V.memset(w4s[:, FEAT:FEAT + 1], 0.0).then_inc(s_h3one, 1)
            V.memset(b3f, 0.0).then_inc(s_b3, 1)
            V.memset(ones3[:, :], 1.0).then_inc(s_h3one, 1)
            dve.wait_ge(s_h3one, 5)
            V.memset(w4s[HID:HID + 1, FEAT:FEAT + 1], 1.0).then_inc(s_h3one, 1)
            dve.wait_ge(s_x, 32)
            center(x_sb, xc, sq)
            V.tensor_scalar(stats[:, 1, :], stats[:, 0, :], 1.0 / FEAT, EPS, ALU.mult, ALU.add).then_inc(s_var, 1)
            dve.wait_ge(s_w, 16 * 12)
            V.tensor_tensor(wpq[0:FEAT, 0:HID], wpq[0:FEAT, 0:HID], w1b[:, :], ALU.subtract).then_inc(s_wpq, 1)
            dve.wait_ge(s_std, 1)
            link(V.reciprocal(stats[:, 3, :], stats[:, 2, :]))
            link(V.tensor_tensor(hn, xc, stats[:, 3, :].unsqueeze(2).to_broadcast([P, BLOCKS, FEAT]), ALU.mult))
            V.tensor_scalar(hn, hn, 0.0, None, ALU.max).then_inc(s_h, 1)
            dve.wait_ge(s_edges, 96)
            V.tensor_copy(srcf[:, :, :], sN).then_inc(s_idxN, 1)
            d4 = dN.rearrange("p c (u e) -> p (c u) e", u=2)
            link(V.tensor_reduce(pmn[:, :], d4, AX.X, ALU.min))
            link(V.tensor_reduce(pmx[:, :], d4, AX.X, ALU.max))
            link(V.tensor_scalar(pmn[:, :], pmn[:, :], float(NODES - 1), None, ALU.min))
            link(V.tensor_scalar(pmx[:, :], pmx[:, :], float(NODES - 1), None, ALU.min))
            pn = pmn[:, :].rearrange("p (c u) -> p c u", u=2)
            px = pmx[:, :].rearrange("p (c u) -> p c u", u=2)
            link(V.tensor_tensor(bmn[:, :], pn[:, :, 0], pn[:, :, 1], ALU.min))
            link(V.tensor_tensor(bmx[:, :], px[:, :, 0], px[:, :, 1], ALU.max))
            for c in range(2):
                for u in range(2):
                    q = slice(u * 256, u * 256 + 256)
                    link(V.tensor_scalar(relN[:, c, q], dN[:, c, q], pmn[:, 2 * c + u:2 * c + u + 1], None, ALU.subtract))
            link(V.tensor_tensor(pmx[:, :], pmx[:, :], pmn[:, :], ALU.subtract))
            link(V.tensor_tensor(bmx[:, :], bmx[:, :], bmn[:, :], ALU.subtract))
            link(V.tensor_scalar(pfl[:, :], pmx[:, :], float(PSPAN), None, ALU.is_ge))
            link(V.tensor_scalar(bmx[:, :], bmx[:, :], float(SPAN), None, ALU.is_ge))
            fl = pfl[:, :].rearrange("p (c u) -> p c u", u=2)
            link(V.memset(tabN[:, :, :], 0))
            link(V.tensor_tensor(bmx[:, :], bmx[:, :], fl[:, :, 0], ALU.max))
            link(V.tensor_tensor(tabN[:, :, 3], bmx[:, :], fl[:, :, 1], ALU.max))
            link(V.tensor_copy(tabN[:, :, 0], bmn[:, :]))
            link(V.tensor_copy(tabN[:, :, 4:6], pn))
            V.tensor_scalar(tabN[:, :, 1:3], pn, float(HI), None, ALU.mult).then_inc(s_keyN, 1)
            def third_part(n):
                k = len(groups(n))
                dve.wait_ge(s_pq1, n + 1)
                V.tensor_tensor(part(n, 2), by_half(pqr[:, n % 2, :], k), part(n, 1), ALU.subtract).then_inc(s_pq2, 1)

            for n in range(7):
                k = len(groups(n))
                f = FILLS.index(("pq", n))
                dve.wait_ge(s_evac, f + 1)
                if n >= 2:
                    dve.wait_ge(s_pq2, n - 1)
                V.tensor_tensor(by_half(pqr[:, n % 2, :], k), by_half(banks[f % 8], k), part(n, 0), ALU.subtract).then_inc(s_pqr, 1)
                if n:
                    third_part(n - 1)
            third_part(6)
            dve.wait_ge(s_tab, 16)
            V.tensor_reduce(flags[:, 0:1], tab[:, :].rearrange("o (g c) -> o g c", c=TABC)[:, :, 3], AX.X, ALU.max).then_inc(flag_set, 1)
            for c in range(2):
                link(V.tensor_scalar(relF[:, c, :], dN[:, c, :], bmn[:, c:c + 1], None, ALU.subtract))
            V.memset(stats[:, 0, 0:1], 0.0).then_inc(s_idxN, 1)
            link(V.tensor_scalar(aN, sN, P - 1, None, ALU.bitwise_and))
            V.tensor_copy(floF, aN).then_inc(s_idxN, 1)
            dve.wait_ge(s_idxN, 3)
            link(V.tensor_scalar(aN, sN, 7, None, ALU.arith_shift_right))
            link(V.tensor_copy(fhi, aN))
            link(V.tensor_scalar(keyF, relN, float(HI), None, ALU.mult))
            V.tensor_tensor(keyF, keyF, fhi, ALU.add).then_inc(s_idxN, 1)
            V.tensor_scalar(dclF, dN, float(SCOLS - 1), None, ALU.min).then_inc(s_idxN, 1)
            rest = pqr[0:96, 0, 0:TILES * HID].rearrange("p (j n) -> p j n", j=TILES)
            link(V.tensor_copy(b3p[:, :, :], b3f))
            link(V.tensor_tensor(rest, b3f, b3p[:, :, :], ALU.subtract))
            for k in (1, 2):
                link(V.tensor_copy(b3p[32 * k:32 * k + 32, :, :], rest[32 * k:32 * k + 32]))
            link(V.tensor_tensor(rest[64:96], rest[64:96], b3p[64:96, :, :], ALU.subtract))
            V.tensor_copy(b3p[64:96, :, :], rest[64:96]).then_inc(s_b3p, 1)
            dve.wait_ge(s_evac, PRE)
            dve.wait_ge(s_gen, 32)
            V.memset(C[:, T0 + 2 * SCOLS:T1].bitcast(F32), 0.0).then_inc(s_clear, 1)
            dve.wait_ge(s_tables, 16 * 3)
            dve.wait_ge(s_rel, 32)
            dve.wait_ge(s_dcol, 16)
            V.memset(h3s[:, :, HID:HID + 1], 1.0).then_inc(s_h3one, 1)

            def onehots_p(i, s, loads):
                dve.wait_ge(rel_loaded[s], loads)
                if later(i, 2):
                    dve.wait_ge(h1_done, i - 1)
                V.tensor_scalar(ohT[:, s, :], relb[:, s, :], pmod[0:PROWS, 0:1], None, ALU.is_equal).then_inc(ohT_made, 1)

            def onehots_s(i, s):
                if later(i, 2):
                    dve.wait_ge(seg_done, i - 1)
                V.tensor_tensor(ohS[:, s, :, :], iota_s[:, :].unsqueeze(1).to_broadcast([P, TILES, SPAN]),
                                relcol[:, bass.ds(i, 1), :].rearrange("p o j -> p (o j)").unsqueeze(2).to_broadcast([P, TILES, SPAN]),
                                ALU.is_equal).then_inc(ohS_made, 1)

            def onehots_lo(i, s):
                if later(i, 2):
                    dve.wait_ge(cp_done[1], i - 1)
                V.tensor_tensor(ohL[:, s, :, :], iota_l[:, :].unsqueeze(1).to_broadcast([P, TILES, P]),
                                locol[:, bass.ds(i, 1), :].rearrange("p o j -> p (o j)").unsqueeze(2).to_broadcast([P, TILES, P]),
                                ALU.is_equal)
                V.tensor_tensor(ohH[:, s, :, :], iota_l[:, 0:HI].unsqueeze(1).to_broadcast([P, TILES, HI]),
                                hicol[:, bass.ds(i, 1), :].rearrange("p o j -> p (o j)").unsqueeze(2).to_broadcast([P, TILES, HI]),
                                ALU.is_equal)

            def onehots_c(i, s):
                kcol = key[:, bass.ds(i, 1), :].rearrange("p o j -> p (o j)")
                for j in range(TILES):
                    ins = V.tensor_scalar(ohC[:, s, j, :], iota_c[:, :], kcol[:, j:j + 1], None, ALU.is_equal)
                    if j % 2:
                        ins.then_inc(ohC_made[j // 2], 1)

            def value(i, col, top):
                return dve.value_load(tab[0:1, bass.ds(TABC * i + col, 1)], min_val=0, max_val=top)

            def add_count(i, u, base):
                dve.wait_ge(cst_made[u], i + 1)
                if later(i, 1) or u:
                    dve.wait_ge(cp_added[1 - u], i + u)
                w = C[:, bass.ds(base, PCOLS)]
                V.tensor_tensor(w, cst[:, u, :], w, ALU.add).then_inc(cp_added[u], 1)

            def add_sums(i, base):
                dve.wait_ge(seg_done, i + 1)
                if later(i, 1):
                    dve.wait_ge(seg_added, i)
                w = sT[0:HID + 1, bass.ds(base, SPAN)]
                V.tensor_tensor(w, SEG[0:HID + 1, :], w, ALU.add).then_inc(seg_added, 1)

            def cleared():
                dve.wait_ge(s_clear, 4)
                dve.wait_ge(s_clear0, 1)

            def step(i, s, loads):
                ahead = loads is not None
                base = [value(i - 1, 1 + u, (NODES - 1) * HI) for u in range(2)] if later(i, 1) else None
                sums = value(i - 2, 0, NODES - 1) if later(i, 2) else None
                if ahead:
                    onehots_p(i + 1, 1 - s, loads)
                if sums is not None:
                    add_sums(i - 2, sums)
                if base:
                    add_count(i - 1, 0, base[0])
                if ahead:
                    onehots_lo(i + 1, 1 - s)
                if base:
                    add_count(i - 1, 1, base[1])
                if ahead:
                    onehots_c(i + 1, 1 - s)
                if ahead:
                    onehots_s(i + 1, 1 - s)

            def edges():
                onehots_p(0, 0, 16)
                onehots_lo(0, 0)
                onehots_c(0, 0)
                onehots_s(0, 0)
                cleared()
                for i in range(3):
                    step(i, i % 2, 16 * ((i + 1) // 2 + 1))
                with dve.Fori(1, BATCHES // 2 - 1) as m:
                    step(2 * m + 1, 1, 16 * m + 32)
                    step(2 * m + 2, 0, 16 * m + 32)
                step(BATCHES - 1, 1, None)
                base = [value(BATCHES - 1, 1 + u, (NODES - 1) * HI) for u in range(2)]
                for u in range(2):
                    add_count(BATCHES - 1, u, base[u])
                for b in (BATCHES - 2, BATCHES - 1):
                    add_sums(b, value(b, 0, NODES - 1))
                dve.wait_ge(cp_added[1], BATCHES)
                dve.wait_ge(seg_added, BATCHES)

            def edges_general():
                cleared()
                wcol = ohS[0:PROWS, 1, 0, 0:1]
                with dve.Fori(0, BATCHES) as i:
                    at = i * TURNS + 1
                    dve.wait_ge(turns, at + LOADS + 1)
                    V.tensor_copy(wcol, pmod[0:PROWS, 0:1]).then_inc(turns, 1)
                    with dve.Fori(0, NP) as w:
                        dve.wait_ge(turns, at + P_AT + w * PSTEP + 16)
                        V.tensor_scalar(ohT[:, 0, :], grow, wcol, None, ALU.is_equal).then_inc(turns, 1)
                        dve.wait_ge(turns, at + P_AT + w * PSTEP + 18)
                        V.tensor_scalar(wcol, wcol, float(PWIN), None, ALU.add).then_inc(turns, 1)
                    dve.wait_ge(turns, at + MLP_AT + 5)
                    V.memset(roff[:, :], 0.0).then_inc(turns, 1)
                    tcol = gidx[:, 1, :].unsqueeze(2).to_broadcast([P, TILES, SPAN])
                    with dve.Fori(0, NW) as w:
                        dve.wait_ge(turns, at + S_AT + w * SSTEP)
                        V.scalar_tensor_tensor(out=ohS[:, 0, :, :], in0=iota_s[:, :].unsqueeze(1).to_broadcast([P, TILES, SPAN]),
                                               scalar=roff[:, 0:1], in1=tcol, op0=ALU.add, op1=ALU.is_equal).then_inc(turns, 1)
                        dve.wait_ge(turns, at + S_AT + w * SSTEP + 2)
                        v = sT[0:HID + 1, bass.ds(w * SPAN, SPAN)]
                        V.tensor_tensor(v, SEG[0:HID + 1, :], v, ALU.add).then_inc(turns, 1)
                        dve.wait_ge(turns, at + S_AT + w * SSTEP + 3)
                        V.tensor_scalar(roff[:, :], roff[:, :], float(SPAN), None, ALU.add).then_inc(turns, 1)
                    dve.wait_ge(turns, at + K_AT)
                    V.tensor_scalar(gidx[:, 2, :], idx[:, 0, :], 7, None, ALU.arith_shift_right).then_inc(turns, 1)
                    dve.wait_ge(turns, at + K_AT + 1)
                    V.tensor_scalar(gidx[:, 3, :], idx[:, 0, :], P - 1, None, ALU.bitwise_and).then_inc(turns, 1)
                    dve.wait_ge(turns, at + K_AT + 2)
                    gkey = gidx[:, 4, :].bitcast(F32)
                    V.tensor_scalar(gkey, gidx[:, 1, :], float(HI), None, ALU.mult).then_inc(turns, 1)
                    dve.wait_ge(turns, at + K_AT + 3)
                    V.tensor_tensor(gkey, gkey, gidx[:, 2, :], ALU.add).then_inc(turns, 1)
                    dve.wait_ge(turns, at + K_AT + 4)
                    V.tensor_tensor(ohL[:, 0, :, :], iota_l[:, :].unsqueeze(1).to_broadcast([P, TILES, P]),
                                    gidx[:, 3, :].unsqueeze(2).to_broadcast([P, TILES, P]), ALU.is_equal).then_inc(turns, 1)
                    dve.wait_ge(turns, at + K_AT + 5)
                    V.tensor_tensor(ohH[:, 0, :, :], iota_l[:, 0:HI].unsqueeze(1).to_broadcast([P, TILES, HI]),
                                    gidx[:, 2, :].unsqueeze(2).to_broadcast([P, TILES, HI]), ALU.is_equal).then_inc(turns, 1)
                    dve.wait_ge(turns, at + K_AT + 7)
                    V.memset(roff[:, :], 0.0).then_inc(turns, 1)
                    with dve.Fori(0, NC) as w:
                        dve.wait_ge(turns, at + C_AT + w * CSTEP)
                        for j in range(TILES):
                            last = V.tensor_scalar(ohC[:, 0, j, :], iota_c[:, :], roff[:, 0:1], gkey[:, j:j + 1], ALU.add, ALU.is_equal)
                        last.then_inc(turns, 1)
                        dve.wait_ge(turns, at + C_AT + w * CSTEP + 2)
                        v = C[:, bass.ds(w * PCOLS, PCOLS)]
                        V.tensor_tensor(v, CP[0][:, 0:PCOLS], v, ALU.add).then_inc(turns, 1)
                        dve.wait_ge(turns, at + C_AT + w * CSTEP + 3)
                        V.tensor_scalar(roff[:, :], roff[:, :], float(PCOLS), None, ALU.add).then_inc(turns, 1)
                dve.wait_ge(turns, BATCHES * TURNS + 1)

            dve.sem_inc(turns, 1)
            general(dve, edges, edges_general)
            dve.sem_inc(edges_done, 1)
            V.memset(x1[:, BLOCKS - 1, :], 0.0).then_inc(s_x1pad, 1)

            def copy_block(w, s, k):
                if later(w, 2):
                    dve.wait_ge(turned, w - 1)
                V.tensor_copy(stage[s][:, 0:k * HI], C[:, bass.ds(w * (P * HI), k * HI)]).then_inc(staged, 1)

            def turn_out(w, s, k):
                dve.wait_ge(turned, w + 1)
                V.tensor_copy(turned_cols(w, 0, TD * P)[0:k, :].rearrange("p (f n) -> p f n", f=2),
                              psum_b[0:k, 4 * s:4 * s + 2, 0:TD * P // 2]).then_inc(turn_d, 1)

            V.tensor_scalar(deg, DEG, 1.0, None, ALU.max).then_inc(dmx, 1)
            copy_block(0, 0, P)
            copy_block(1, 1, P)
            dve.wait_ge(m_done, 1)
            dve.wait_ge(s_x1, 32)
            msum = [(banks[6], 0, MB), (banks[7], MB, BLOCKS)]
            tmpf = work[:, TMPF:TMPF + BLOCKS * FEAT].rearrange("p (b f) -> p b f", f=FEAT)
            tmpg = y3[1].rearrange("p b k f -> p (b k f)").bitcast(F32)[:, 0:BLOCKS * FEAT].rearrange("p (b f) -> p b f", f=FEAT)
            for b, lo, hi in msum:
                v = b[:, 0:(hi - lo) * (FEAT + 1)].rearrange("p (b f) -> p b f", f=FEAT + 1)
                link(V.tensor_scalar(stats[:, 0, lo:hi], v[:, :, FEAT], 1.0, None, ALU.max))
            link(V.reciprocal(stats[:, 1, :], stats[:, 0, :]))
            for b, lo, hi in msum:
                v = b[:, 0:(hi - lo) * (FEAT + 1)].rearrange("p (b f) -> p b f", f=FEAT + 1)
                link(V.tensor_tensor(tmpf[:, lo:hi, :], v[:, :, 0:FEAT], wide(stats[:, 1, lo:hi]), ALU.mult))
            dve.sem_inc(m_read, 1)
            link(V.tensor_tensor(x1, x1, tmpf, ALU.add))
            center(x1, ah, tmpf)
            V.tensor_scalar(stats[:, 1, :], stats[:, 0, :], 1.0 / FEAT, EPS, ALU.mult, ALU.add).then_inc(v2, 1)
            turn_out(0, 0, P)
            copy_block(2, 0, P)
            turn_out(1, 1, P)
            dve.wait_ge(sd2, 1)
            link(V.reciprocal(stats[:, 3, :], stats[:, 2, :]))
            link(V.tensor_tensor(hg, ah, wide(stats[:, 3, :]), ALU.mult))
            link(V.tensor_scalar(hg, hg, 0.0, None, ALU.max))
            dve.wait_ge(sdd, 1)
            link(V.reciprocal(dinv, droot))
            link(V.scalar_tensor_tensor(out=c1, in0=dinv, scalar=BETA, in1=dinv, op0=ALU.mult, op1=ALU.mult))
            link(V.tensor_scalar(cf, dinv, BETA / GAMMA, None, ALU.mult))
            link(V.tensor_tensor(tmpf, hg, wide(dinv), ALU.mult))
            link(V.tensor_scalar(ah, tmpf, ALPHA, None, ALU.mult))
            link(V.tensor_scalar(hg, hg, ALPHA / GAMMA, None, ALU.mult))

            def split(y, res, dest):
                link(V.tensor_copy(dest[:, :, 0, :], y))
                link(V.tensor_tensor(res, y, dest[:, :, 0, :], ALU.subtract))
                link(V.tensor_copy(dest[:, :, 1, :], res))
                return V.tensor_tensor(dest[:, :, 2, :], res, dest[:, :, 1, :], ALU.subtract)

            for k in range(3):
                q = slice(k * FEAT, (k + 1) * FEAT)
                V.tensor_copy(sum3[q, :], identb[q, q]).then_inc(ones_set, 1)
            split(tmpf, tmpg, y3[0]).then_inc(y_set, 1)
            with dve.Fori(1, BLOCKS // 2 - 1) as m:
                for s in range(2):
                    copy_block(2 * m + 1 + s, 1 - s, P)
                    turn_out(2 * m + s, s, P)
            copy_block(BLOCKS - 2, 1, P)
            turn_out(BLOCKS - 3, 0, P)
            copy_block(BLOCKS - 1, 0, LASTN)
            turn_out(BLOCKS - 2, 1, P)
            turn_out(BLOCKS - 1, 0, LASTN)
            dve.wait_ge(turn_d, BLOCKS)
            dve.wait_ge(turned, BLOCKS)
            V.memset(maxima, 0.0).then_inc(scanned, 1)

            def new_y(t, n, par, src_par, last=False):
                q = CHUNKS * t + n
                lo, hi = 4 * n, min(4 * n + 4, BLOCKS)
                k = hi - lo
                rows = P if hi < BLOCKS else LASTN
                dve.wait_ge(r_done, q + 1)
                if last and n:
                    dve.wait_ge(s_res, n)
                rv = banks[2 + par][0:rows, 0:k * FEAT].rearrange("p (b f) -> p b f", f=FEAT)
                c = (cf if last else c1)[0:rows, lo:hi].unsqueeze(2).to_broadcast([rows, k, FEAT])
                yb, rb = yv[0:rows, 0:k, :], yr[0:rows, 0:k, :]
                done = [0]

                def step(ins):
                    done[0] += 1
                    ins.then_inc(y_step, 1)
                    dve.wait_ge(y_step, (5 * q if not last else 5 * CHUNKS * t + n) + done[0])

                step(V.tensor_tensor(yb, rv, c, ALU.mult))
                if last:
                    V.tensor_tensor(yb, yb, hg[0:rows, lo:hi, :], ALU.add).then_inc(y_made, 1)
                    dve.wait_ge(y_made, q + 1)
                    V.tensor_tensor(ycur[0:rows, lo:hi, :], x1[0:rows, lo:hi, :], yb, ALU.add).then_inc(s_res, 1)
                    return
                step(V.tensor_tensor(yb, yb, ah[0:rows, lo:hi, :], ALU.add))
                dest = y3[1 - src_par][0:rows, lo:hi]
                step(V.tensor_copy(dest[:, :, 0, :], yb))
                step(V.tensor_tensor(rb, yb, dest[:, :, 0, :], ALU.subtract))
                step(V.tensor_copy(dest[:, :, 1, :], rb))
                V.tensor_tensor(dest[:, :, 2, :], rb, dest[:, :, 1, :], ALU.subtract).then_inc(y_made, 1)

            for n in range(CHUNKS):
                new_y(0, n, n % 2, 0)
            with dve.Fori(0, (ITERS - 2) // 2) as m:
                for u in range(2):
                    for n in range(CHUNKS):
                        new_y(2 * m + 1 + u, n, (1 + u + n) % 2, (1 + u) % 2)
                        if n < SCANS:
                            at = (2 * m + u) * SCANS + n
                            dve.wait_ge(scanned, at + 1)
                            V.tensor_tensor(maxima, maxima, C[:, bass.ds(at * SCAN, SCAN)], ALU.max).then_inc(scanned, 1)
            dve.wait_ge(scanned, (ITERS - 2) * SCANS + 1)
            V.tensor_reduce(roff[:, :], maxima, AX.X, ALU.max).then_inc(s_max, 1)
            for n in range(CHUNKS):
                new_y(ITERS - 1, n, (ITERS - 1 + n) % 2, (ITERS - 1) % 2, last=True)
                if n == 2:
                    dve.wait_ge(s_max2, 32)
                    link(V.tensor_reduce(mrow[:, 0:1], mrow[:, 1:P + 1], AX.X, ALU.max))
                    V.tensor_scalar(flags[:, 1:2], mrow[:, 0:1], 256.0, None, ALU.is_ge).then_inc(flag2_set, 1)

            def passes(t, k, before):
                with dve.Fori(0, BATCHES) as i:
                    at = t * PASS + 17 + i * YTURNS + 1 + Y_LOADS
                    dve.wait_ge(turns2, at)
                    dve.wait_ge(landed_y[k], before * (64 * BATCHES) + 64 * i + 64)
                    V.tensor_scalar(gidx[:, 2, :], gidx[:, 0, :], 7, None, ALU.arith_shift_right).then_inc(turns2, 1)
                    dve.wait_ge(turns2, at + 1)
                    V.tensor_scalar(gidx[:, 3, :], gidx[:, 0, :], P - 1, None, ALU.bitwise_and).then_inc(turns2, 1)
                    dve.wait_ge(turns2, at + 2)
                    V.tensor_tensor(ylo, iota_l[:, :].unsqueeze(1).to_broadcast([P, TILES, P]),
                                    gidx[:, 3, :].unsqueeze(2).to_broadcast([P, TILES, P]), ALU.is_equal).then_inc(turns2, 1)
                    dve.wait_ge(turns2, at + 3)
                    V.tensor_tensor(yhi, iota_l[:, 0:HI].unsqueeze(1).to_broadcast([P, TILES, HI]),
                                    gidx[:, 2, :].unsqueeze(2).to_broadcast([P, TILES, HI]), ALU.is_equal).then_inc(turns2, 1)
                    for j in range(TILES):
                        dve.wait_ge(turns2, at + 4 + 2 * j)
                        V.tensor_tensor(yexp, yhi[:, j, :].unsqueeze(2).to_broadcast([P, HI, FEAT]),
                                        ygat[:, j * FEAT:(j + 1) * FEAT].unsqueeze(1).to_broadcast([P, HI, FEAT]), ALU.mult).then_inc(turns2, 1)
                dve.wait_ge(turns2, (t + 1) * PASS)

            dve.wait_ge(flag2_set, 1)
            large = dve.value_load(flags[0:1, 1:2], min_val=0, max_val=1)
            with dve.If(large > 0):
                dve.wait_ge(s_out, 16 * CHUNKS)
                sums = [psum[:, 0, 0:GCOL * FEAT].rearrange("p (b f) -> p b f", f=FEAT),
                        psum[:, 1, 0:(HI - GCOL) * FEAT].rearrange("p (b f) -> p b f", f=FEAT)]
                parts = [(sums[0], 0, GCOL), (sums[1], GCOL, HI)]
                link(V.memset(zrow, 0.0))
                link(V.memset(ycur, 1.0))
                link(V.memset(ycur[:, BLOCKS - 1, :], 0.0))
                link(V.memset(ycur[0:LASTN, BLOCKS - 1, :], 1.0))
                dve.sem_inc(turns2, 1)
                passes(0, 0, 0)
                for v, lo, hi in parts:
                    link(V.tensor_scalar(deg[:, lo:hi], v[:, :, 0], 1.0, None, ALU.max))
                V.memset(roff[:, :], 0.0).then_inc(dmx, 1)
                dve.wait_ge(sdd, 2)
                link(V.reciprocal(dinv, droot))
                link(V.scalar_tensor_tensor(out=c1, in0=dinv, scalar=BETA, in1=dinv, op0=ALU.mult, op1=ALU.mult))
                link(V.tensor_scalar(cf, dinv, BETA / GAMMA, None, ALU.mult))
                link(V.tensor_tensor(ah, hg, wide(dinv), ALU.mult))
                link(V.tensor_scalar(ycur, ah, GAMMA / ALPHA, None, ALU.mult))
                V.tensor_scalar(ah, ah, GAMMA, None, ALU.mult).then_inc(turns2, 1)
                with dve.Fori(0, (ITERS - 1) // 3) as m:
                    for u in (1, 2, 3):
                        t = 3 * m + u
                        passes(t, u % 3, m + u // 3)
                        for v, lo, hi in parts:
                            V.tensor_tensor(ycur[:, lo:hi, :], v, wide(c1[:, lo:hi]), ALU.mult).then_inc(y2_step, 1)
                        dve.wait_ge(y2_step, 2 * t)
                        V.tensor_tensor(ycur, ycur, ah, ALU.add).then_inc(turns2, 1)
                passes(ITERS, ITERS % 3, ITERS // 3)
                for k, (v, lo, hi) in enumerate(parts):
                    link(V.tensor_tensor(ycur[:, lo:hi, :], v, wide(cf[:, lo:hi]), ALU.mult))
                link(V.tensor_tensor(ycur, ycur, hg, ALU.add))
                V.tensor_tensor(ycur, ycur, x1, ALU.add).then_inc(turns2, 1)

        @block.tensor
        def _(pe):
            pe.wait_ge(s_const, 11)
            for f, (what, n) in enumerate(FILLS):
                bank = banks[f % 8]
                if f >= 8:
                    pe.wait_ge(s_evac, f - 7)
                    if FILLS[f - 8][0] == "pq":
                        pe.wait_ge(s_pqr, FILLS[f - 8][1] + 1)
                if what == "hT":
                    pe.wait_ge(s_h, 1)
                    for k, b in enumerate(groups(n)):
                        last = T.transpose(bank[0:FEAT, k * P:(k + 1) * P], hn[:, b, :], ident[:, :])
                elif what == "pq":
                    pe.wait_ge(s_evac, 7)
                    pe.wait_ge(s_wpq, 1)
                    pe.wait_ge(s_h3one, 6)
                    for k, b in enumerate(groups(n)):
                        last = T.matmul(bank[:, k * P:(k + 1) * P], hT[:, b * P:(b + 1) * P], wpq[:, :], start=True, stop=True)
                else:
                    pe.wait_ge(s_idxN, {"src": 1, "rel": 2, "lo": 3, "hi": 4, "key": 4, "dcol": 5}[what])
                    gc = P if n == 0 else GB
                    for j in range(TILES):
                        last = T.transpose(bank[:, j * P:j * P + gc], NAT[what][0:gc, n, j * P:(j + 1) * P], ident[0:gc, 0:gc])
                last.then_inc(s_fill, 1)
            pe.wait_ge(s_evac, PRE)

            def rows_q(bank, q, start):
                for j in range(TILES):
                    for k in range(PARTS):
                        last = T.matmul(bank[0:HID, j * P:(j + 1) * P], gat[:, q, j, k, :], identb[:, :],
                                        start=start and j == 0 and k == 0, stop=not start, skip_group_check=True)
                return last

            def stage1(i, s, q, loads, lands):
                pe.wait_ge(pw_loaded[s], loads)
                pe.wait_ge(ohT_made, i + 1)
                if later(i, 2):
                    pe.wait_ge(h1_out, i - 1)
                for u in range(2):
                    h = slice(u * 256, u * 256 + 256)
                    T.matmul(H1[s][0:HID, h], pw[:, s, u, :], ohT[:, s, h], start=u == 0, stop=False, skip_group_check=True)
                pe.wait_ge(landed[q], lands)
                rows_q(H1[s], q, False).then_inc(h1_done, 1)

            def third_layer():
                T.matmul(H3[:, 0:TILES * HID], ones3[:, :], b3p[:, :, :].rearrange("o j f -> o (j f)"), start=True, stop=False, skip_group_check=True)
                for j in range(TILES):
                    last = T.matmul(H3[:, j * HID:(j + 1) * HID], h2s[:, j * P:(j + 1) * P], w3s[:, :], start=False, stop=True, skip_group_check=True)
                return last

            def stage2(i):
                pe.wait_ge(h1_out, i + 1)
                if later(i, 1):
                    pe.wait_ge(h2_out, i)
                T.matmul(H2, w2s[:, :], h1s, start=True, stop=True).then_inc(h2_done, 1)

            def stage3(i):
                pe.wait_ge(h2_out, i + 1)
                if later(i, 1):
                    pe.wait_ge(h3_out, i)
                third_layer().then_inc(h3_done, 1)

            def node_sums(i, s):
                pe.wait_ge(h3_out, i + 1)
                pe.wait_ge(ohS_made, i + 1)
                if later(i, 1):
                    pe.wait_ge(seg_added, i)
                for j in range(TILES):
                    last = T.matmul(SEG[0:HID + 1, :], h3s[:, j, :], ohS[:, s, j, :], start=j == 0, stop=j == TILES - 1)
                last.then_inc(seg_done, 1)

            def counts(i, s, u):
                pe.wait_ge(ohC_made[u], i + 1)
                if later(i, 1):
                    pe.wait_ge(cst_made[u], i)
                for j in (2 * u, 2 * u + 1):
                    T.matmul(DEG, ohL[:, s, j, :], ohH[:, s, j, :], start=False, stop=False, skip_group_check=True)
                    last = T.matmul(CP[u][:, 0:PCOLS], ohL[:, s, j, :], ohC[:, s, j, :], start=j == 2 * u, stop=j == 2 * u + 1)
                last.then_inc(cp_done[u], 1)

            def step(i, s, q, loads, lands):
                stage1(i, s, q, loads, lands)
                if later(i, 1):
                    stage3(i - 1)
                counts(i, s, 0)
                stage2(i)
                if later(i, 1):
                    node_sums(i - 1, 1 - s)
                counts(i, s, 1)

            def edges():
                pe.wait_ge(s_b3p, 1)
                for i in range(SLOTS):
                    step(i, i % 2, i, 32 * (i // 2) + 32, 64)
                with pe.Fori(1, BATCHES // SLOTS) as m:
                    for q in range(SLOTS):
                        step(SLOTS * m + q, q % 2, q, 64 * m + 32 * (q // 2) + 32, 64 * m + 64)
                stage3(BATCHES - 1)
                node_sums(BATCHES - 1, 1)

            def edges_general():
                pe.wait_ge(s_b3p, 1)
                with pe.Fori(0, BATCHES) as i:
                    at = i * TURNS + 1
                    pe.wait_ge(turns, at + LOADS)
                    pe.wait_ge(landed_gen, 64 * i + 64)
                    rows_q(H1[0], 0, True).then_inc(turns, 1)
                    with pe.Fori(0, NP) as w:
                        pe.wait_ge(turns, at + P_AT + w * PSTEP + 17)
                        T.matmul(H1[0][0:HID, :], pw[:, 0, 0, :], ohT[:, 0, :], start=False, stop=False, skip_group_check=True).then_inc(turns, 1)
                    pe.wait_ge(turns, at + MLP_AT + 1)
                    T.matmul(H2, w2s[:, :], h1s, start=True, stop=True).then_inc(turns, 1)
                    pe.wait_ge(turns, at + MLP_AT + 3)
                    third_layer().then_inc(turns, 1)
                    with pe.Fori(0, NW) as w:
                        pe.wait_ge(turns, at + S_AT + w * SSTEP + 1)
                        for j in range(TILES):
                            last = T.matmul(SEG[0:HID + 1, :], h3s[:, j, :], ohS[:, 0, j, :], start=j == 0, stop=j == TILES - 1)
                        last.then_inc(turns, 1)
                    pe.wait_ge(turns, at + K_AT + 6)
                    for j in range(TILES):
                        last = T.matmul(DEG, ohL[:, 0, j, :], ohH[:, 0, j, :], start=False, stop=False, skip_group_check=True)
                    last.then_inc(turns, 1)
                    with pe.Fori(0, NC) as w:
                        pe.wait_ge(turns, at + C_AT + w * CSTEP + 1)
                        for j in range(TILES):
                            last = T.matmul(CP[0][:, 0:PCOLS], ohL[:, 0, j, :], ohC[:, 0, j, :], start=j == 0, stop=j == TILES - 1)
                        last.then_inc(turns, 1)

            pe.wait_ge(s_clear0, 1)
            T.matmul(DEG, identb[:, :], C[:, 0:HI], start=True, stop=False, skip_group_check=True)
            general(pe, edges, edges_general)
            pe.wait_ge(edges_done, 1)
            for b in range(BLOCKS):
                bank, k = (banks[6], b) if b < MB else (banks[7], b - MB)
                last = T.matmul(bank[:, k * (FEAT + 1):(k + 1) * (FEAT + 1)], sT[0:HID + 1, b * P:(b + 1) * P], w4s[:, :], start=True, stop=True)
            last.then_inc(m_done, 1)
            def turn(w, s, k):
                pe.wait_ge(staged, w + 1)
                if later(w, 2):
                    pe.wait_ge(turn_a, w - 1)
                    pe.wait_ge(turn_d, w - 1)
                v = stage[s].rearrange("p (t a) -> p t a", a=HI)
                for f, (lo, hi) in enumerate(SPLIT):
                    for a in range(lo, hi):
                        last = T.transpose(bankb[4 * s + f][0:k, (a - lo) * P:(a - lo + 1) * P], v[:, 0:k, a], identb[:, :])
                last.then_inc(turned, 1)

            pe.wait_ge(dmx, 1)
            turn(0, 0, P)
            pe.wait_ge(m_read, 1)
            turn(1, 1, P)
            with pe.Fori(1, BLOCKS // 2) as m:
                for s in range(2):
                    turn(2 * m + s, s, P)
            turn(BLOCKS - 1, 0, LASTN)
            pe.wait_ge(turn_a, BLOCKS)
            pe.wait_ge(turn_d, BLOCKS)
            def gather_groups(t, n, par):
                q = CHUNKS * t + n
                pe.wait_ge(o_out, q + 1)
                if later(t, 1) or q >= 2:
                    pe.wait_ge(y_made, q - 1)
                for b in range(4 * n, min(4 * n + 4, BLOCKS)):
                    k = P if b < BLOCKS - 1 else LASTN
                    o = b - 4 * n
                    last = T.matmul(banks[2 + par][0:k, o * FEAT:(o + 1) * FEAT], osb[par][:, o * P:o * P + k], sum3[0:3 * FEAT, :],
                                    start=True, stop=True)
                last.then_inc(r_done, 1)

            def iteration(t, tp):
                for n in range(CHUNKS):
                    q = CHUNKS * t + n
                    par = (tp + n) % 2
                    w = min(CHUNK, NODES - n * CHUNK)
                    if later(t, 1) or q >= 2:
                        pe.wait_ge(o_out, q - 1)
                    for b in range(BLOCKS):
                        if n == 0 and b % 4 == 0 and later(t, 1):
                            pe.wait_ge(y_made, CHUNKS * (t - 1) + b // 4 + 1)
                        k = P if b < BLOCKS - 1 else LASTN
                        last = T.matmul(banks[par][0:3 * FEAT, 0:w], y3[tp][0:k, b, :, :].rearrange("p k f -> p (k f)"),
                                        C[0:k, b * NODES + n * CHUNK:b * NODES + n * CHUNK + w], start=b == 0, stop=b == BLOCKS - 1)
                        if b == 8 and (n > 0 or later(t, 1)):
                            if n > 0:
                                gather_groups(t, n - 1, 1 - par)
                            else:
                                gather_groups(t - 1, CHUNKS - 1, 1 - par)
                    last.then_inc(o_done, 1)

            pe.wait_ge(y_set, 1)
            pe.wait_ge(ones_set, 3)
            iteration(0, 0)
            with pe.Fori(0, (ITERS - 2) // 2) as m:
                iteration(2 * m + 1, 1)
                iteration(2 * m + 2, 0)
            iteration(ITERS - 1, (ITERS - 1) % 2)
            gather_groups(ITERS - 1, CHUNKS - 1, (ITERS + CHUNKS) % 2)
            pe.wait_ge(flag2_set, 1)
            large = pe.value_load(flags[0:1, 1:2], min_val=0, max_val=1)
            with pe.If(large > 0):
                with pe.Fori(0, ITERS + 1) as t:
                    pe.wait_ge(turns2, t * PASS + 1 + 16)
                    for k in range(2):
                        last = T.matmul(banks[k][:, :], ones1[:, :], zrow[0:1, :], start=True, stop=False, skip_group_check=True)
                    last.then_inc(turns2, 1)
                    with pe.Fori(0, BATCHES) as i:
                        at = t * PASS + 17 + i * YTURNS + 1 + YT_AT
                        for j in range(TILES):
                            pe.wait_ge(turns2, at + 2 * j + 1)
                            for k, (lo, hi) in enumerate(((0, GCOL), (GCOL, HI))):
                                last = T.matmul(banks[k][:, 0:(hi - lo) * FEAT], ylo[:, j, :], yexp[:, lo:hi, :].rearrange("p a f -> p (a f)"),
                                                start=False, stop=False, skip_group_check=True)
                            last.then_inc(turns2, 1)


_INS = ["x", "src", "dst"] + [f"L0_gnn_{a}{n}" for n in range(1, 5) for a in "Wb"]


def kernel(**inputs):
    import concourse.bacc as bacc
    from concourse.bass_utils import run_bass_kernel_spmd as run

    nc = bacc.Bacc("TRN2", target_bir_lowering=False, num_devices=1)
    arrays, args = {}, []
    for name in _INS:
        a = np.ascontiguousarray(inputs[name])
        arrays[f"in_{name}"] = a
        args.append(nc.dram_tensor(f"in_{name}", a.shape, mybir.dt.from_np(a.dtype), kind="ExternalInput").ap())
    result = nc.dram_tensor("out_0", (NODES, FEAT), F32, kind="ExternalOutput").ap()
    build(nc, *args, result)
    return run(nc, [arrays], core_ids=[0]).results[0]["out_0"]
```

```python
import numpy as np

import concourse.bass as bass
from concourse import mybir
from contextlib import ExitStack

F32 = mybir.dt.float32
BF16 = mybir.dt.bfloat16
F16 = mybir.dt.float16
I32 = mybir.dt.int32
I16 = mybir.dt.int16
ALU = mybir.AluOpType
ACT = mybir.ActivationFunctionType
AX = mybir.AxisListType

NODES, EDGES, FEAT, HID, HID2 = 3125, 100000, 32, 64, 128
P = 128
BLOCKS = -(-NODES // P)
LASTN = NODES - (BLOCKS - 1) * P
HI = BLOCKS
TILES = 4
BATCH = TILES * P
BATCHES = -(-EDGES // BATCH)
TAIL = EDGES - (BATCHES - 1) * BATCH
GB = BATCHES - P
SPAN = 64
PSPAN = 20
PWIN, PARTS = 32, 3
PCOLS = PSPAN * HI
SLOTS = 4
PROWS = PARTS * PWIN
PAD_DST = 4095
CCOLS = -(-(NODES + PSPAN) * HI // 2) * 2
SCOLS = BLOCKS * P
ITERS, ALPHA, BETA = 10, 0.1, 0.9
GAMMA = float(np.float32(BETA ** ITERS + ALPHA * sum(BETA ** i for i in range(ITERS))))
EPS = 1e-5
FIRST = [0, 4, 8, 12, 16, 19, 22, BLOCKS]
CHUNKS = len(FIRST) - 1
GATHER_AT = [12, 14, 14, 14, 18, 20, 20]


def columns(n):
    return FIRST[n] * P, min(FIRST[n + 1] * P, NODES) - FIRST[n] * P


SCAN_AFTER = [0, 1, 2, 3, CHUNKS - 1]
SCANS = len(SCAN_AFTER)
SCAN = -(-NODES * BLOCKS // ((ITERS - 2) * SCANS) // 2) * 2
assert SCAN * (ITERS - 2) * SCANS <= CCOLS


def build(nc, x, src, dst, W1, b1, W2, b2, W3, b3, W4, b4, out):
    V, A, T, G = nc.vector, nc.scalar, nc.tensor, nc.gpsimd
    ctx = ExitStack()
    with ctx:
        def sb(name, shape, dt):
            return ctx.enter_context(nc.sbuf_tensor(name, shape, dt))

        def sem(name):
            return ctx.enter_context(nc.semaphore(name))

        def dram(name, shape, dt):
            return nc.dram_tensor(name, shape, dt, kind="Internal").ap()

        TABC = 8
        p_tab = dram("p_tab", (SCOLS, PARTS * HID), BF16)
        q_tab = dram("q_tab", (SCOLS, PARTS * HID), BF16)
        idx_d = dram("idx_d", (P, BATCHES * TILES), I32)
        rel_d = dram("rel_d", (BATCHES, BATCH), I16)
        dst_d = dram("dst_d", (BATCHES, BATCH), I32)
        dcol_d = dram("dcol_d", (P, BATCHES * TILES), I32)
        y_tab = dram("y_tab", (SCOLS, FEAT), F32)
        max_d = dram("max_d", (P,), F32)
        tab_d = dram("tab_d", (BATCHES, TABC), I32)

        C = sb("C", [P, CCOLS], BF16)
        sT = sb("sT", [P, SCOLS], F32)
        key = sb("key", [P, BATCHES, TILES], F32)
        locol = sb("locol", [P, BATCHES, TILES], F16)
        hicol = sb("hicol", [P, BATCHES, TILES], F16)
        relcol = sb("relcol", [P, BATCHES, TILES], I16)
        tab = sT[96:97, 0:BATCHES * TABC].bitcast(I32)
        identb = sb("identb", [P, P], BF16)
        iota_c = sb("iota_c", [P, PCOLS], F16)
        iota_l = sb("iota_l", [P, P], F16)
        iota_s = sb("iota_s", [P, SPAN], F16)
        pcol = sb("pcol", [P, 1], F32)
        w2s = sb("w2s", [HID, HID2], F32)
        w3s = sb("w3s", [HID2, HID], F32)
        w4s = sb("w4s", [HID + 1, FEAT + 1], F32)
        b2c = sb("b2c", [HID2, 1], F32)
        ones1 = sb("ones1", [1, P], F32)
        b3p = sb("b3p", [96, TILES, HID], BF16)
        ones3 = sb("ones3", [96, P], BF16)
        pmod = sb("pmod", [P, 1], F32)
        idx = sb("idx", [P, SLOTS, TILES], I32)
        stats = sb("stats", [P, 4, BLOCKS], F32)

        class Region:
            def __init__(self, ap):
                self.ap, self.at = ap, 0

            def take(self, n):
                self.at += n
                assert self.at <= self.ap.shape[1], (self.at, self.ap.shape)
                return self.ap[:, self.at - n:self.at]

        work = sb("work", [P, 7600], F32)
        flags = sb("flags", [1, 2], I32)
        roff = sb("roff", [P, 1], F32)
        gidx = work[:, 1520:1520 + 5 * TILES].bitcast(I32).rearrange("p (c j) -> p c j", j=TILES)
        r = Region(work[:, :])
        gat = r.take(SLOTS * TILES * PARTS * HID // 2).bitcast(BF16).rearrange("p (s j k n) -> p s j k n", s=SLOTS, j=TILES, k=PARTS)
        relb = r.take(BATCH).bitcast(I16).rearrange("p (s n) -> p s n", s=2)[0:PROWS]
        pw = r.take(2 * HID).bitcast(BF16).rearrange("p (s u n) -> p s u n", s=2, u=2)[0:PROWS]
        ohT = r.take(BATCH).bitcast(BF16).rearrange("p (s n) -> p s n", s=2)[0:PROWS]
        ohS = r.take(2 * TILES * SPAN).rearrange("p (s j n) -> p s j n", s=2, j=TILES)
        ohL = r.take(TILES * P).bitcast(BF16).rearrange("p (s j n) -> p s j n", s=2, j=TILES)
        ohH = r.take(TILES * HI).bitcast(BF16).rearrange("p (s j n) -> p s j n", s=2, j=TILES)
        ohC = r.take(TILES * PCOLS).bitcast(BF16).rearrange("p (s j n) -> p s j n", s=2, j=TILES)
        cst = r.take(PCOLS).bitcast(BF16).rearrange("p (u n) -> p u n", u=2)
        h1s = r.take(BATCH)[0:HID]
        h2s = r.take(BATCH)
        h3s = r.take(TILES * (HID + 1)).rearrange("p (j n) -> p j n", j=TILES)
        grow = work[0:PROWS, 2 * TILES * PARTS * HID // 2:2 * TILES * PARTS * HID // 2 + BATCH].bitcast(I32)
        r = Region(work[:, :])
        stage = [r.take(P * HI // 2).bitcast(BF16) for _ in range(2)]
        maxima = stage[1][:, 0:SCAN]
        mrow = stage[1].bitcast(F32)[0:1, 1400:1400 + P + 1]
        ycur = stage[0].bitcast(F32)[:, 0:BLOCKS * FEAT].rearrange("p (b f) -> p b f", f=FEAT)
        ygat = stage[0].bitcast(F32)[:, 800:800 + TILES * FEAT]
        ylo = stage[0].bitcast(F32)[:, 1000:1000 + TILES * P].rearrange("p (j n) -> p j n", j=TILES)
        yexp = stage[1].bitcast(F32)[:, 0:HI * FEAT].rearrange("p (a f) -> p a f", f=FEAT)
        zrow = stage[1].bitcast(F32)[0:1, 1088:1600]
        yhi = stage[1].bitcast(F32)[:, 800:800 + TILES * HI].rearrange("p (j n) -> p j n", j=TILES)
        x1 = r.take(BLOCKS * FEAT).rearrange("p (b f) -> p b f", f=FEAT)
        hg = r.take(BLOCKS * FEAT).rearrange("p (b f) -> p b f", f=FEAT)
        ah = r.take(BLOCKS * FEAT).rearrange("p (b f) -> p b f", f=FEAT)
        TMPF = r.at
        osb = [r.take(3 * 512 // 2).bitcast(BF16).rearrange("p (k n) -> p k n", k=3)[0:3 * FEAT] for _ in range(2)]
        rest = stage[0].bitcast(F32)[0:3 * FEAT, 800:800 + 512]
        r = Region(sT[:, :])
        y3 = [r.take(BLOCKS * 3 * FEAT // 2).bitcast(BF16).rearrange("p (b k f) -> p b k f", k=3, f=FEAT) for _ in range(2)]
        yv = r.take(4 * FEAT).rearrange("p (b f) -> p b f", f=FEAT)
        yr = r.take(4 * FEAT).rearrange("p (b f) -> p b f", f=FEAT)
        sum3 = r.take(FEAT // 2).bitcast(BF16)

        tmpf = work[:, TMPF:TMPF + BLOCKS * FEAT].rearrange("p (b f) -> p b f", f=FEAT)
        tmpg = y3[1].rearrange("p b k f -> p (b k f)").bitcast(F32)[:, 0:BLOCKS * FEAT].rearrange("p (b f) -> p b f", f=FEAT)

        TAILF = SCOLS + 9 * 1024
        T0 = CCOLS - 2 * TAILF
        T1 = CCOLS - 2 * 4 * 2 * BATCH
        r = Region(C[:, T0:T0 + 2 * TAILF].bitcast(F32))

        def batches(dt):
            return r.take(2 * BATCH).bitcast(dt).rearrange("p (c e) -> p c e", c=2)

        hT = r.take(SCOLS)[0:FEAT + 1, :]
        dN, sN, aN = (batches(I32) for _ in range(3))
        relF, keyF, floF, srcf, dclF = (batches(F32) for _ in range(5))
        fhi = srcf
        pqr = batches(F32)
        r = Region(sT[:, :])
        xc, sq, hn, x_sb = (r.take(BLOCKS * FEAT).rearrange("p (b f) -> p b f", f=FEAT) for _ in range(4))
        r = Region(work[:, :])
        pq = r.take(BLOCKS * PARTS * HID).bitcast(BF16).rearrange("p (h b k f) -> p h b k f", h=2, k=PARTS, f=HID)
        idxt = r.take(BATCHES * TILES).bitcast(I32).rearrange("p (g j) -> p g j", j=TILES)
        wpq = r.take(2 * HID)[0:FEAT + 1]
        w1b = r.take(HID)[0:FEAT]
        b3f = r.take(TILES * HID).rearrange("p (j n) -> p j n", j=TILES)[0:96]
        ident = r.take(P)
        relN = r.take(BATCH).bitcast(I16).rearrange("p (c e) -> p c e", c=2)
        dcolt = r.take(BATCHES * TILES).bitcast(I32).rearrange("p (g j) -> p g j", j=TILES)
        pmn = r.take(4)
        pmx = r.take(4)
        bmn = r.take(2)
        bmx = r.take(2)
        pfl = r.take(4)
        tabN = r.take(2 * TABC).bitcast(I32).rearrange("p (c k) -> p c k", c=2)

        psum = ctx.enter_context(nc.psum_tensor("psum", [P, 8, 512], F32))
        banks = [psum[:, n, :] for n in range(8)]
        H1, H2, H3, CP = banks[0:2], banks[2], banks[3], banks[6:8]
        SEG, DEG = psum[:, 4, 0:SPAN], psum[:, 5, 0:HI]
        key_f = key[:, :, :].rearrange("p g j -> p (g j)")
        deg, droot, dinv, c1, cf = (key_f[:, n * BLOCKS:(n + 1) * BLOCKS] for n in range(5))

        s_edges, s_x, s_w, s_pads, s_const = (sem(n) for n in ("s_edges", "s_x", "s_w", "s_pads", "s_const"))
        s_dve = sem("s_dve")
        s_var, s_std = sem("s_var"), sem("s_std")
        s_h, s_wpq, s_h3one = sem("s_h"), sem("s_wpq"), sem("s_h3one")
        s_idxN, s_keyN = sem("s_idxN"), sem("s_keyN")
        s_fill, s_evac = sem("s_fill"), sem("s_evac")
        s_idxd, s_qtab, s_ptab, s_rel, s_tabw, s_tab, s_clear = (sem(n) for n in ("s_idxd", "s_qtab", "s_ptab", "s_rel", "s_tabw", "s_tab", "s_clear"))
        idx_loaded = [sem(f"idx_loaded{i}") for i in range(SLOTS)]
        landed = [sem(f"landed{i}") for i in range(SLOTS)]
        rel_loaded = [sem(f"rel_loaded{i}") for i in range(2)]
        pw_loaded = [sem(f"pw_loaded{i}") for i in range(2)]
        cst_made, s_pqr, s_pq2 = [sem(f"cst_made{u}") for u in range(2)], sem("s_pqr"), sem("s_pq2")
        s_pool, scales_made = sem("s_pool"), sem("scales_made")
        s_clear0, s_dcol = sem("s_clear0"), sem("s_dcol")
        s_pq1 = sem("s_pq1")
        s_b3, s_b3p = sem("s_b3"), sem("s_b3p")
        ohT_made, ohS_made = sem("ohT_made"), sem("ohS_made")
        ohC_made = [sem(f"ohC_made{u}") for u in range(2)]
        cp_done = [sem(f"cp_done{u}") for u in range(2)]
        cp_added = [sem(f"cp_added{u}") for u in range(2)]
        h1_done, h1_out = sem("h1_done"), sem("h1_out")
        h2_done, h2_out, h3_done, h3_out = sem("h2_done"), sem("h2_out"), sem("h3_done"), sem("h3_out")
        seg_done, seg_added = sem("seg_done"), sem("seg_added")
        s_gen, flag_set, turns, edges_done = sem("s_gen"), sem("flag_set"), sem("turns"), sem("edges_done")
        scanned, s_max, s_max2, flag2_set, turns2 = sem("scanned"), sem("s_max"), sem("s_max2"), sem("flag2_set"), sem("turns2")
        s_x1pad, s_x1, s_res, s_out, s_out2 = sem("s_x1pad"), sem("s_x1"), sem("s_res"), sem("s_out"), sem("s_out2")
        staged, turned, turn_a, turn_d = sem("staged"), sem("turned"), sem("turn_a"), sem("turn_d")
        m_done, m_read, ones_set = sem("m_done"), sem("m_read"), sem("ones_set")
        v2, sd2, dmx, sdd = sem("v2"), sem("sd2"), sem("dmx"), sem("sdd")
        o_hi, o_rest, o_mid = sem("o_hi"), sem("o_rest"), sem("o_mid")
        y_set, o_done, o_out, r_done, y_made = sem("y_set"), sem("o_done"), sem("o_out"), sem("r_done"), sem("y_made")
        y_step, gathers_begun = sem("y_step"), sem("gathers_begun")
        y2_step, landed_gen = sem("y2_step"), sem("landed_gen")
        landed_y = [sem(f"landed_y{k}") for k in range(3)]

        NP, NW, NC = (-(-NODES // n) for n in (PWIN, SPAN, PSPAN))
        LOADS = 3 * 16
        PSTEP, SSTEP, CSTEP = 16 + 3, 4, 4
        P_AT = LOADS + 2
        MLP_AT = P_AT + NP * PSTEP
        S_AT = MLP_AT + 6
        K_AT = S_AT + NW * SSTEP
        C_AT = K_AT + 8
        TURNS = C_AT + NC * CSTEP
        GCOL = 13
        Y_LOADS = 2 * 16
        YT_AT = Y_LOADS + 4
        YTURNS = YT_AT + 2 * TILES
        PASS = 16 + 1 + BATCHES * YTURNS + 1

        def general(e, body_fast, body_general):
            e.wait_ge(flag_set, 1)
            wide_batches = e.value_load(flags[0:1, 0:1], min_val=0, max_val=1)
            with e.If(wide_batches < 1):
                body_fast()
            with e.Else():
                body_general()

        SPLIT = [(0, 5), (5, 10), (10, 18), (18, HI)]
        TD = 2 * 5
        psum_b = psum[:, :, :].bitcast(BF16)
        bankb = [b[:, :].bitcast(BF16) for b in banks]
        MB = 15
        ALONE = 4

        def later(i, n):
            return not (isinstance(i, int) and i < n)

        def turned_cols(w, lo, n):
            return C[:, bass.ds(w * NODES + lo, n)]

        FILLS = [("hT", n) for n in range(7)] + [("src", c) for c in range(2)] + [("pq", n) for n in range(7)] + \
                [(a, c) for a in ("rel", "lo", "hi", "key", "dcol") for c in range(2)]
        PQ_DONE = FILLS.index(("pq", 6)) + 1
        SRC_DONE = FILLS.index(("src", 1)) + 1
        PRE = len(FILLS)
        NAT = {"src": srcf, "lo": floF, "hi": fhi, "key": keyF, "rel": relF, "dcol": dclF}

        def groups(n):
            return range(4 * n, min(4 * n + 4, BLOCKS))

        def wide(ap):
            return ap.unsqueeze(2).to_broadcast([P, ap.shape[1], FEAT])

        def part(n, k):
            return pq[:, :, 4 * n:4 * n + len(groups(n)), k, :]

        def by_half(buf, k):
            return buf.rearrange("p (b h f) -> p h b f", h=2, f=HID)[:, :, 0:k, :]

        block = ctx.enter_context(nc.Block())

        @block.sync
        def _(sp):
            xv = x[0:(BLOCKS - 1) * P, :].rearrange("(b p) f -> p b f", p=P)
            sp.dma_start(x_sb[:, 0:BLOCKS - 1, :], xv).then_inc(s_x, 16)
            sp.wait_ge(s_pads, 3)
            sp.dma_start(x_sb[0:LASTN, BLOCKS - 1, :], x[(BLOCKS - 1) * P:NODES, :]).then_inc(s_x, 16)
            full = (BATCHES - 1 - P)
            for nat, e in ((dN, dst), (sN, src)):
                sp.dma_start(nat[:, 0, :], e[0:P * BATCH].rearrange("(p e) -> p e", e=BATCH)).then_inc(s_edges, 16)
                sp.dma_start(nat[0:full, 1, :], e[P * BATCH:(P + full) * BATCH].rearrange("(p e) -> p e", e=BATCH)).then_inc(s_edges, 16)
                sp.dma_start(nat[full:full + 1, 1, 0:TAIL], e[EDGES - TAIL:EDGES].rearrange("(p e) -> p e", p=1)).then_inc(s_edges, 16)
            sp.wait_ge(s_edges, 96)
            sp.dma_start(dst_d[0:P, :], dN[:, 0, :]).then_inc(s_gen, 16)
            sp.dma_start(dst_d[P:BATCHES, :], dN[0:GB, 1, :]).then_inc(s_gen, 16)
            sp.wait_ge(s_keyN, 1)
            sp.dma_start(rel_d[0:P, :], relN[:, 0, :]).then_inc(s_rel, 16)
            sp.dma_start(rel_d[P:BATCHES, :], relN[0:GB, 1, :]).then_inc(s_rel, 16)
            sp.dma_start(tab_d[0:P, :], tabN[:, 0, :]).then_inc(s_tabw, 16)
            sp.dma_start(tab_d[P:BATCHES, :], tabN[0:GB, 1, :]).then_inc(s_tabw, 16)
            sp.wait_ge(s_evac, SRC_DONE)
            sp.dma_start(idx_d, idxt[:, :, :].rearrange("p g j -> p (g j)")).then_inc(s_idxd, 16)
            sp.wait_ge(s_tabw, 32)
            sp.dma_start(tab[:, :], tab_d.rearrange("g c -> (g c)").rearrange("(o n) -> o n", o=1)).then_inc(s_tab, 16)
            def load_indices(i, q):
                sp.dma_start(idx[:, q, :], idx_d[:, bass.ds(TILES * i, TILES)]).then_inc(idx_loaded[q], 16)

            def store_table(table, h, lo, hi, landed_at):
                sp.dma_start(table[lo * P:hi * P, :].rearrange("(b p) c -> p b c", p=P),
                             pq[:, h, lo:hi, :, :].rearrange("p b k f -> p b (k f)")).then_inc(landed_at, 16)

            sp.wait_ge(s_pq1, 4)
            sp.wait_ge(s_pq2, 4)
            store_table(q_tab, 0, 0, 16, s_qtab)
            sp.wait_ge(s_pq1, 7)
            sp.wait_ge(s_pq2, 7)
            store_table(q_tab, 0, 16, BLOCKS, s_qtab)
            sp.wait_ge(s_idxd, 16)
            load_indices(0, 0)
            load_indices(1, 1)
            store_table(p_tab, 1, 0, 16, s_ptab)
            store_table(p_tab, 1, 16, BLOCKS, s_ptab)
            sp.wait_ge(s_tab, 16)
            sp.wait_ge(s_rel, 32)

            def load(i, s, q):
                base = nc.values_load_multi_w_load_instructions(
                    tab[0:1, bass.ds(TABC * i + 4, 2)], (mybir.EngineType.SP,), min_val=0, max_val=NODES - 1)[1]
                if later(i, 2):
                    sp.wait_ge(ohT_made, i - 1)
                sp.dma_start(relb[:, s, :], rel_d[bass.ds(i, 1), :].rearrange("o e -> (o e)").partition_broadcast(PROWS)).then_inc(rel_loaded[s], 16)
                if later(i, 2):
                    sp.wait_ge(h1_done, i - 1)
                for u in range(2):
                    sp.dma_start(pw[:, s, u, :], p_tab[bass.ds(base[u], PWIN), :].rearrange("r (k f) -> k r f", k=PARTS)).then_inc(pw_loaded[s], 16)
                if q is not None:
                    load_indices(i + 2, q)

            def edges():
                sp.wait_ge(s_qtab, 32)
                sp.wait_ge(s_ptab, 32)
                for i in range(SLOTS):
                    load(i, i % 2, (i + 2) % SLOTS)
                with sp.Fori(1, BATCHES // SLOTS - 1) as m:
                    for q in range(SLOTS):
                        load(SLOTS * m + q, q % 2, (q + 2) % SLOTS)
                for i in range(BATCHES - SLOTS, BATCHES):
                    load(i, i % 2, (i + 2) % SLOTS if i + 2 < BATCHES else None)

            def edges_general():
                sp.wait_ge(s_gen, 32)
                sp.wait_ge(idx_loaded[0], 16)
                sp.wait_ge(s_qtab, 32)
                sp.wait_ge(s_ptab, 32)
                sp.wait_ge(s_dcol, 16)
                with sp.Fori(0, BATCHES) as i:
                    at = i * TURNS + 1
                    sp.wait_ge(turns, at)
                    sp.dma_start(idx[:, 0, :], idx_d[:, bass.ds(TILES * i, TILES)]).then_inc(turns, 16)
                    sp.wait_ge(turns, at + 16)
                    sp.dma_start(gidx[:, 1, :], dcol_d[:, bass.ds(TILES * i, TILES)]).then_inc(turns, 16)
                    sp.wait_ge(turns, at + 32)
                    sp.dma_start(grow, dst_d[bass.ds(i, 1), :].rearrange("o e -> (o e)").partition_broadcast(PROWS)).then_inc(turns, 16)
                    with sp.Fori(0, NP) as w:
                        sp.wait_ge(turns, at + P_AT + w * PSTEP)
                        sp.dma_start(pw[:, 0, 0, :], p_tab[bass.ds(w * PWIN, PWIN), :].rearrange("r (k f) -> k r f", k=PARTS)).then_inc(turns, 16)

            general(sp, edges, edges_general)
            sp.wait_ge(s_x1pad, 1)
            sp.dma_start(x1[:, 0:BLOCKS - 1, :], xv).then_inc(s_x1, 16)
            sp.dma_start(x1[0:LASTN, BLOCKS - 1, :], x[(BLOCKS - 1) * P:NODES, :]).then_inc(s_x1, 16)
            sp.wait_ge(s_max, 1)
            sp.dma_start(max_d.rearrange("(n o) -> n o", o=1), roff[:, 0:1]).then_inc(s_max2, 16)
            sp.wait_ge(s_max2, 16)
            sp.dma_start(mrow[:, 1:P + 1], max_d.rearrange("(o n) -> o n", o=1)).then_inc(s_max2, 16)
            for n in range(CHUNKS):
                sp.wait_ge(s_res, n + 1)
                lo, hi = FIRST[n], min(FIRST[n + 1], BLOCKS - 1)
                sp.dma_start(out[lo * P:hi * P, :].rearrange("(b p) f -> p b f", p=P), ycur[:, lo:hi, :]).then_inc(s_out, 16)
            sp.dma_start(out[(BLOCKS - 1) * P:NODES, :], ycur[0:LASTN, BLOCKS - 1, :]).then_inc(s_out, 16)
            sp.wait_ge(s_out, 16 * (CHUNKS + 1))
            sp.wait_ge(flag2_set, 1)
            large = sp.value_load(flags[0:1, 1:2], min_val=0, max_val=1)
            with sp.If(large > 0):
                with sp.Fori(0, ITERS + 1) as t:
                    sp.wait_ge(turns2, t * PASS + 1)
                    sp.dma_start(y_tab.rearrange("(b p) f -> p b f", p=P), ycur).then_inc(turns2, 16)
                    with sp.Fori(0, BATCHES) as i:
                        at = t * PASS + 17 + i * YTURNS + 1
                        sp.wait_ge(turns2, at)
                        sp.dma_start(gidx[:, 0, :], idx_d[:, bass.ds(TILES * i, TILES)]).then_inc(turns2, 16)
                        sp.wait_ge(turns2, at + 16)
                        sp.dma_start(gidx[:, 1, :], dcol_d[:, bass.ds(TILES * i, TILES)]).then_inc(turns2, 16)
                sp.wait_ge(turns2, (ITERS + 1) * PASS + 1)
                sp.dma_start(out[0:(BLOCKS - 1) * P, :].rearrange("(b p) f -> p b f", p=P), ycur[:, 0:BLOCKS - 1, :]).then_inc(s_out2, 16)
                sp.dma_start(out[(BLOCKS - 1) * P:NODES, :], ycur[0:LASTN, BLOCKS - 1, :]).then_inc(s_out2, 16)
                sp.wait_ge(s_out2, 32)

        @block.gpsimd
        def _(g):
            G.iota(iota_c[:, :], [[1, PCOLS]], base=0, channel_multiplier=0, allow_small_or_imprecise_dtypes=True).then_inc(s_const, 1)
            G.iota(iota_l[:, :], [[1, P]], base=0, channel_multiplier=0, allow_small_or_imprecise_dtypes=True).then_inc(s_const, 1)
            G.iota(iota_s[:, :], [[1, SPAN]], base=0, channel_multiplier=0, allow_small_or_imprecise_dtypes=True).then_inc(s_const, 1)
            G.iota(pcol[:, :], [[1, 1]], base=0, channel_multiplier=1, allow_small_or_imprecise_dtypes=True).then_inc(s_const, 1)
            for k in range(PARTS):
                g.wait_ge(s_const, 4 + k)
                G.iota(pmod[k * PWIN:(k + 1) * PWIN, :], [[1, 1]], base=0, channel_multiplier=1, allow_small_or_imprecise_dtypes=True).then_inc(s_const, 1)
            g.wait_ge(s_const, 7)
            G.memset(ident[:, :], 0.0).then_inc(s_const, 1)
            G.memset(identb[:, :], 0.0).then_inc(s_const, 1)
            g.wait_ge(s_const, 9)
            for m in (ident, identb):
                G.affine_select(out=m[:, :], in_=m[:, :], compare_op=ALU.not_equal, fill=1.0, base=0,
                                pattern=[[-1, P]], channel_multiplier=1).then_inc(s_const, 1)
            G.memset(C[:, 0:T0].bitcast(F32), 0.0).then_inc(s_clear0, 1)
            g.wait_ge(s_evac, 7)
            G.memset(sT[0:HID + 1, :], 0.0).then_inc(s_clear, 1)
            g.wait_ge(s_evac, PQ_DONE)
            G.memset(C[:, T0:T0 + 2 * SCOLS].bitcast(F32), 0.0).then_inc(s_clear, 1)
            g.wait_ge(s_qtab, 32)

            def gather(q, loads):
                g.wait_ge(idx_loaded[q], loads)
                g.sem_inc(gathers_begun, 1)
                for j in range(TILES):
                    G.indirect_dma_start(out=gat[:, q, j, :, :].rearrange("p k f -> p (k f)"), out_offset=None, in_=q_tab,
                                         in_offset=bass.IndirectOffsetOnAxis(ap=idx[:, q, j:j + 1], axis=0)).then_inc(landed[q], 16)

            def edges():
                for i in range(SLOTS):
                    gather(i, 16)
                with g.Fori(1, BATCHES // SLOTS) as m:
                    for q in range(SLOTS):
                        gather(q, 16 * m + 16)

            def edges_general():
                with g.Fori(0, BATCHES) as i:
                    g.wait_ge(turns, i * TURNS + 1 + 48)
                    g.sem_inc(gathers_begun, 1)
                    for j in range(TILES):
                        G.indirect_dma_start(out=gat[:, 0, j, :, :].rearrange("p k f -> p (k f)"), out_offset=None, in_=q_tab,
                                             in_offset=bass.IndirectOffsetOnAxis(ap=idx[:, 0, j:j + 1], axis=0)).then_inc(landed_gen, 16)

            general(g, edges, edges_general)
            steps = [0]

            def link(ins):
                steps[0] += 1
                ins.then_inc(s_pool, 1)
                g.wait_ge(s_pool, steps[0])

            g.wait_ge(scales_made, 1)
            link(G.tensor_tensor(hg, ah, wide(stats[:, 3, :]), ALU.mult))
            link(G.tensor_tensor(tmpf, hg, wide(dinv), ALU.mult))
            link(G.tensor_scalar(ah, tmpf, ALPHA, None, ALU.mult))
            link(G.tensor_scalar(hg, hg, ALPHA / GAMMA, None, ALU.mult))
            parts = y3[0]
            link(G.tensor_copy(parts[:, :, 0, :], tmpf))
            link(G.tensor_tensor(tmpg, tmpf, parts[:, :, 0, :], ALU.subtract))
            link(G.tensor_copy(parts[:, :, 1, :], tmpg))
            G.tensor_tensor(parts[:, :, 2, :], tmpg, parts[:, :, 1, :], ALU.subtract).then_inc(y_set, 1)
            g.wait_ge(flag2_set, 1)
            large = g.value_load(flags[0:1, 1:2], min_val=0, max_val=1)
            with g.If(large > 0):
                def gather_y(t, k):
                    with g.Fori(0, BATCHES) as i:
                        g.wait_ge(turns2, t * PASS + 17 + i * YTURNS + 1 + 32)
                        g.sem_inc(gathers_begun, 1)
                        for j in range(TILES):
                            G.indirect_dma_start(out=ygat[:, j * FEAT:(j + 1) * FEAT], out_offset=None, in_=y_tab,
                                                 in_offset=bass.IndirectOffsetOnAxis(ap=gidx[:, 1, j:j + 1], axis=0)).then_inc(landed_y[k], 16)

                gather_y(0, 0)
                with g.Fori(0, (ITERS - 1) // 3) as m:
                    for k in range(3):
                        gather_y(3 * m + k + 1, (k + 1) % 3)
                gather_y(ITERS, ITERS % 3)

        @block.scalar
        def _(act):
            for dst_ap, src_ap in ((wpq[FEAT:FEAT + 1, HID:2 * HID], b1.rearrange("(o n) -> o n", o=1)),
                                   (wpq[0:FEAT, HID:2 * HID], W1[0:FEAT, :]), (wpq[0:FEAT, 0:HID], W1[FEAT:2 * FEAT, :]),
                                   (w1b[:, :], W1[FEAT:2 * FEAT, :]),
                                   (w2s[:, :], W2), (w3s[:, :], W3),
                                   (w4s[0:HID, 0:FEAT], W4), (w4s[HID:HID + 1, 0:FEAT], b4.rearrange("(o n) -> o n", o=1)),
                                   (b2c[:, :], b2.rearrange("(n o) -> n o", o=1))):
                act.dma_start(dst_ap, src_ap).then_inc(s_w, 16)
            act.wait_ge(s_b3, 1)
            for k in range(PARTS):
                act.dma_start(b3f[32 * k:32 * k + 1, :, :], b3.rearrange("(o n) -> o n", o=1).unsqueeze(1).to_broadcast([1, TILES, HID])).then_inc(s_w, 16)
            act.wait_ge(s_var, 1)
            A.activation(stats[:, 2, :], stats[:, 1, :], ACT.Sqrt).then_inc(s_std, 1)

            def second_part(n):
                k = len(groups(n))
                act.wait_ge(s_pqr, n + 1)
                A.activation(part(n, 1), by_half(pqr[:, n % 2, :], k), ACT.Copy).then_inc(s_pq1, 1)

            for f, (what, n) in enumerate(FILLS):
                act.wait_ge(s_fill, f + 1)
                bank = banks[f % 8]
                if what == "hT":
                    w = len(groups(n)) * P
                    A.activation(hT[0:FEAT, n * 512:n * 512 + w], bank[0:FEAT, 0:w], ACT.Copy).then_inc(s_evac, 1)
                elif what == "pq":
                    k = len(groups(n))
                    A.activation(part(n, 0), by_half(bank, k), ACT.Copy).then_inc(s_evac, 1)
                    if n:
                        second_part(n - 1)
                    if n == 6:
                        second_part(n)
                else:
                    dest = {"src": idxt, "lo": locol, "hi": hicol, "key": key, "rel": relcol, "dcol": dcolt}[what]
                    gc = P if n == 0 else GB
                    A.activation(dest[:, n * P:n * P + gc, :].rearrange("p g j -> p j g"),
                                 bank[:, :].rearrange("p (j g) -> p j g", j=TILES)[:, :, 0:gc], ACT.Copy).then_inc(s_evac, 1)

            def stage1(i, s):
                act.wait_ge(h1_done, i + 1)
                if later(i, 1):
                    act.wait_ge(h2_done, i)
                A.activation(h1s, H1[s][0:HID, :], ACT.Relu).then_inc(h1_out, 1)

            def stage2(i):
                act.wait_ge(h2_done, i + 1)
                if later(i, 1):
                    act.wait_ge(h3_done, i)
                A.activation(h2s, H2, ACT.Relu, bias=b2c[:, 0:1]).then_inc(h2_out, 1)

            def stage3(i):
                act.wait_ge(h3_done, i + 1)
                if later(i, 1):
                    act.wait_ge(seg_done, i)
                A.activation(h3s[:, :, 0:HID], H3[:, 0:TILES * HID].rearrange("p (j f) -> p j f", f=HID), ACT.Relu).then_inc(h3_out, 1)

            def counts_out(i, u):
                act.wait_ge(cp_done[u], i + 1)
                if later(i, 1):
                    act.wait_ge(cp_added[u], i)
                A.activation(cst[:, u, :], CP[u][:, 0:PCOLS], ACT.Copy).then_inc(cst_made[u], 1)

            def step(i, s):
                stage1(i, s)
                if later(i, 1):
                    stage3(i - 1)
                counts_out(i, 0)
                stage2(i)
                counts_out(i, 1)

            def edges():
                step(0, 0)
                step(1, 1)
                with act.Fori(1, BATCHES // 2) as m:
                    step(2 * m, 0)
                    step(2 * m + 1, 1)
                stage3(BATCHES - 1)

            def edges_general():
                with act.Fori(0, BATCHES) as i:
                    at = i * TURNS + 1 + MLP_AT
                    act.wait_ge(turns, at)
                    A.activation(h1s, H1[0][0:HID, :], ACT.Relu).then_inc(turns, 1)
                    act.wait_ge(turns, at + 2)
                    A.activation(h2s, H2, ACT.Relu, bias=b2c[:, 0:1]).then_inc(turns, 1)
                    act.wait_ge(turns, at + 4)
                    A.activation(h3s[:, :, 0:HID], H3[:, 0:TILES * HID].rearrange("p (j f) -> p j f", f=HID), ACT.Relu).then_inc(turns, 1)

            act.wait_ge(s_evac, PRE)
            act.dma_start(dcol_d, dcolt[:, :, :].rearrange("p g j -> p (g j)")).then_inc(s_dcol, 16)
            act.wait_ge(s_clear0, 1)
            act.wait_ge(s_b3p, 1)
            act.wait_ge(s_gen, 32)
            A.activation(C[:, T1:CCOLS].bitcast(F32), C[:, 0:CCOLS - T1].bitcast(F32), ACT.Copy).then_inc(s_clear, 1)
            general(act, edges, edges_general)
            act.wait_ge(edges_done, 1)
            def turn_out(w, s, k):
                act.wait_ge(turned, w + 1)
                for f in (2, 3):
                    lo, hi = SPLIT[f][0] * P, min(SPLIT[f][1] * P, NODES)
                    ins = A.activation(turned_cols(w, lo, hi - lo)[0:k, :], bankb[4 * s + f][0:k, 0:hi - lo], ACT.Copy)
                ins.then_inc(turn_a, 1)

            act.wait_ge(dmx, 1)
            A.activation(droot, deg, ACT.Sqrt).then_inc(sdd, 1)
            for w in range(ALONE):
                turn_out(w, 0, P)
            act.wait_ge(v2, 1)
            A.activation(stats[:, 2, :], stats[:, 1, :], ACT.Sqrt).then_inc(sd2, 1)
            with act.Fori(1, BLOCKS // 4) as m:
                for u in range(4):
                    turn_out(4 * m + u, u % 2, P)
            turn_out(BLOCKS - 1, 0, LASTN)

            def chunk_out(t, n, par):
                q = CHUNKS * t + n
                w = columns(n)[1]
                act.wait_ge(o_done, q + 1)
                if later(t, 1) or q >= 2:
                    act.wait_ge(r_done, q - 1)
                A.activation(osb[par][:, 0, 0:w], banks[par][0:3 * FEAT, 0:w], ACT.Copy).then_inc(o_hi, 1)
                act.wait_ge(o_rest, q + 1)
                A.activation(osb[par][:, 1, 0:w], rest[:, 0:w], ACT.Copy).then_inc(o_mid, 1)

            act.wait_ge(turn_d, BLOCKS)
            for n in range(CHUNKS):
                chunk_out(0, n, n % 2)
            with act.Fori(0, (ITERS - 2) // 2) as m:
                for u in range(2):
                    for n in range(CHUNKS):
                        chunk_out(2 * m + 1 + u, n, (1 + u + n) % 2)
            for n in range(CHUNKS):
                chunk_out(ITERS - 1, n, (ITERS - 1 + n) % 2)
            act.wait_ge(flag2_set, 1)
            large = act.value_load(flags[0:1, 1:2], min_val=0, max_val=1)
            with act.If(large > 0):
                act.wait_ge(dmx, 2)
                A.activation(droot, deg, ACT.Sqrt).then_inc(sdd, 1)

        @block.vector
        def _(dve):
            chain = [0]

            def link(ins):
                chain[0] += 1
                ins.then_inc(s_dve, 1)
                dve.wait_ge(s_dve, chain[0])

            def center(xin, xc, sq):
                link(V.tensor_reduce(stats[:, 0, :], xin, AX.X, ALU.add))
                link(V.tensor_scalar(stats[:, 1, :], stats[:, 0, :], 1.0 / FEAT, None, ALU.mult))
                link(V.tensor_tensor(xc, xin, wide(stats[:, 1, :]), ALU.subtract))
                link(V.tensor_tensor(sq, xc, xc, ALU.mult))
                link(V.tensor_reduce(stats[:, 0, :], sq, AX.X, ALU.add))

            V.memset(x_sb[:, BLOCKS - 1, :], 0.0).then_inc(s_pads, 1)
            V.memset(dN[:, 1, :], PAD_DST).then_inc(s_pads, 1)
            V.memset(sN[:, 1, :], SCOLS - 1).then_inc(s_pads, 1)
            V.memset(ones1[:, :], 1.0).then_inc(s_h3one, 1)
            V.memset(hT[FEAT:FEAT + 1, :], 1.0).then_inc(s_h3one, 1)
            V.memset(wpq[FEAT:FEAT + 1, 0:HID], 0.0).then_inc(s_h3one, 1)
            V.memset(w4s[:, FEAT:FEAT + 1], 0.0).then_inc(s_h3one, 1)
            V.memset(b3f, 0.0).then_inc(s_b3, 1)
            V.memset(ones3[:, :], 1.0).then_inc(s_h3one, 1)
            dve.wait_ge(s_h3one, 5)
            V.memset(w4s[HID:HID + 1, FEAT:FEAT + 1], 1.0).then_inc(s_h3one, 1)
            dve.wait_ge(s_x, 32)
            center(x_sb, xc, sq)
            V.tensor_scalar(stats[:, 1, :], stats[:, 0, :], 1.0 / FEAT, EPS, ALU.mult, ALU.add).then_inc(s_var, 1)
            dve.wait_ge(s_w, 16 * 12)
            V.tensor_tensor(wpq[0:FEAT, HID:2 * HID], wpq[0:FEAT, HID:2 * HID], w1b[:, :], ALU.subtract).then_inc(s_wpq, 1)
            dve.wait_ge(s_std, 1)
            link(V.reciprocal(stats[:, 3, :], stats[:, 2, :]))
            link(V.tensor_tensor(hn, xc, stats[:, 3, :].unsqueeze(2).to_broadcast([P, BLOCKS, FEAT]), ALU.mult))
            V.tensor_scalar(hn, hn, 0.0, None, ALU.max).then_inc(s_h, 1)
            dve.wait_ge(s_edges, 96)
            V.tensor_copy(srcf[:, :, :], sN).then_inc(s_idxN, 1)
            d4 = dN.rearrange("p c (u e) -> p (c u) e", u=2)
            link(V.tensor_reduce(pmn[:, :], d4, AX.X, ALU.min))
            link(V.tensor_reduce(pmx[:, :], d4, AX.X, ALU.max))
            link(V.tensor_scalar(pmn[:, :], pmn[:, :], float(NODES - 1), None, ALU.min))
            link(V.tensor_scalar(pmx[:, :], pmx[:, :], float(NODES - 1), None, ALU.min))
            pn = pmn[:, :].rearrange("p (c u) -> p c u", u=2)
            px = pmx[:, :].rearrange("p (c u) -> p c u", u=2)
            link(V.tensor_tensor(bmn[:, :], pn[:, :, 0], pn[:, :, 1], ALU.min))
            link(V.tensor_tensor(bmx[:, :], px[:, :, 0], px[:, :, 1], ALU.max))
            for c in range(2):
                for u in range(2):
                    q = slice(u * 256, u * 256 + 256)
                    link(V.tensor_scalar(relN[:, c, q], dN[:, c, q], pmn[:, 2 * c + u:2 * c + u + 1], None, ALU.subtract))
            link(V.tensor_tensor(pmx[:, :], pmx[:, :], pmn[:, :], ALU.subtract))
            link(V.tensor_tensor(bmx[:, :], bmx[:, :], bmn[:, :], ALU.subtract))
            link(V.tensor_scalar(pfl[:, :], pmx[:, :], float(PSPAN), None, ALU.is_ge))
            link(V.tensor_scalar(bmx[:, :], bmx[:, :], float(SPAN), None, ALU.is_ge))
            fl = pfl[:, :].rearrange("p (c u) -> p c u", u=2)
            link(V.memset(tabN[:, :, :], 0))
            link(V.tensor_tensor(bmx[:, :], bmx[:, :], fl[:, :, 0], ALU.max))
            link(V.tensor_tensor(tabN[:, :, 3], bmx[:, :], fl[:, :, 1], ALU.max))
            link(V.tensor_copy(tabN[:, :, 2], bmn[:, :]))
            link(V.tensor_copy(tabN[:, :, 4:6], pn))
            V.tensor_scalar(tabN[:, :, 0:2], pn, float(HI), None, ALU.mult).then_inc(s_keyN, 1)
            def third_part(n):
                k = len(groups(n))
                dve.wait_ge(s_pq1, n + 1)
                V.tensor_tensor(part(n, 2), by_half(pqr[:, n % 2, :], k), part(n, 1), ALU.subtract).then_inc(s_pq2, 1)

            for n in range(7):
                k = len(groups(n))
                f = FILLS.index(("pq", n))
                dve.wait_ge(s_evac, f + 1)
                if n >= 2:
                    dve.wait_ge(s_pq2, n - 1)
                V.tensor_tensor(by_half(pqr[:, n % 2, :], k), by_half(banks[f % 8], k), part(n, 0), ALU.subtract).then_inc(s_pqr, 1)
                if n:
                    third_part(n - 1)
            third_part(6)
            dve.wait_ge(s_tab, 16)
            V.tensor_reduce(flags[:, 0:1], tab[:, :].rearrange("o (g c) -> o g c", c=TABC)[:, :, 3], AX.X, ALU.max).then_inc(flag_set, 1)
            for c in range(2):
                link(V.tensor_scalar(relF[:, c, :], dN[:, c, :], bmn[:, c:c + 1], None, ALU.subtract))
            V.memset(stats[:, 0, 0:1], 0.0).then_inc(s_idxN, 1)
            link(V.tensor_scalar(aN, sN, P - 1, None, ALU.bitwise_and))
            V.tensor_copy(floF, aN).then_inc(s_idxN, 1)
            dve.wait_ge(s_idxN, 3)
            link(V.tensor_scalar(aN, sN, 7, None, ALU.arith_shift_right))
            link(V.tensor_copy(fhi, aN))
            link(V.tensor_scalar(keyF, relN, float(HI), None, ALU.mult))
            V.tensor_tensor(keyF, keyF, fhi, ALU.add).then_inc(s_idxN, 1)
            V.tensor_scalar(dclF, dN, float(SCOLS - 1), None, ALU.min).then_inc(s_idxN, 1)
            b3rest = pqr[0:96, 0, 0:TILES * HID].rearrange("p (j n) -> p j n", j=TILES)
            link(V.tensor_copy(b3p[:, :, :], b3f))
            link(V.tensor_tensor(b3rest, b3f, b3p[:, :, :], ALU.subtract))
            for k in (1, 2):
                link(V.tensor_copy(b3p[32 * k:32 * k + 32, :, :], b3rest[32 * k:32 * k + 32]))
            link(V.tensor_tensor(b3rest[64:96], b3rest[64:96], b3p[64:96, :, :], ALU.subtract))
            V.tensor_copy(b3p[64:96, :, :], b3rest[64:96]).then_inc(s_b3p, 1)
            dve.wait_ge(s_evac, PRE)
            dve.wait_ge(s_gen, 32)
            V.memset(C[:, T0 + 2 * SCOLS:T1].bitcast(F32), 0.0).then_inc(s_clear, 1)
            dve.wait_ge(s_qtab, 32)
            dve.wait_ge(s_ptab, 32)
            dve.wait_ge(s_idxd, 16)
            dve.wait_ge(s_rel, 32)
            dve.wait_ge(s_dcol, 16)
            V.memset(h3s[:, :, HID:HID + 1], 1.0).then_inc(s_h3one, 1)

            def onehots_p(i, s, loads):
                dve.wait_ge(rel_loaded[s], loads)
                if later(i, 2):
                    dve.wait_ge(h1_done, i - 1)
                V.tensor_scalar(ohT[:, s, :], relb[:, s, :], pmod[0:PROWS, 0:1], None, ALU.is_equal).then_inc(ohT_made, 1)

            def onehots_s(i, s):
                if later(i, 2):
                    dve.wait_ge(seg_done, i - 1)
                V.tensor_tensor(ohS[:, s, :, :], iota_s[:, :].unsqueeze(1).to_broadcast([P, TILES, SPAN]),
                                relcol[:, bass.ds(i, 1), :].rearrange("p o j -> p (o j)").unsqueeze(2).to_broadcast([P, TILES, SPAN]),
                                ALU.is_equal).then_inc(ohS_made, 1)

            def onehots_lo(i, s):
                if later(i, 2):
                    dve.wait_ge(cp_done[1], i - 1)
                V.tensor_tensor(ohL[:, s, :, :], iota_l[:, :].unsqueeze(1).to_broadcast([P, TILES, P]),
                                locol[:, bass.ds(i, 1), :].rearrange("p o j -> p (o j)").unsqueeze(2).to_broadcast([P, TILES, P]),
                                ALU.is_equal)
                V.tensor_tensor(ohH[:, s, :, :], iota_l[:, 0:HI].unsqueeze(1).to_broadcast([P, TILES, HI]),
                                hicol[:, bass.ds(i, 1), :].rearrange("p o j -> p (o j)").unsqueeze(2).to_broadcast([P, TILES, HI]),
                                ALU.is_equal)

            def onehots_c(i, s, u):
                kcol = key[:, bass.ds(i, 1), :].rearrange("p o j -> p (o j)")
                for j in (2 * u, 2 * u + 1):
                    last = V.tensor_scalar(ohC[:, s, j, :], iota_c[:, :], kcol[:, j:j + 1], None, ALU.is_equal)
                last.then_inc(ohC_made[u], 1)

            def base_of_sums(i):
                return dve.value_load(tab[0:1, bass.ds(TABC * i + 2, 1)], min_val=0, max_val=NODES - 1)

            def bases_of_counts(i):
                return nc.values_load_multi_w_load_instructions(
                    tab[0:1, bass.ds(TABC * i, 2)], (mybir.EngineType.DVE,), min_val=0, max_val=(NODES - 1) * HI)[1]

            def add_count(i, u, base):
                dve.wait_ge(cst_made[u], i + 1)
                if later(i, 1) or u:
                    dve.wait_ge(cp_added[1 - u], i + u)
                w = C[:, bass.ds(base, PCOLS)]
                V.tensor_tensor(w, cst[:, u, :], w, ALU.add).then_inc(cp_added[u], 1)

            def add_sums(i, base):
                dve.wait_ge(seg_done, i + 1)
                if later(i, 1):
                    dve.wait_ge(seg_added, i)
                w = sT[0:HID + 1, bass.ds(base, SPAN)]
                V.tensor_tensor(w, SEG[0:HID + 1, :], w, ALU.add).then_inc(seg_added, 1)

            def cleared():
                dve.wait_ge(s_clear, 4)
                dve.wait_ge(s_clear0, 1)

            def step(i, s, loads):
                ahead = loads is not None
                if ahead:
                    onehots_p(i + 1, 1 - s, loads)
                if later(i, 2):
                    add_sums(i - 2, base_of_sums(i - 2))
                if ahead:
                    onehots_lo(i + 1, 1 - s)
                if later(i, 1):
                    base = bases_of_counts(i - 1)
                    add_count(i - 1, 0, base[0])
                if ahead:
                    onehots_c(i + 1, 1 - s, 0)
                    onehots_c(i + 1, 1 - s, 1)
                if later(i, 1):
                    add_count(i - 1, 1, base[1])
                if ahead:
                    onehots_s(i + 1, 1 - s)

            def edges():
                onehots_p(0, 0, 16)
                onehots_lo(0, 0)
                onehots_c(0, 0, 0)
                onehots_c(0, 0, 1)
                onehots_s(0, 0)
                cleared()
                for i in range(3):
                    step(i, i % 2, 16 * ((i + 1) // 2 + 1))
                with dve.Fori(1, BATCHES // 2 - 1) as m:
                    step(2 * m + 1, 1, 16 * m + 32)
                    step(2 * m + 2, 0, 16 * m + 32)
                step(BATCHES - 1, 1, None)
                base = bases_of_counts(BATCHES - 1)
                for u in range(2):
                    add_count(BATCHES - 1, u, base[u])
                for b in (BATCHES - 2, BATCHES - 1):
                    add_sums(b, base_of_sums(b))
                dve.wait_ge(cp_added[1], BATCHES)
                dve.wait_ge(seg_added, BATCHES)

            def edges_general():
                cleared()
                wcol = ohS[0:PROWS, 1, 0, 0:1]
                with dve.Fori(0, BATCHES) as i:
                    at = i * TURNS + 1
                    dve.wait_ge(turns, at + LOADS + 1)
                    V.tensor_copy(wcol, pmod[0:PROWS, 0:1]).then_inc(turns, 1)
                    with dve.Fori(0, NP) as w:
                        dve.wait_ge(turns, at + P_AT + w * PSTEP + 16)
                        V.tensor_scalar(ohT[:, 0, :], grow, wcol, None, ALU.is_equal).then_inc(turns, 1)
                        dve.wait_ge(turns, at + P_AT + w * PSTEP + 18)
                        V.tensor_scalar(wcol, wcol, float(PWIN), None, ALU.add).then_inc(turns, 1)
                    dve.wait_ge(turns, at + MLP_AT + 5)
                    V.memset(roff[:, :], 0.0).then_inc(turns, 1)
                    tcol = gidx[:, 1, :].unsqueeze(2).to_broadcast([P, TILES, SPAN])
                    with dve.Fori(0, NW) as w:
                        dve.wait_ge(turns, at + S_AT + w * SSTEP)
                        V.scalar_tensor_tensor(out=ohS[:, 0, :, :], in0=iota_s[:, :].unsqueeze(1).to_broadcast([P, TILES, SPAN]),
                                               scalar=roff[:, 0:1], in1=tcol, op0=ALU.add, op1=ALU.is_equal).then_inc(turns, 1)
                        dve.wait_ge(turns, at + S_AT + w * SSTEP + 2)
                        v = sT[0:HID + 1, bass.ds(w * SPAN, SPAN)]
                        V.tensor_tensor(v, SEG[0:HID + 1, :], v, ALU.add).then_inc(turns, 1)
                        dve.wait_ge(turns, at + S_AT + w * SSTEP + 3)
                        V.tensor_scalar(roff[:, :], roff[:, :], float(SPAN), None, ALU.add).then_inc(turns, 1)
                    dve.wait_ge(turns, at + K_AT)
                    V.tensor_scalar(gidx[:, 2, :], idx[:, 0, :], 7, None, ALU.arith_shift_right).then_inc(turns, 1)
                    dve.wait_ge(turns, at + K_AT + 1)
                    V.tensor_scalar(gidx[:, 3, :], idx[:, 0, :], P - 1, None, ALU.bitwise_and).then_inc(turns, 1)
                    dve.wait_ge(turns, at + K_AT + 2)
                    gkey = gidx[:, 4, :].bitcast(F32)
                    V.tensor_scalar(gkey, gidx[:, 1, :], float(HI), None, ALU.mult).then_inc(turns, 1)
                    dve.wait_ge(turns, at + K_AT + 3)
                    V.tensor_tensor(gkey, gkey, gidx[:, 2, :], ALU.add).then_inc(turns, 1)
                    dve.wait_ge(turns, at + K_AT + 4)
                    V.tensor_tensor(ohL[:, 0, :, :], iota_l[:, :].unsqueeze(1).to_broadcast([P, TILES, P]),
                                    gidx[:, 3, :].unsqueeze(2).to_broadcast([P, TILES, P]), ALU.is_equal).then_inc(turns, 1)
                    dve.wait_ge(turns, at + K_AT + 5)
                    V.tensor_tensor(ohH[:, 0, :, :], iota_l[:, 0:HI].unsqueeze(1).to_broadcast([P, TILES, HI]),
                                    gidx[:, 2, :].unsqueeze(2).to_broadcast([P, TILES, HI]), ALU.is_equal).then_inc(turns, 1)
                    dve.wait_ge(turns, at + K_AT + 7)
                    V.memset(roff[:, :], 0.0).then_inc(turns, 1)
                    with dve.Fori(0, NC) as w:
                        dve.wait_ge(turns, at + C_AT + w * CSTEP)
                        for j in range(TILES):
                            last = V.tensor_scalar(ohC[:, 0, j, :], iota_c[:, :], roff[:, 0:1], gkey[:, j:j + 1], ALU.add, ALU.is_equal)
                        last.then_inc(turns, 1)
                        dve.wait_ge(turns, at + C_AT + w * CSTEP + 2)
                        v = C[:, bass.ds(w * PCOLS, PCOLS)]
                        V.tensor_tensor(v, CP[0][:, 0:PCOLS], v, ALU.add).then_inc(turns, 1)
                        dve.wait_ge(turns, at + C_AT + w * CSTEP + 3)
                        V.tensor_scalar(roff[:, :], roff[:, :], float(PCOLS), None, ALU.add).then_inc(turns, 1)
                dve.wait_ge(turns, BATCHES * TURNS + 1)

            dve.sem_inc(turns, 1)
            general(dve, edges, edges_general)
            dve.sem_inc(edges_done, 1)
            V.memset(x1[:, BLOCKS - 1, :], 0.0).then_inc(s_x1pad, 1)

            def copy_block(w, s, k):
                if later(w, 2):
                    dve.wait_ge(turned, w - 1)
                V.tensor_copy(stage[s][:, 0:k * HI], C[:, bass.ds(w * (P * HI), k * HI)]).then_inc(staged, 1)

            def turn_out(w, s, k):
                dve.wait_ge(turned, w + 1)
                V.tensor_copy(turned_cols(w, 0, TD * P)[0:k, :].rearrange("p (f n) -> p f n", f=2),
                              psum_b[0:k, 4 * s:4 * s + 2, 0:TD * P // 2]).then_inc(turn_d, 1)

            V.tensor_scalar(deg, DEG, 1.0, None, ALU.max).then_inc(dmx, 1)
            copy_block(0, 0, P)
            for w in range(ALONE):
                copy_block(w + 1, (w + 1) % 2, P)
                turn_out(w, 0, P)
            dve.wait_ge(m_done, 1)
            dve.wait_ge(s_x1, 32)
            msum = [(banks[6], 0, MB), (banks[7], MB, BLOCKS)]
            for b, lo, hi in msum:
                v = b[:, 0:(hi - lo) * (FEAT + 1)].rearrange("p (b f) -> p b f", f=FEAT + 1)
                link(V.tensor_scalar(stats[:, 0, lo:hi], v[:, :, FEAT], 1.0, None, ALU.max))
            link(V.reciprocal(stats[:, 1, :], stats[:, 0, :]))
            for b, lo, hi in msum:
                v = b[:, 0:(hi - lo) * (FEAT + 1)].rearrange("p (b f) -> p b f", f=FEAT + 1)
                link(V.tensor_tensor(tmpf[:, lo:hi, :], v[:, :, 0:FEAT], wide(stats[:, 1, lo:hi]), ALU.mult))
            dve.sem_inc(m_read, 1)
            link(V.tensor_tensor(x1, x1, tmpf, ALU.add))
            center(x1, ah, tmpf)
            link(V.tensor_scalar(ah, ah, 0.0, None, ALU.max))
            V.tensor_scalar(stats[:, 1, :], stats[:, 0, :], 1.0 / FEAT, EPS, ALU.mult, ALU.add).then_inc(v2, 1)
            dve.wait_ge(sd2, 1)
            link(V.reciprocal(stats[:, 3, :], stats[:, 2, :]))
            dve.wait_ge(sdd, 1)
            link(V.reciprocal(dinv, droot))
            link(V.scalar_tensor_tensor(out=c1, in0=dinv, scalar=BETA, in1=dinv, op0=ALU.mult, op1=ALU.mult))
            V.tensor_scalar(cf, dinv, BETA / GAMMA, None, ALU.mult).then_inc(scales_made, 1)
            for k in range(3):
                q = slice(k * FEAT, (k + 1) * FEAT)
                V.tensor_copy(sum3[q, :], identb[q, q]).then_inc(ones_set, 1)
            with dve.Fori(1, BLOCKS // 4 - 1) as m:
                for u in range(4):
                    copy_block(4 * m + u + 1, (u + 1) % 2, P)
                    turn_out(4 * m + u, u % 2, P)
            for w in range(4 * (BLOCKS // 4 - 1), BLOCKS - 2):
                copy_block(w + 1, (w + 1) % 2, P)
                turn_out(w, w % 2, P)
            copy_block(BLOCKS - 1, 0, LASTN)
            turn_out(BLOCKS - 2, 1, P)
            turn_out(BLOCKS - 1, 0, LASTN)
            dve.wait_ge(turn_d, BLOCKS)
            dve.wait_ge(turned, BLOCKS)
            dve.wait_ge(y_set, 1)
            V.memset(maxima, 0.0).then_inc(scanned, 1)

            def chunk_out(t, n, par):
                q = CHUNKS * t + n
                w = columns(n)[1]
                dve.wait_ge(o_hi, q + 1)
                if later(t, 1) or q >= 1:
                    dve.wait_ge(o_mid, q)
                    dve.wait_ge(o_out, q)
                V.tensor_tensor(rest[:, 0:w], banks[par][0:3 * FEAT, 0:w], osb[par][:, 0, 0:w], ALU.subtract).then_inc(o_rest, 1)
                dve.wait_ge(o_mid, q + 1)
                V.tensor_tensor(osb[par][:, 2, 0:w], rest[:, 0:w], osb[par][:, 1, 0:w], ALU.subtract).then_inc(o_out, 1)

            def new_y(t, n, par, src_par, last=False):
                chunk_out(t, n, par)
                q = CHUNKS * t + n
                lo, hi = FIRST[n], FIRST[n + 1]
                k = hi - lo
                rows = P
                dve.wait_ge(r_done, q + 1)
                if last and n:
                    dve.wait_ge(s_res, n)
                rv = banks[2 + par][0:rows, 0:k * FEAT].rearrange("p (b f) -> p b f", f=FEAT)
                c = (cf if last else c1)[0:rows, lo:hi].unsqueeze(2).to_broadcast([rows, k, FEAT])
                yb, rb = yv[0:rows, 0:k, :], yr[0:rows, 0:k, :]
                done = [0]

                def step(ins):
                    done[0] += 1
                    ins.then_inc(y_step, 1)
                    dve.wait_ge(y_step, (5 * q if not last else 5 * CHUNKS * t + n) + done[0])

                step(V.tensor_tensor(yb, rv, c, ALU.mult))
                if last:
                    V.tensor_tensor(yb, yb, hg[0:rows, lo:hi, :], ALU.add).then_inc(y_made, 1)
                    dve.wait_ge(y_made, q + 1)
                    V.tensor_tensor(ycur[0:rows, lo:hi, :], x1[0:rows, lo:hi, :], yb, ALU.add).then_inc(s_res, 1)
                    return
                step(V.tensor_tensor(yb, yb, ah[0:rows, lo:hi, :], ALU.add))
                dest = y3[1 - src_par][0:rows, lo:hi]
                step(V.tensor_copy(dest[:, :, 0, :], yb))
                step(V.tensor_tensor(rb, yb, dest[:, :, 0, :], ALU.subtract))
                step(V.tensor_copy(dest[:, :, 1, :], rb))
                V.tensor_tensor(dest[:, :, 2, :], rb, dest[:, :, 1, :], ALU.subtract).then_inc(y_made, 1)

            for n in range(CHUNKS):
                new_y(0, n, n % 2, 0)
            with dve.Fori(0, (ITERS - 2) // 2) as m:
                for u in range(2):
                    for n in range(CHUNKS):
                        new_y(2 * m + 1 + u, n, (1 + u + n) % 2, (1 + u) % 2)
                        if n in SCAN_AFTER:
                            at = (2 * m + u) * SCANS + SCAN_AFTER.index(n)
                            dve.wait_ge(scanned, at + 1)
                            V.tensor_tensor(maxima, maxima, C[:, bass.ds(at * SCAN, SCAN)], ALU.max).then_inc(scanned, 1)
            dve.wait_ge(scanned, (ITERS - 2) * SCANS + 1)
            V.tensor_reduce(roff[:, :], maxima, AX.X, ALU.max).then_inc(s_max, 1)
            for n in range(CHUNKS):
                new_y(ITERS - 1, n, (ITERS - 1 + n) % 2, (ITERS - 1) % 2, last=True)
                if n == 2:
                    dve.wait_ge(s_max2, 32)
                    link(V.tensor_reduce(mrow[:, 0:1], mrow[:, 1:P + 1], AX.X, ALU.max))
                    V.tensor_scalar(flags[:, 1:2], mrow[:, 0:1], 256.0, None, ALU.is_ge).then_inc(flag2_set, 1)

            def passes(t, k, before):
                with dve.Fori(0, BATCHES) as i:
                    at = t * PASS + 17 + i * YTURNS + 1 + Y_LOADS
                    dve.wait_ge(turns2, at)
                    dve.wait_ge(landed_y[k], before * (64 * BATCHES) + 64 * i + 64)
                    V.tensor_scalar(gidx[:, 2, :], gidx[:, 0, :], 7, None, ALU.arith_shift_right).then_inc(turns2, 1)
                    dve.wait_ge(turns2, at + 1)
                    V.tensor_scalar(gidx[:, 3, :], gidx[:, 0, :], P - 1, None, ALU.bitwise_and).then_inc(turns2, 1)
                    dve.wait_ge(turns2, at + 2)
                    V.tensor_tensor(ylo, iota_l[:, :].unsqueeze(1).to_broadcast([P, TILES, P]),
                                    gidx[:, 3, :].unsqueeze(2).to_broadcast([P, TILES, P]), ALU.is_equal).then_inc(turns2, 1)
                    dve.wait_ge(turns2, at + 3)
                    V.tensor_tensor(yhi, iota_l[:, 0:HI].unsqueeze(1).to_broadcast([P, TILES, HI]),
                                    gidx[:, 2, :].unsqueeze(2).to_broadcast([P, TILES, HI]), ALU.is_equal).then_inc(turns2, 1)
                    for j in range(TILES):
                        dve.wait_ge(turns2, at + 4 + 2 * j)
                        V.tensor_tensor(yexp, yhi[:, j, :].unsqueeze(2).to_broadcast([P, HI, FEAT]),
                                        ygat[:, j * FEAT:(j + 1) * FEAT].unsqueeze(1).to_broadcast([P, HI, FEAT]), ALU.mult).then_inc(turns2, 1)
                dve.wait_ge(turns2, (t + 1) * PASS)

            dve.wait_ge(flag2_set, 1)
            large = dve.value_load(flags[0:1, 1:2], min_val=0, max_val=1)
            with dve.If(large > 0):
                dve.wait_ge(s_out, 16 * (CHUNKS + 1))
                sums = [psum[:, 0, 0:GCOL * FEAT].rearrange("p (b f) -> p b f", f=FEAT),
                        psum[:, 1, 0:(HI - GCOL) * FEAT].rearrange("p (b f) -> p b f", f=FEAT)]
                parts = [(sums[0], 0, GCOL), (sums[1], GCOL, HI)]
                link(V.memset(zrow, 0.0))
                link(V.memset(ycur, 1.0))
                link(V.memset(ycur[:, BLOCKS - 1, :], 0.0))
                link(V.memset(ycur[0:LASTN, BLOCKS - 1, :], 1.0))
                dve.sem_inc(turns2, 1)
                passes(0, 0, 0)
                for v, lo, hi in parts:
                    link(V.tensor_scalar(deg[:, lo:hi], v[:, :, 0], 1.0, None, ALU.max))
                V.memset(roff[:, :], 0.0).then_inc(dmx, 1)
                dve.wait_ge(sdd, 2)
                link(V.reciprocal(dinv, droot))
                link(V.scalar_tensor_tensor(out=c1, in0=dinv, scalar=BETA, in1=dinv, op0=ALU.mult, op1=ALU.mult))
                link(V.tensor_scalar(cf, dinv, BETA / GAMMA, None, ALU.mult))
                link(V.tensor_tensor(ah, hg, wide(dinv), ALU.mult))
                link(V.tensor_scalar(ycur, ah, GAMMA / ALPHA, None, ALU.mult))
                V.tensor_scalar(ah, ah, GAMMA, None, ALU.mult).then_inc(turns2, 1)
                with dve.Fori(0, (ITERS - 1) // 3) as m:
                    for u in (1, 2, 3):
                        t = 3 * m + u
                        passes(t, u % 3, m + u // 3)
                        for v, lo, hi in parts:
                            V.tensor_tensor(ycur[:, lo:hi, :], v, wide(c1[:, lo:hi]), ALU.mult).then_inc(y2_step, 1)
                        dve.wait_ge(y2_step, 2 * t)
                        V.tensor_tensor(ycur, ycur, ah, ALU.add).then_inc(turns2, 1)
                passes(ITERS, ITERS % 3, ITERS // 3)
                for k, (v, lo, hi) in enumerate(parts):
                    link(V.tensor_tensor(ycur[:, lo:hi, :], v, wide(cf[:, lo:hi]), ALU.mult))
                link(V.tensor_tensor(ycur, ycur, hg, ALU.add))
                V.tensor_tensor(ycur, ycur, x1, ALU.add).then_inc(turns2, 1)

        @block.tensor
        def _(pe):
            pe.wait_ge(s_const, 11)
            for f, (what, n) in enumerate(FILLS):
                bank = banks[f % 8]
                if f >= 8:
                    pe.wait_ge(s_evac, f - 7)
                    if FILLS[f - 8][0] == "pq":
                        pe.wait_ge(s_pqr, FILLS[f - 8][1] + 1)
                if what == "hT":
                    pe.wait_ge(s_h, 1)
                    for k, b in enumerate(groups(n)):
                        last = T.transpose(bank[0:FEAT, k * P:(k + 1) * P], hn[:, b, :], ident[:, :])
                elif what == "pq":
                    pe.wait_ge(s_evac, 7)
                    pe.wait_ge(s_wpq, 1)
                    pe.wait_ge(s_h3one, 6)
                    for k, b in enumerate(groups(n)):
                        last = T.matmul(bank[:, k * P:(k + 1) * P], hT[:, b * P:(b + 1) * P], wpq[:, :], start=True, stop=True)
                else:
                    pe.wait_ge(s_idxN, {"src": 1, "rel": 2, "lo": 3, "hi": 4, "key": 4, "dcol": 5}[what])
                    gc = P if n == 0 else GB
                    for j in range(TILES):
                        last = T.transpose(bank[:, j * P:j * P + gc], NAT[what][0:gc, n, j * P:(j + 1) * P], ident[0:gc, 0:gc])
                last.then_inc(s_fill, 1)
            pe.wait_ge(s_evac, PRE)

            def rows_q(bank, q, start):
                for j in range(TILES):
                    for k in range(PARTS):
                        last = T.matmul(bank[0:HID, j * P:(j + 1) * P], gat[:, q, j, k, :], identb[:, :],
                                        start=start and j == 0 and k == 0, stop=not start, skip_group_check=True)
                return last

            def stage1(i, s, q, loads, lands):
                pe.wait_ge(pw_loaded[s], loads)
                pe.wait_ge(ohT_made, i + 1)
                if later(i, 2):
                    pe.wait_ge(h1_out, i - 1)
                for u in range(2):
                    h = slice(u * 256, u * 256 + 256)
                    T.matmul(H1[s][0:HID, h], pw[:, s, u, :], ohT[:, s, h], start=u == 0, stop=False, skip_group_check=True)
                pe.wait_ge(landed[q], lands)
                rows_q(H1[s], q, False).then_inc(h1_done, 1)

            def third_layer():
                T.matmul(H3[:, 0:TILES * HID], ones3[:, :], b3p[:, :, :].rearrange("o j f -> o (j f)"), start=True, stop=False, skip_group_check=True)
                for j in range(TILES):
                    last = T.matmul(H3[:, j * HID:(j + 1) * HID], h2s[:, j * P:(j + 1) * P], w3s[:, :], start=False, stop=True, skip_group_check=True)
                return last

            def stage2(i):
                pe.wait_ge(h1_out, i + 1)
                if later(i, 1):
                    pe.wait_ge(h2_out, i)
                T.matmul(H2, w2s[:, :], h1s, start=True, stop=True).then_inc(h2_done, 1)

            def stage3(i):
                pe.wait_ge(h2_out, i + 1)
                if later(i, 1):
                    pe.wait_ge(h3_out, i)
                third_layer().then_inc(h3_done, 1)

            def node_sums(i, s):
                pe.wait_ge(h3_out, i + 1)
                pe.wait_ge(ohS_made, i + 1)
                if later(i, 1):
                    pe.wait_ge(seg_added, i)
                for j in range(TILES):
                    last = T.matmul(SEG[0:HID + 1, :], h3s[:, j, :], ohS[:, s, j, :], start=j == 0, stop=j == TILES - 1)
                last.then_inc(seg_done, 1)

            def counts(i, s, u):
                pe.wait_ge(ohC_made[u], i + 1)
                if later(i, 1):
                    pe.wait_ge(cst_made[u], i)
                for j in (2 * u, 2 * u + 1):
                    T.matmul(DEG, ohL[:, s, j, :], ohH[:, s, j, :], start=False, stop=False, skip_group_check=True)
                    last = T.matmul(CP[u][:, 0:PCOLS], ohL[:, s, j, :], ohC[:, s, j, :], start=j == 2 * u, stop=j == 2 * u + 1)
                last.then_inc(cp_done[u], 1)

            def step(i, s, q, loads, lands):
                stage1(i, s, q, loads, lands)
                if later(i, 1):
                    stage3(i - 1)
                counts(i, s, 0)
                stage2(i)
                if later(i, 1):
                    node_sums(i - 1, 1 - s)
                counts(i, s, 1)

            def edges():
                pe.wait_ge(s_b3p, 1)
                for i in range(SLOTS):
                    step(i, i % 2, i, 32 * (i // 2) + 32, 64)
                with pe.Fori(1, BATCHES // SLOTS) as m:
                    for q in range(SLOTS):
                        step(SLOTS * m + q, q % 2, q, 64 * m + 32 * (q // 2) + 32, 64 * m + 64)
                stage3(BATCHES - 1)
                node_sums(BATCHES - 1, 1)

            def edges_general():
                pe.wait_ge(s_b3p, 1)
                with pe.Fori(0, BATCHES) as i:
                    at = i * TURNS + 1
                    pe.wait_ge(turns, at + LOADS)
                    pe.wait_ge(landed_gen, 64 * i + 64)
                    rows_q(H1[0], 0, True).then_inc(turns, 1)
                    with pe.Fori(0, NP) as w:
                        pe.wait_ge(turns, at + P_AT + w * PSTEP + 17)
                        T.matmul(H1[0][0:HID, :], pw[:, 0, 0, :], ohT[:, 0, :], start=False, stop=False, skip_group_check=True).then_inc(turns, 1)
                    pe.wait_ge(turns, at + MLP_AT + 1)
                    T.matmul(H2, w2s[:, :], h1s, start=True, stop=True).then_inc(turns, 1)
                    pe.wait_ge(turns, at + MLP_AT + 3)
                    third_layer().then_inc(turns, 1)
                    with pe.Fori(0, NW) as w:
                        pe.wait_ge(turns, at + S_AT + w * SSTEP + 1)
                        for j in range(TILES):
                            last = T.matmul(SEG[0:HID + 1, :], h3s[:, j, :], ohS[:, 0, j, :], start=j == 0, stop=j == TILES - 1)
                        last.then_inc(turns, 1)
                    pe.wait_ge(turns, at + K_AT + 6)
                    for j in range(TILES):
                        last = T.matmul(DEG, ohL[:, 0, j, :], ohH[:, 0, j, :], start=False, stop=False, skip_group_check=True)
                    last.then_inc(turns, 1)
                    with pe.Fori(0, NC) as w:
                        pe.wait_ge(turns, at + C_AT + w * CSTEP + 1)
                        for j in range(TILES):
                            last = T.matmul(CP[0][:, 0:PCOLS], ohL[:, 0, j, :], ohC[:, 0, j, :], start=j == 0, stop=j == TILES - 1)
                        last.then_inc(turns, 1)

            pe.wait_ge(s_clear0, 1)
            T.matmul(DEG, identb[:, :], C[:, 0:HI], start=True, stop=False, skip_group_check=True)
            general(pe, edges, edges_general)
            pe.wait_ge(edges_done, 1)

            def turn(w, s, k):
                pe.wait_ge(staged, w + 1)
                if later(w, ALONE):
                    pe.wait_ge(turn_a, w - 1)
                    pe.wait_ge(turn_d, w - 1)
                v = stage[w % 2 if isinstance(w, int) else s].rearrange("p (t a) -> p t a", a=HI)
                for f, (lo, hi) in enumerate(SPLIT):
                    for a in range(lo, hi):
                        last = T.transpose(bankb[4 * s + f][0:k, (a - lo) * P:(a - lo + 1) * P], v[:, 0:k, a], identb[:, :])
                last.then_inc(turned, 1)

            for w in range(ALONE):
                if w:
                    pe.wait_ge(turn_a, w)
                    pe.wait_ge(turn_d, w)
                turn(w, 0, P)
                for b in range(BLOCKS * w // ALONE, BLOCKS * (w + 1) // ALONE):
                    bank, k = (banks[6], b) if b < MB else (banks[7], b - MB)
                    last = T.matmul(bank[:, k * (FEAT + 1):(k + 1) * (FEAT + 1)], sT[0:HID + 1, b * P:(b + 1) * P], w4s[:, :], start=True, stop=True)
            last.then_inc(m_done, 1)
            pe.wait_ge(turn_a, ALONE)
            pe.wait_ge(turn_d, ALONE)
            pe.wait_ge(dmx, 1)
            pe.wait_ge(m_read, 1)
            with pe.Fori(1, BLOCKS // 4) as m:
                for u in range(4):
                    turn(4 * m + u, u % 2, P)
            turn(BLOCKS - 1, 0, LASTN)
            pe.wait_ge(turn_a, BLOCKS)
            pe.wait_ge(turn_d, BLOCKS)
            def gather_groups(t, n, par):
                q = CHUNKS * t + n
                pe.wait_ge(o_out, q + 1)
                if later(t, 1) or q >= 2:
                    pe.wait_ge(y_made, q - 1)
                for b in range(FIRST[n], FIRST[n + 1]):
                    k = P if b < BLOCKS - 1 else LASTN
                    o = b - FIRST[n]
                    for part in range(3):
                        last = T.matmul(banks[2 + par][0:k, o * FEAT:(o + 1) * FEAT], osb[par][:, part, o * P:o * P + k], sum3[0:3 * FEAT, :],
                                        start=part == 0, stop=part == 2)
                last.then_inc(r_done, 1)

            def iteration(t, tp):
                for n in range(CHUNKS):
                    q = CHUNKS * t + n
                    par = (tp + n) % 2
                    at, w = columns(n)
                    if later(t, 1) or q >= 2:
                        pe.wait_ge(o_rest, q - 1)
                    for b in range(BLOCKS):
                        if n == 0 and b in FIRST and later(t, 1):
                            pe.wait_ge(y_made, CHUNKS * (t - 1) + FIRST.index(b) + 1)
                        k = P if b < BLOCKS - 1 else LASTN
                        last = T.matmul(banks[par][0:3 * FEAT, 0:w], y3[tp][0:k, b, :, :].rearrange("p k f -> p (k f)"),
                                        C[0:k, b * NODES + at:b * NODES + at + w], start=b == 0, stop=b == BLOCKS - 1)
                        if b + 1 == GATHER_AT[n] and (n > 0 or later(t, 1)):
                            if n > 0:
                                gather_groups(t, n - 1, 1 - par)
                            else:
                                gather_groups(t - 1, CHUNKS - 1, 1 - par)
                    last.then_inc(o_done, 1)

            pe.wait_ge(y_set, 1)
            pe.wait_ge(ones_set, 3)
            iteration(0, 0)
            with pe.Fori(0, (ITERS - 2) // 2) as m:
                iteration(2 * m + 1, 1)
                iteration(2 * m + 2, 0)
            iteration(ITERS - 1, (ITERS - 1) % 2)
            gather_groups(ITERS - 1, CHUNKS - 1, (ITERS + CHUNKS) % 2)
            pe.wait_ge(flag2_set, 1)
            large = pe.value_load(flags[0:1, 1:2], min_val=0, max_val=1)
            with pe.If(large > 0):
                with pe.Fori(0, ITERS + 1) as t:
                    pe.wait_ge(turns2, t * PASS + 1 + 16)
                    for k in range(2):
                        last = T.matmul(banks[k][:, :], ones1[:, :], zrow[0:1, :], start=True, stop=False, skip_group_check=True)
                    last.then_inc(turns2, 1)
                    with pe.Fori(0, BATCHES) as i:
                        at = t * PASS + 17 + i * YTURNS + 1 + YT_AT
                        for j in range(TILES):
                            pe.wait_ge(turns2, at + 2 * j + 1)
                            for k, (lo, hi) in enumerate(((0, GCOL), (GCOL, HI))):
                                last = T.matmul(banks[k][:, 0:(hi - lo) * FEAT], ylo[:, j, :], yexp[:, lo:hi, :].rearrange("p a f -> p (a f)"),
                                                start=False, stop=False, skip_group_check=True)
                            last.then_inc(turns2, 1)


_INS = ["x", "src", "dst"] + [f"L0_gnn_{a}{n}" for n in range(1, 5) for a in "Wb"]


def kernel(**inputs):
    import concourse.bacc as bacc
    from concourse.bass_utils import run_bass_kernel_spmd as run

    nc = bacc.Bacc("TRN2", target_bir_lowering=False, num_devices=1)
    arrays, args = {}, []
    for name in _INS:
        a = np.ascontiguousarray(inputs[name])
        arrays[f"in_{name}"] = a
        args.append(nc.dram_tensor(f"in_{name}", a.shape, mybir.dt.from_np(a.dtype), kind="ExternalInput").ap())
    result = nc.dram_tensor("out_0", (NODES, FEAT), F32, kind="ExternalOutput").ap()
    build(nc, *args, result)
    return run(nc, [arrays], core_ids=[0]).results[0]["out_0"]
```
